# Optimizing a Trainium2 kernel written in Bass

```python
import numpy as np
import jax
import jax.numpy as jnp

def _softmax(x, axis=-1):
    return jax.nn.softmax(x, axis=axis)

def _gelu(x):
    return jax.nn.gelu(x, approximate=True)

def _silu(x):
    return jax.nn.silu(x)

def _sigmoid(x):
    return jax.nn.sigmoid(x)

def _layernorm(x, axis=-1, eps=1e-05):
    m = jnp.mean(x, axis=axis, keepdims=True)
    v = jnp.var(x, axis=axis, keepdims=True)
    return (x - m) / jnp.sqrt(v + eps)

def _scatter_add(tgt, idx, src, axis=0):
    return tgt.at[idx].add(src)

def _segment_sum(src, seg, n):
    return jax.ops.segment_sum(src, seg, n)
kernel_name = 'mk_perceiver_d2_seqx_r8_2f6557'

def setup_inputs(seed: int=0):
    np.random.seed(seed)
    _w = jnp.asarray

    def _rec_inputs():
        import jax
        import jax.numpy as jnp
        _rk = jax.random.key(seed)
        x = -0.0003929 + 0.9999 * jax.random.normal(jax.random.fold_in(_rk, 1), (64, 64, 128), jnp.float32)
        _lenS = 64 - jax.random.randint(jax.random.fold_in(_rk, 7), (64,), 0, max(1, 64 // 4) + 1, jnp.int32)
        _lenS2 = 128 - jax.random.randint(jax.random.fold_in(_rk, 8), (64,), 0, max(1, 128 // 4) + 1, jnp.int32)
        _ctx_1024P = jax.random.normal(jax.random.fold_in(_rk, 11), (64, 16, 128), jnp.float32)
        _ctx_1024c = jax.random.dirichlet(jax.random.fold_in(_rk, 511), 0.3 * jnp.ones((16,), jnp.float32), (64, 128))
        _ctx_1024t = jnp.einsum('bsk,bkd->bsd', _ctx_1024c, _ctx_1024P)
        _ctx_1024t = _ctx_1024t * jax.lax.rsqrt(jnp.mean(jnp.square(_ctx_1024t)) + 1e-12) * 0.953939
        ctx_1024 = 2.81802e-05 + 1.00001 * (_ctx_1024t + 0.3 * jax.random.normal(jax.random.fold_in(_rk, 611), (64, 128, 128), jnp.float32))
        _validS = jnp.arange(64)[None, :] < _lenS[:, None]
        _validS2 = jnp.arange(128)[None, :] < _lenS2[:, None]
        _causal = jnp.tril(jnp.ones((64, 64), dtype=bool))
        mask_1x1xSxS2_ik0 = jnp.where(jnp.broadcast_to(_validS2[0:1, None, None, :], (1, 1, 64, 128)), 0, 1).astype(jnp.int32)
        return (x, ctx_1024, mask_1x1xSxS2_ik0)
    x, ctx_1024, mask_1x1xSxS2_ik0 = _rec_inputs()

    def _L0_xattn_setup():
        import jax, jax.numpy as jnp
        import numpy as np
        B, LQ, LKV, D = (8, 256, 256, 128)
        key = jax.random.key(seed)
        k1, k2, k3, k4, k5, k6, k7 = jax.random.split(key, 7)
        s = 1.0 / np.sqrt(D)
        return {'query': jax.random.normal(k1, (B, LQ, D), jnp.float32), 'key': jax.random.normal(k2, (B, LKV, D), jnp.float32), 'value': jax.random.normal(k3, (B, LKV, D), jnp.float32), 'Wq': jax.random.uniform(k4, (D, D), jnp.float32, -s, s), 'bq': jax.random.uniform(k5, (D,), jnp.float32, -s, s), 'Wk': jax.random.uniform(k6, (D, D), jnp.float32, -s, s), 'bk': jax.random.uniform(k7, (D,), jnp.float32, -s, s), 'scale_factor': 32, 'dropout_p': 0}
    _L0_xattn_all = _L0_xattn_setup()
    _L0_xattn_in = {k: v for k, v in _L0_xattn_all.items() if k in ('Wq', 'bq', 'Wk', 'bk')}
    del _L0_xattn_all

    def _L0_attn_setup():
        import jax, jax.numpy as jnp
        import numpy as np
        B, L, D, NLAYERS, KCONV = (8, 256, 128, 3, 4)

        def _rmsnorm(x, w, eps=1e-06):
            return x * w * jax.lax.rsqrt(jnp.mean(x * x, axis=-1, keepdims=True) + eps)

        def _parallel_scan(a, b):
            a32 = a.astype(jnp.float32)
            b32 = b.astype(jnp.float32)
            log_A = jnp.cumsum(jnp.log(jnp.maximum(a32, 1e-07)), axis=1)
            log_A = jnp.maximum(log_A, -80.0)
            A = jnp.exp(log_A)
            h = A * jnp.cumsum(b32 * jnp.exp(-log_A), axis=1)
            return h.astype(a.dtype)

        def _rglru_layer(x, cw, cb, wrw, wrb, wiw, wib, la, wow, nw):
            Lx = x.shape[1]
            xp = jnp.pad(x, ((0, 0), (KCONV - 1, 0), (0, 0)))
            x_conv = cb + sum((xp[:, k:k + Lx, :] * cw[:, k] for k in range(KCONV)))
            r_t = jax.nn.sigmoid(x_conv @ wrw.T + wrb)
            i_t = jax.nn.sigmoid(x_conv @ wiw.T + wib)
            a_base = jax.nn.sigmoid(la.astype(jnp.float32)).astype(x.dtype)
            a_t = a_base ** (8.0 * r_t)
            b_t = jnp.sqrt(jnp.clip(1.0 - a_t * a_t, 1e-06, None)) * (i_t * x_conv)
            h = _parallel_scan(a_t, b_t)
            return _rmsnorm(h @ wow.T, nw)
        key = jax.random.key(seed)
        ks = jax.random.split(key, 8)
        inp = {'x': jax.random.normal(ks[0], (B, L, D), jnp.float32), 'conv_w': jax.random.normal(ks[1], (NLAYERS, D, KCONV), jnp.float32) * 0.02, 'conv_b': jnp.zeros((NLAYERS, D), jnp.float32), 'wr_w': jax.random.normal(ks[2], (NLAYERS, D, D), jnp.float32) * (1.0 / np.sqrt(D)), 'wr_b': jnp.zeros((NLAYERS, D), jnp.float32), 'wi_w': jax.random.normal(ks[3], (NLAYERS, D, D), jnp.float32) * (1.0 / np.sqrt(D)), 'wi_b': jnp.zeros((NLAYERS, D), jnp.float32), 'log_a': 3.0 + 0.1 * jax.random.normal(ks[4], (NLAYERS, D), jnp.float32), 'wo_w': jax.random.normal(ks[5], (NLAYERS, D, D), jnp.float32) * (1.0 / np.sqrt(D)), 'norm_w': jnp.ones((NLAYERS, D), jnp.float32), 'norm_out_w': jnp.ones((D,), jnp.float32)}
        return inp
    _L0_attn_all = _L0_attn_setup()
    _L0_attn_in = {k: v for k, v in _L0_attn_all.items() if k in ('conv_w', 'conv_b', 'wr_w', 'wr_b', 'wi_w', 'wi_b', 'log_a', 'wo_w', 'norm_w', 'norm_out_w')}
    del _L0_attn_all

    def _L0_ffn_setup():
        import jax, jax.numpy as jnp
        import numpy as np
        CAPACITY = 2
        B, S, D, E, I = (4, 512, 128, 8, 512)
        key = jax.random.key(seed)
        k0, k1, k2, k3, k4 = jax.random.split(key, 5)
        x = jax.random.normal(k0, (B, S, D), dtype=jnp.float32)
        gate_w = jax.random.normal(k1, (E, D), dtype=jnp.float32) * 0.006
        w_gate = jax.random.normal(k2, (E, I, D), dtype=jnp.float32) * (1.0 / np.sqrt(D))
        w_up = jax.random.normal(k3, (E, I, D), dtype=jnp.float32) * (1.0 / np.sqrt(D))
        w_down = jax.random.normal(k4, (E, D, I), dtype=jnp.float32) * (1.0 / np.sqrt(I))
        return {'x': x, 'gate_w': gate_w, 'w_gate': w_gate, 'w_up': w_up, 'w_down': w_down}
    _L0_ffn_all = _L0_ffn_setup()
    _L0_ffn_in = {k: v for k, v in _L0_ffn_all.items() if k in ('gate_w', 'w_gate', 'w_up', 'w_down')}
    del _L0_ffn_all

    def _L1_xattn_setup():
        import jax, jax.numpy as jnp
        import numpy as np
        EMBED_SIZE = 128
        HEADS = 16
        HEAD_DIM = EMBED_SIZE // HEADS
        B, S = (2, 256)

        def xavier(key, shape):
            fan_in, fan_out = (shape[0], shape[1])
            limit = float(np.sqrt(6.0 / (fan_in + fan_out)))
            return jax.random.uniform(key, shape, jnp.float32, -limit, limit)
        key = jax.random.key(seed)
        ks = jax.random.split(key, 8)
        values = jax.random.normal(ks[0], (B, S, EMBED_SIZE), jnp.float32)
        keys = jax.random.normal(ks[1], (B, S, EMBED_SIZE), jnp.float32)
        query = jax.random.normal(ks[2], (B, S, EMBED_SIZE), jnp.float32)
        mask = jnp.tril(jnp.ones((S, S), jnp.int32))[None, None, :, :]
        return {'values': values, 'keys': keys, 'query': query, 'mask': mask, 'values_weight': xavier(ks[3], (HEAD_DIM, HEAD_DIM)), 'keys_weight': xavier(ks[4], (HEAD_DIM, HEAD_DIM)), 'queries_weight': xavier(ks[5], (HEAD_DIM, HEAD_DIM)), 'fc_weight': xavier(ks[6], (EMBED_SIZE, EMBED_SIZE))}
    _L1_xattn_all = _L1_xattn_setup()
    _L1_xattn_in = {k: v for k, v in _L1_xattn_all.items() if k in ('values_weight', 'keys_weight', 'queries_weight', 'fc_weight')}
    del _L1_xattn_all

    def _L1_attn_setup():
        import jax, jax.numpy as jnp
        import numpy as np
        B, S, D, E, N, K = (4, 256, 128, 256, 16, 4)

        def _layernorm(x, g, b, eps=1e-05):
            mu = jnp.mean(x, axis=-1, keepdims=True)
            var = jnp.var(x, axis=-1, keepdims=True)
            return (x - mu) * jax.lax.rsqrt(var + eps) * g + b

        def _forward(x, ln_g, ln_b, W_in, b_in, conv_w, conv_b, A, Bm, W_c, b_c, W_d, b_d, log_delta, W_out, b_out):
            x_ln = _layernorm(x, ln_g, ln_b)
            x_proj = jnp.einsum('bsd,ed->bse', x_ln, W_in) + b_in
            xp, gate = jnp.split(x_proj, 2, axis=-1)
            xc = jax.lax.conv_general_dilated(xp.transpose(0, 2, 1), conv_w, (1,), [(K - 1, 0)], dimension_numbers=('NCH', 'OIH', 'NCH'), feature_group_count=E)
            xc = (xc + conv_b[None, :, None]).transpose(0, 2, 1)
            xc = jax.nn.silu(xc)
            delta = jax.nn.softplus(log_delta)
            A_diag = jnp.exp(-delta)
            u = (jnp.einsum('bse,fe->bsf', xc, W_c) + b_c) * jax.nn.sigmoid(jnp.einsum('bse,fe->bsf', xc, W_d) + b_d)

            def step(h, u_t):
                h = h * A_diag[None, :, None] + u_t[:, :, None] * Bm[None]
                y = jnp.sum(h * A[None], axis=-1)
                return (h, y)
            h0 = jnp.zeros((x.shape[0], E, N), x.dtype)
            _, ys = jax.lax.scan(step, h0, u.transpose(1, 0, 2))
            x_ssm = ys.transpose(1, 0, 2)
            x_gated = x_ssm * jax.nn.sigmoid(gate)
            out = jnp.einsum('bse,de->bsd', x_gated, W_out) + b_out
            return out + x
        key = jax.random.key(seed)
        ks = jax.random.split(key, 16)
        w = lambda k, shape, s=0.02: jax.random.normal(k, shape, dtype=jnp.float32) * s
        return {'x': jax.random.normal(ks[0], (B, S, D), dtype=jnp.float32), 'ln_g': jnp.ones((D,), jnp.float32), 'ln_b': jnp.zeros((D,), jnp.float32), 'W_in': w(ks[1], (2 * E, D)), 'b_in': jnp.zeros((2 * E,), jnp.float32), 'conv_w': w(ks[2], (E, 1, K), 0.1), 'conv_b': jnp.zeros((E,), jnp.float32), 'A': w(ks[3], (E, N), 0.1), 'Bm': w(ks[4], (E, N), 0.1), 'W_c': w(ks[5], (E, E)), 'b_c': jnp.zeros((E,), jnp.float32), 'W_d': w(ks[6], (E, E)), 'b_d': jnp.zeros((E,), jnp.float32), 'log_delta': jnp.zeros((E,), jnp.float32), 'W_out': w(ks[7], (D, E)), 'b_out': jnp.zeros((D,), jnp.float32)}
    _L1_attn_all = _L1_attn_setup()
    _L1_attn_in = {k: v for k, v in _L1_attn_all.items() if k in ('ln_g', 'ln_b', 'W_in', 'b_in', 'conv_w', 'conv_b', 'A', 'Bm', 'W_c', 'b_c', 'W_d', 'b_d', 'log_delta', 'W_out', 'b_out')}
    del _L1_attn_all

    def _L1_ffn_setup():
        import jax, jax.numpy as jnp
        import numpy as np
        B, L, D, I, E, K = (2, 256, 128, 512, 8, 2)
        LN_EPS = 1e-05

        def _layernorm(x, g, b):
            m = jnp.mean(x, axis=-1, keepdims=True)
            v = jnp.mean(jnp.square(x - m), axis=-1, keepdims=True)
            return (x - m) * jax.lax.rsqrt(v + LN_EPS) * g + b
        key = jax.random.key(seed)
        ks = jax.random.split(key, 4)
        return {'hidden_states': jax.random.normal(ks[0], (B, L, D), dtype=jnp.float32), 'rn_g': jnp.ones((D,), jnp.float32), 'rn_b': jnp.zeros((D,), jnp.float32), 'router_w': jax.random.normal(ks[1], (E, D), jnp.float32) * 0.02, 'router_b': jnp.zeros((E,), jnp.float32), 'ln_g': jnp.ones((E, D), jnp.float32), 'ln_b': jnp.zeros((E, D), jnp.float32), 'w1': jax.random.normal(ks[2], (E, D, I), jnp.float32) * 0.02, 'b1': jnp.zeros((E, I), jnp.float32), 'w2': jax.random.normal(ks[3], (E, I, D), jnp.float32) * 0.02, 'b2': jnp.zeros((E, D), jnp.float32)}
    _L1_ffn_all = _L1_ffn_setup()
    _L1_ffn_in = {k: v for k, v in _L1_ffn_all.items() if k in ('rn_g', 'rn_b', 'router_w', 'router_b', 'ln_g', 'ln_b', 'w1', 'b1', 'w2', 'b2')}
    del _L1_ffn_all
    return {'x': x, 'ctx_1024': ctx_1024, 'mask_1x1xSxS2_ik0': mask_1x1xSxS2_ik0, 'L0_xattn_Wq': _L0_xattn_in['Wq'], 'L0_xattn_bq': _L0_xattn_in['bq'], 'L0_xattn_Wk': _L0_xattn_in['Wk'], 'L0_xattn_bk': _L0_xattn_in['bk'], 'L0_attn_conv_w': _L0_attn_in['conv_w'], 'L0_attn_conv_b': _L0_attn_in['conv_b'], 'L0_attn_wr_w': _L0_attn_in['wr_w'], 'L0_attn_wr_b': _L0_attn_in['wr_b'], 'L0_attn_wi_w': _L0_attn_in['wi_w'], 'L0_attn_wi_b': _L0_attn_in['wi_b'], 'L0_attn_log_a': _L0_attn_in['log_a'], 'L0_attn_wo_w': _L0_attn_in['wo_w'], 'L0_attn_norm_w': _L0_attn_in['norm_w'], 'L0_attn_norm_out_w': _L0_attn_in['norm_out_w'], 'L0_ffn_gate_w': _L0_ffn_in['gate_w'], 'L0_ffn_w_gate': _L0_ffn_in['w_gate'], 'L0_ffn_w_up': _L0_ffn_in['w_up'], 'L0_ffn_w_down': _L0_ffn_in['w_down'], 'L1_xattn_values_weight': _L1_xattn_in['values_weight'], 'L1_xattn_keys_weight': _L1_xattn_in['keys_weight'], 'L1_xattn_queries_weight': _L1_xattn_in['queries_weight'], 'L1_xattn_fc_weight': _L1_xattn_in['fc_weight'], 'L1_attn_ln_g': _L1_attn_in['ln_g'], 'L1_attn_ln_b': _L1_attn_in['ln_b'], 'L1_attn_W_in': _L1_attn_in['W_in'], 'L1_attn_b_in': _L1_attn_in['b_in'], 'L1_attn_conv_w': _L1_attn_in['conv_w'], 'L1_attn_conv_b': _L1_attn_in['conv_b'], 'L1_attn_A': _L1_attn_in['A'], 'L1_attn_Bm': _L1_attn_in['Bm'], 'L1_attn_W_c': _L1_attn_in['W_c'], 'L1_attn_b_c': _L1_attn_in['b_c'], 'L1_attn_W_d': _L1_attn_in['W_d'], 'L1_attn_b_d': _L1_attn_in['b_d'], 'L1_attn_log_delta': _L1_attn_in['log_delta'], 'L1_attn_W_out': _L1_attn_in['W_out'], 'L1_attn_b_out': _L1_attn_in['b_out'], 'L1_ffn_rn_g': _L1_ffn_in['rn_g'], 'L1_ffn_rn_b': _L1_ffn_in['rn_b'], 'L1_ffn_router_w': _L1_ffn_in['router_w'], 'L1_ffn_router_b': _L1_ffn_in['router_b'], 'L1_ffn_ln_g': _L1_ffn_in['ln_g'], 'L1_ffn_ln_b': _L1_ffn_in['ln_b'], 'L1_ffn_w1': _L1_ffn_in['w1'], 'L1_ffn_b1': _L1_ffn_in['b1'], 'L1_ffn_w2': _L1_ffn_in['w2'], 'L1_ffn_b2': _L1_ffn_in['b2']}

def reference(x, ctx_1024, mask_1x1xSxS2_ik0, L0_xattn_Wq, L0_xattn_bq, L0_xattn_Wk, L0_xattn_bk, L0_attn_conv_w, L0_attn_conv_b, L0_attn_wr_w, L0_attn_wr_b, L0_attn_wi_w, L0_attn_wi_b, L0_attn_log_a, L0_attn_wo_w, L0_attn_norm_w, L0_attn_norm_out_w, L0_ffn_gate_w, L0_ffn_w_gate, L0_ffn_w_up, L0_ffn_w_down, L1_xattn_values_weight, L1_xattn_keys_weight, L1_xattn_queries_weight, L1_xattn_fc_weight, L1_attn_ln_g, L1_attn_ln_b, L1_attn_W_in, L1_attn_b_in, L1_attn_conv_w, L1_attn_conv_b, L1_attn_A, L1_attn_Bm, L1_attn_W_c, L1_attn_b_c, L1_attn_W_d, L1_attn_b_d, L1_attn_log_delta, L1_attn_W_out, L1_attn_b_out, L1_ffn_rn_g, L1_ffn_rn_b, L1_ffn_router_w, L1_ffn_router_b, L1_ffn_ln_g, L1_ffn_ln_b, L1_ffn_w1, L1_ffn_b1, L1_ffn_w2, L1_ffn_b2):
    import jax
    import jax.numpy as jnp

    def _L0_xattn_ref(query, key, value, Wq, bq, Wk, bk, scale_factor, dropout_p):
        import jax, jax.numpy as jnp
        import numpy as np
        B, LQ, LKV, D = (8, 256, 256, 128)
        q = jnp.einsum('bld,ed->ble', query, Wq) + bq
        k = jnp.einsum('bld,ed->ble', key, Wk) + bk
        scores = jnp.einsum('bqd,bkd->bqk', q, k) / jnp.float32(scale_factor)
        attn = jax.nn.softmax(scores, axis=-1)
        return jnp.einsum('bqk,bkd->bqd', attn, value)

    def _L0_attn_ref(x, conv_w, conv_b, wr_w, wr_b, wi_w, wi_b, log_a, wo_w, norm_w, norm_out_w):
        import jax, jax.numpy as jnp
        import numpy as np
        B, L, D, NLAYERS, KCONV = (8, 256, 128, 3, 4)

        def _rmsnorm(x, w, eps=1e-06):
            return x * w * jax.lax.rsqrt(jnp.mean(x * x, axis=-1, keepdims=True) + eps)

        def _parallel_scan(a, b):
            a32 = a.astype(jnp.float32)
            b32 = b.astype(jnp.float32)
            log_A = jnp.cumsum(jnp.log(jnp.maximum(a32, 1e-07)), axis=1)
            log_A = jnp.maximum(log_A, -80.0)
            A = jnp.exp(log_A)
            h = A * jnp.cumsum(b32 * jnp.exp(-log_A), axis=1)
            return h.astype(a.dtype)

        def _rglru_layer(x, cw, cb, wrw, wrb, wiw, wib, la, wow, nw):
            Lx = x.shape[1]
            xp = jnp.pad(x, ((0, 0), (KCONV - 1, 0), (0, 0)))
            x_conv = cb + sum((xp[:, k:k + Lx, :] * cw[:, k] for k in range(KCONV)))
            r_t = jax.nn.sigmoid(x_conv @ wrw.T + wrb)
            i_t = jax.nn.sigmoid(x_conv @ wiw.T + wib)
            a_base = jax.nn.sigmoid(la.astype(jnp.float32)).astype(x.dtype)
            a_t = a_base ** (8.0 * r_t)
            b_t = jnp.sqrt(jnp.clip(1.0 - a_t * a_t, 1e-06, None)) * (i_t * x_conv)
            h = _parallel_scan(a_t, b_t)
            return _rmsnorm(h @ wow.T, nw)
        h = x
        for l in range(NLAYERS):
            h = _rglru_layer(h, conv_w[l], conv_b[l], wr_w[l], wr_b[l], wi_w[l], wi_b[l], log_a[l], wo_w[l], norm_w[l])
        return _rmsnorm(h, norm_out_w)

    def _L0_ffn_ref(x, gate_w, w_gate, w_up, w_down):
        import jax, jax.numpy as jnp
        import numpy as np
        CAPACITY = 2
        B, S, D = x.shape
        E = gate_w.shape[0]
        k = S // E * CAPACITY
        logits = jnp.einsum('bsd,ed->bse', x, gate_w)
        affinity = jax.nn.softmax(logits, axis=-1)
        affinity = jnp.transpose(affinity, (0, 2, 1))
        gating, idx = jax.lax.top_k(affinity, k)
        bidx = jnp.arange(B)[:, None, None]
        x_in = x[bidx, idx]
        h = jax.nn.silu(jnp.einsum('bekd,eid->beki', x_in, w_gate)) * jnp.einsum('bekd,eid->beki', x_in, w_up)
        x_e = jnp.einsum('beki,edi->bekd', h, w_down)
        out = jnp.zeros_like(x).at[bidx, idx].add(gating[..., None] * x_e)
        return out

    def _L1_xattn_ref(values, keys, query, mask, values_weight, keys_weight, queries_weight, fc_weight):
        import jax, jax.numpy as jnp
        import numpy as np
        EMBED_SIZE = 128
        HEADS = 16
        HEAD_DIM = EMBED_SIZE // HEADS
        B, S = (2, 256)

        def xavier(key, shape):
            fan_in, fan_out = (shape[0], shape[1])
            limit = float(np.sqrt(6.0 / (fan_in + fan_out)))
            return jax.random.uniform(key, shape, jnp.float32, -limit, limit)
        n, q_len, _ = query.shape
        v = values.reshape(n, -1, HEADS, HEAD_DIM)
        k = keys.reshape(n, -1, HEADS, HEAD_DIM)
        q = query.reshape(n, q_len, HEADS, HEAD_DIM)
        v = jnp.einsum('nlhd,df->nlhf', v, values_weight)
        k = jnp.einsum('nlhd,df->nlhf', k, keys_weight)
        q = jnp.einsum('nqhd,df->nqhf', q, queries_weight)
        energy = jnp.einsum('nqhd,nkhd->nhqk', q, k)
        energy = jnp.where(mask == 0, jnp.float32(-1e+20), energy)
        attn = jax.nn.softmax(energy / jnp.sqrt(jnp.float32(EMBED_SIZE)), axis=3)
        out = jnp.einsum('nhql,nlhd->nqhd', attn, v).reshape(n, q_len, EMBED_SIZE)
        return jnp.einsum('nqd,df->nqf', out, fc_weight)

    def _L1_attn_ref(x, ln_g, ln_b, W_in, b_in, conv_w, conv_b, A, Bm, W_c, b_c, W_d, b_d, log_delta, W_out, b_out):
        import jax, jax.numpy as jnp
        import numpy as np
        B, S, D, E, N, K = (4, 256, 128, 256, 16, 4)

        def _layernorm(x, g, b, eps=1e-05):
            mu = jnp.mean(x, axis=-1, keepdims=True)
            var = jnp.var(x, axis=-1, keepdims=True)
            return (x - mu) * jax.lax.rsqrt(var + eps) * g + b

        def _forward(x, ln_g, ln_b, W_in, b_in, conv_w, conv_b, A, Bm, W_c, b_c, W_d, b_d, log_delta, W_out, b_out):
            x_ln = _layernorm(x, ln_g, ln_b)
            x_proj = jnp.einsum('bsd,ed->bse', x_ln, W_in) + b_in
            xp, gate = jnp.split(x_proj, 2, axis=-1)
            xc = jax.lax.conv_general_dilated(xp.transpose(0, 2, 1), conv_w, (1,), [(K - 1, 0)], dimension_numbers=('NCH', 'OIH', 'NCH'), feature_group_count=E)
            xc = (xc + conv_b[None, :, None]).transpose(0, 2, 1)
            xc = jax.nn.silu(xc)
            delta = jax.nn.softplus(log_delta)
            A_diag = jnp.exp(-delta)
            u = (jnp.einsum('bse,fe->bsf', xc, W_c) + b_c) * jax.nn.sigmoid(jnp.einsum('bse,fe->bsf', xc, W_d) + b_d)

            def step(h, u_t):
                h = h * A_diag[None, :, None] + u_t[:, :, None] * Bm[None]
                y = jnp.sum(h * A[None], axis=-1)
                return (h, y)
            h0 = jnp.zeros((x.shape[0], E, N), x.dtype)
            _, ys = jax.lax.scan(step, h0, u.transpose(1, 0, 2))
            x_ssm = ys.transpose(1, 0, 2)
            x_gated = x_ssm * jax.nn.sigmoid(gate)
            out = jnp.einsum('bse,de->bsd', x_gated, W_out) + b_out
            return out + x
        return _forward(x, ln_g, ln_b, W_in, b_in, conv_w, conv_b, A, Bm, W_c, b_c, W_d, b_d, log_delta, W_out, b_out)

    def _L1_ffn_ref(hidden_states, rn_g, rn_b, router_w, router_b, ln_g, ln_b, w1, b1, w2, b2):
        import jax, jax.numpy as jnp
        import numpy as np
        B, L, D, I, E, K = (2, 256, 128, 512, 8, 2)
        LN_EPS = 1e-05

        def _layernorm(x, g, b):
            m = jnp.mean(x, axis=-1, keepdims=True)
            v = jnp.mean(jnp.square(x - m), axis=-1, keepdims=True)
            return (x - m) * jax.lax.rsqrt(v + LN_EPS) * g + b
        normed = _layernorm(hidden_states, rn_g, rn_b)
        logits = (jnp.einsum('bld,ed->ble', normed, router_w) + router_b).astype(jnp.float32)
        top_w, top_idx = jax.lax.top_k(logits, K)
        top_w = jax.nn.softmax(top_w, axis=-1).astype(hidden_states.dtype)
        onehot = jax.nn.one_hot(top_idx, E, dtype=top_w.dtype)
        combine = jnp.einsum('blke,blk->ble', onehot, top_w)
        out = jnp.zeros_like(hidden_states)
        for e in range(E):
            h = _layernorm(hidden_states, ln_g[e], ln_b[e])
            h = jax.nn.gelu(jnp.einsum('bld,di->bli', h, w1[e]) + b1[e], approximate=False)
            h = jnp.einsum('bli,id->bld', h, w2[e]) + b2[e]
            out = out + combine[..., e:e + 1] * h
        return out
    x = x + _L0_xattn_ref(_layernorm(x, axis=-1), ctx_1024, ctx_1024, L0_xattn_Wq, L0_xattn_bq, L0_xattn_Wk, L0_xattn_bk, 32, 0)
    x = x + _L0_attn_ref(_layernorm(x, axis=-1), L0_attn_conv_w, L0_attn_conv_b, L0_attn_wr_w, L0_attn_wr_b, L0_attn_wi_w, L0_attn_wi_b, L0_attn_log_a, L0_attn_wo_w, L0_attn_norm_w, L0_attn_norm_out_w)
    x = x + _L0_ffn_ref(_layernorm(x, axis=-1), L0_ffn_gate_w, L0_ffn_w_gate, L0_ffn_w_up, L0_ffn_w_down)
    x = x + _L1_xattn_ref(ctx_1024, ctx_1024, _layernorm(x, axis=-1), mask_1x1xSxS2_ik0, L1_xattn_values_weight, L1_xattn_keys_weight, L1_xattn_queries_weight, L1_xattn_fc_weight)
    x = x + _L1_attn_ref(_layernorm(x, axis=-1), L1_attn_ln_g, L1_attn_ln_b, L1_attn_W_in, L1_attn_b_in, L1_attn_conv_w, L1_attn_conv_b, L1_attn_A, L1_attn_Bm, L1_attn_W_c, L1_attn_b_c, L1_attn_W_d, L1_attn_b_d, L1_attn_log_delta, L1_attn_W_out, L1_attn_b_out)
    x = x + _L1_ffn_ref(_layernorm(x, axis=-1), L1_ffn_rn_g, L1_ffn_rn_b, L1_ffn_router_w, L1_ffn_router_b, L1_ffn_ln_g, L1_ffn_ln_b, L1_ffn_w1, L1_ffn_b1, L1_ffn_w2, L1_ffn_b2)
    return x

_drawn_inputs = setup_inputs


def setup_inputs(seed=0):
    import zlib

    import numpy as np

    out = dict(_drawn_inputs(seed))
    spreads = {'L0_attn_conv_b': (0.0, 0.1),
     'L0_attn_wr_b': (0.0, 0.421),
     'L0_attn_wi_b': (0.0, 0.1),
     'L0_attn_norm_w': (1.0, 0.2),
     'L0_attn_norm_out_w': (1.0, 0.2),
     'L1_attn_ln_g': (1.0, 0.6),
     'L1_attn_ln_b': (0.0, 0.8),
     'L1_attn_b_in': (0.0, 0.8),
     'L1_attn_conv_b': (0.0, 0.8),
     'L1_attn_b_c': (0.0, 0.8),
     'L1_attn_b_d': (0.0, 0.8),
     'L1_attn_log_delta': (0.0, 0.8),
     'L1_attn_b_out': (0.0, 2.0),
     'L1_ffn_rn_g': (1.0, 0.6),
     'L1_ffn_rn_b': (0.0, 2.0),
     'L1_ffn_router_b': (0.0, 1.177),
     'L1_ffn_ln_g': (1.0, 0.6),
     'L1_ffn_ln_b': (0.0, 2.0),
     'L1_ffn_b1': (0.0, 2.0),
     'L1_ffn_b2': (0.0, 2.0)}
    factors = {'L0_xattn_Wq': 3.317,
     'L0_xattn_bq': 8.0,
     'L0_xattn_Wk': 3.27,
     'L0_xattn_bk': 200.0,
     'L0_attn_wr_w': 2.983,
     'L1_attn_W_in': 8.0,
     'L1_attn_conv_w': 8.0,
     'L1_attn_A': 8.0,
     'L1_attn_Bm': 8.0,
     'L1_attn_W_c': 8.0,
     'L1_attn_W_d': 8.0,
     'L1_attn_W_out': 8.0,
     'L1_ffn_w1': 3.727,
     'L1_ffn_w2': 3.31,
     'L1_ffn_router_w': 4.393}
    for name, (base, spread) in spreads.items():
        noise = np.random.default_rng([zlib.crc32(name.encode()), seed]).standard_normal(out[name].shape)
        drawn = base * np.exp(spread * noise) if base else spread * noise
        out[name] = jnp.asarray(drawn.astype(out[name].dtype))
    for name, factor in factors.items():
        out[name] = (out[name] * factor).astype(out[name].dtype)
    return out
```

```python
from contextlib import ExitStack

import numpy as np

import concourse.bass as bass
from concourse import mybir

F32 = mybir.dt.float32
BF16 = mybir.dt.bfloat16
ALU = mybir.AluOpType
ACT = mybir.ActivationFunctionType
AX_X = mybir.AxisListType.X
ds = bass.ds

P = 128
D = 128
B, S, KV = 64, 64, 128
TILES = B * S // P
TPI = 8
BPI = 2 * TPI
N = TPI * P
STEPS = TILES // TPI
HALF = N // 2
LN_EPS = 1e-5
RMS_EPS = 1e-6
LAYERS, TAPS = 3, 4
E0, CAP, I0 = 8, S // 8 * 2, 512
HEADS, HD = 16, 8
CH, SN = 256, 16
E1, I1 = 8, 512

PACK = [
    ("wqT", D), ("wkT", D), ("bq", 1), ("bk", 1),
    ("wrT", LAYERS * D), ("wiT", LAYERS * D), ("woT", LAYERS * D), ("cw", LAYERS * TAPS), ("cb", LAYERS),
    ("rb", LAYERS), ("ib", LAYERS), ("log_a", LAYERS), ("norm_w", LAYERS), ("norm_out", 1),
    ("router0", E0),
    ("q_bd", D), ("k_bd", D), ("v_bd", D), ("fc", D),
    ("in_g", 1), ("in_b", 1), ("w_inT", 2 * CH), ("b_in", 4), ("conv_w", 2 * TAPS), ("conv_b", 2),
    ("ssm_A", 2 * SN), ("ssm_B", 2 * SN), ("w_cT", 2 * CH), ("w_dT", 2 * CH), ("b_c", 2), ("b_d", 2),
    ("log_delta", 2), ("w_outT", 2 * D),
    ("rn_g", 1), ("rn_b", 1), ("router1", E1), ("ln_gT", E1), ("ln_bT", E1), ("b1", E1 * 4),
]
AT, _at = {}, 0
for _name, _w in PACK:
    AT[_name] = (_at, _at + _w)
    _at += _w
PACKED = _at


def semaphores(nc, ctx, prefix):
    taken = []

    def give_back():
        nc.clear_and_free_semaphores(taken)
        nc.all_engine_barrier()

    ctx.callback(give_back)

    def sem(name):
        taken.append(nc.alloc_semaphore(prefix + name))
        return taken[-1]

    return sem


class Steps:

    def __init__(self, eng, sem, j=0, per=0, base=0):
        self.eng, self.sem, self.j, self.per, self.base, self.k = eng, sem, j, per, base, 0

    def done(self, ins):
        self.k += 1
        ins.then_inc(self.sem, 1)
        self.eng.wait_ge(self.sem, self.j * self.per + (self.base + self.k))

    def close(self):
        assert self.k == self.per, (self.k, self.per)


class Chip:

    def __init__(self, nc, ctx):
        self.nc = nc

        def sb(name, shape, dt=F32):
            return ctx.enter_context(nc.sbuf_tensor("c_" + name, shape, dt))

        self.x = sb("x", [P, TILES, D])
        self.xn = sb("xn", [P, TPI, D])
        self.stats = sb("stats", [P, TPI, 6])
        self.mv = sb("mv", [P, TPI, 2])
        self.ve = sb("ve", [P, TPI])
        self.rstd = sb("rstd", [P, TPI])
        self.spare = sb("spare", [P, 1])
        self.eps = sb("eps", [P, TPI])
        self.neghalf = sb("neghalf", [P, TPI])
        self.w = sb("w", [P, PACKED])
        self.ident = sb("ident", [P, P])
        self.ones = sb("ones", [P, P])
        self.w1 = sb("w1", [P, E1, I1])
        self.w2 = sb("w2", [P, E1 * I1 // P, D])
        self.ffn0_in = ctx.enter_context(nc.semaphore("ffn0_in"))
        self.ffn1_in = ctx.enter_context(nc.semaphore("ffn1_in"))

    def place_ffn0(self, ctx):
        sb = lambda name, shape: ctx.enter_context(self.nc.sbuf_tensor("c_" + name, shape, F32))
        self.gate0 = sb("gate0", [P, E0, I0])
        self.up0 = sb("up0", [P, E0, I0])
        self.down0 = sb("down0", [P, E0 * I0 // P, D])

    def weight(self, name, rows=P):
        a, b = AT[name]
        return self.w[0:rows, a:b]



def norm_stats(chip, steps, jn, mv_ready):
    nc = chip.nc
    for t in range(TPI):
        last = nc.vector.bn_stats(chip.stats[:, t, :], chip.x[:, ds(jn * TPI + t, 1), :])
    steps.done(last)
    nc.vector.tensor_copy(chip.spare[:], chip.stats[:, 0, 0:1])
    for t in range(TPI):
        last = nc.vector.bn_aggr(chip.mv[:, t, :], chip.stats[:, t, :])
    last.then_inc(mv_ready, 1)


def norm_rstd(chip, pool, j, mv_ready, pool_steps, rstd_ready):
    nc = chip.nc
    pool.wait_ge(mv_ready, j + 1)
    pool_steps.done(nc.gpsimd.tensor_tensor(chip.ve[:], chip.mv[:, :, 1], chip.eps[:], ALU.add))
    nc.gpsimd.tensor_tensor(chip.rstd[:], chip.ve[:], chip.neghalf[:], ALU.pow).then_inc(rstd_ready, 1)


def norm_rows(chip, dve, jn, j, rstd_ready, xn_ready):
    nc = chip.nc
    dve.wait_ge(rstd_ready, j + 1)
    for t in range(TPI):
        last = nc.vector.tensor_scalar(chip.xn[:, t, :], chip.x[:, ds(jn * TPI + t, 1), :], chip.mv[:, t, 0:1],
                                       chip.rstd[:, t:t + 1], ALU.subtract, ALU.mult)
    last.then_inc(xn_ready, 1)


def fetch_ffn0(chip, sp, gate, up, down):
    for dst, src in ((chip.gate0, gate), (chip.up0, up), (chip.down0, down)):
        sp.dma_start(dst[:], src).then_inc(chip.ffn0_in, 16)


def fetch_ffn1(chip, sp, w1, w2):
    for dst, src in ((chip.w1, w1), (chip.w2, w2)):
        sp.dma_start(dst[:], src).then_inc(chip.ffn1_in, 16)


def stage_load(chip, x_dram, pack_dram, fetch=None):
    nc = chip.nc
    with ExitStack() as ctx:
        sem = semaphores(nc, ctx, "")
        x_in, x_first, w_in = sem("ld_x"), sem("ld_x0"), sem("ld_w")
        made, mv_ready, rstd_ready, xn_ready = sem("ld_made"), sem("ld_mv"), sem("ld_rstd"), sem("ld_xn")
        dve_steps, pool_steps = sem("ld_dve"), sem("ld_pool")
        block = ctx.enter_context(nc.Block())

        @block.sync
        def _(sp):
            xr = x_dram.rearrange("(t p) d -> p t d", p=P)
            sp.dma_start(chip.x[:, 0:TPI, :], xr[:, 0:TPI, :]).then_inc(x_first, 16)
            for n in range(1, STEPS):
                sp.dma_start(chip.x[:, n * TPI:(n + 1) * TPI, :], xr[:, n * TPI:(n + 1) * TPI, :]).then_inc(x_in, 16)
            if fetch:
                fetch(sp)
            sp.wait_ge(x_in, 16 * (STEPS - 1))

        @block.scalar
        def _(act):
            act.dma_start(chip.w[:], pack_dram).then_inc(w_in, 16)
            act.wait_ge(w_in, 16)

        @block.gpsimd
        def _(pool):
            nc.gpsimd.memset(chip.neghalf[:], -0.5).then_inc(made, 1)
            nc.gpsimd.memset(chip.ones[:], 1.0).then_inc(made, 1)
            nc.gpsimd.memset(chip.eps[:], LN_EPS).then_inc(made, 1)
            nc.gpsimd.memset(chip.ident[:], 0.0).then_inc(made, 1)
            pool.wait_ge(made, 4)
            nc.gpsimd.affine_select(out=chip.ident[:], in_=chip.ident[:], compare_op=ALU.not_equal, fill=1.0,
                                    base=0, pattern=[[-1, P]], channel_multiplier=1).then_inc(made, 1)
            norm_rstd(chip, pool, 0, mv_ready, Steps(pool, pool_steps), rstd_ready)

        @block.vector
        def _(dve):
            dve.wait_ge(x_first, 16)
            steps = Steps(dve, dve_steps)
            norm_stats(chip, steps, 0, mv_ready)
            norm_rows(chip, dve, 0, 0, rstd_ready, xn_ready)


def stage_cross0(chip, ctx_dram, ctxT_dram, fetch):
    nc = chip.nc
    SCALE = 1.0 / 32.0
    with ExitStack() as ctx:
        def sb(name, shape, dt=F32):
            return ctx.enter_context(nc.sbuf_tensor("a_" + name, shape, dt))

        def bank(name, shape):
            return ctx.enter_context(nc.psum_tensor("a_" + name, shape, F32))

        sem = semaphores(nc, ctx, "a_")

        ctx_n = sb("ctx_n", [P, BPI, D])
        ctx_t = sb("ctx_t", [P, BPI * KV])
        xT = sb("xT", [P, N])
        qT = sb("qT", [P, N])
        kT = sb("kT", [P, BPI * KV])
        prob = sb("prob", [P, TPI, KV])
        probT = sb("probT", [P, N])
        top = sb("top", [P, TPI])
        negtop = sb("negtop", [P, TPI])
        total = sb("total", [P, TPI])
        share = sb("share", [P, TPI])
        bank_xs = [bank(f"xs{u}", [P, 4, KV]) for u in range(2)]
        bank_qp = [bank(f"qp{u}", [P, HALF]) for u in range(2)]
        bank_k = [bank(f"k{u}", [P, HALF]) for u in range(2)]
        bank_o = [bank(f"o{u}", [P, 4, D]) for u in range(2)]
        ctxT_in, ctx_in = sem("ctxT_in"), sem("ctx_in")
        xT_ps, xT_sb, q_ps, q_sb, k_ps, k_sb = (sem(n) for n in ("xT_ps", "xT_sb", "q_ps", "q_sb", "k_ps", "k_sb"))
        scores, negtop_ready, prob_sb, probT_ps, probT_sb = (
            sem(n) for n in ("scores", "negtop", "prob_sb", "probT_ps", "probT_sb"))
        o_ps, x_done = sem("o_ps"), sem("x_done")
        mv_ready, rstd_ready, xn_ready = sem("mv"), sem("rstd"), sem("xn")
        dve_steps, pool_steps = sem("dve"), sem("pool")
        block = ctx.enter_context(nc.Block())

        @block.sync
        def _(sp):
            flat = ctx_n[:].rearrange("k b d -> k (b d)")
            sp.dma_start(ctx_t[:], ctxT_dram[:, 0:BPI * KV]).then_inc(ctxT_in, 16)
            sp.dma_start(flat, ctx_dram[:, 0:BPI * D]).then_inc(ctx_in, 16)
            with sp.Fori(1, STEPS) as j:
                sp.wait_ge(k_ps, j * 4)
                sp.dma_start(ctx_t[:], ctxT_dram[:, ds(j * (BPI * KV), BPI * KV)]).then_inc(ctxT_in, 16)
                sp.wait_ge(o_ps, j * 2)
                sp.dma_start(flat, ctx_dram[:, ds(j * (BPI * D), BPI * D)]).then_inc(ctx_in, 16)
            fetch(sp)

        @block.tensor
        def _(pe):
            with pe.Fori(0, STEPS) as j:
                for u in range(2):
                    for t in range(4):
                        last = nc.tensor.transpose(bank_xs[u][:, t, :], chip.xn[:, 4 * u + t, :], chip.ident[:])
                    last.then_inc(xT_ps, 1)
                pe.wait_ge(ctxT_in, j * 16 + 16)
                for c in range(4):
                    if c >= 2:
                        pe.wait_ge(k_sb, j * 4 + (c - 1))
                    nc.tensor.matmul(bank_k[c % 2][:], chip.weight("wkT"), ctx_t[:, c * HALF:(c + 1) * HALF],
                                     start=True, stop=True).then_inc(k_ps, 1)
                for u in range(2):
                    pe.wait_ge(xT_sb, j * 2 + u + 1)
                    nc.tensor.matmul(bank_qp[u][:], chip.weight("wqT"), xT[:, u * HALF:(u + 1) * HALF],
                                     start=True, stop=True).then_inc(q_ps, 1)
                for u in range(2):
                    pe.wait_ge(q_sb, j * 2 + u + 1)
                    pe.wait_ge(k_sb, j * 4 + 2 * u + 2)
                    for t in range(4):
                        for h in range(2):
                            b = 2 * (4 * u + t) + h
                            last = nc.tensor.matmul(bank_xs[u][64 * h:64 * h + 64, t, :], qT[:, b * S:(b + 1) * S],
                                                    kT[:, b * KV:(b + 1) * KV], start=True, stop=True)
                    last.then_inc(scores, 1)
                for u in range(2):
                    for t in range(4):
                        pe.wait_ge(prob_sb, j * 8 + 4 * u + t + 1)
                        last = nc.tensor.transpose(bank_qp[u][:, t * P:(t + 1) * P], prob[:, 4 * u + t, :], chip.ident[:])
                    last.then_inc(probT_ps, 1)
                pe.wait_ge(ctx_in, j * 16 + 16)
                for u in range(2):
                    pe.wait_ge(probT_sb, j * 2 + u + 1)
                    for t in range(4):
                        for h in range(2):
                            b = 2 * (4 * u + t) + h
                            last = nc.tensor.matmul(bank_o[u][64 * h:64 * h + 64, t, :], probT[:, b * S:(b + 1) * S],
                                                    ctx_n[:, b, :], start=True, stop=True)
                    last.then_inc(o_ps, 1)
                pe.wait_ge(xn_ready, j + 1)

        @block.scalar
        def _(act):
            with act.Fori(0, STEPS) as j:
                for u in range(2):
                    act.wait_ge(xT_ps, j * 2 + u + 1)
                    nc.scalar.activation(xT[:, u * HALF:(u + 1) * HALF], bank_xs[u][:].rearrange("p t k -> p (t k)"),
                                         ACT.Identity).then_inc(xT_sb, 1)
                for c in range(4):
                    act.wait_ge(k_ps, j * 4 + c + 1)
                    nc.scalar.activation(kT[:, c * HALF:(c + 1) * HALF], bank_k[c % 2][:], ACT.Identity,
                                         bias=chip.weight("bk")).then_inc(k_sb, 1)
                    if c % 2:
                        u = c // 2
                        act.wait_ge(q_ps, j * 2 + u + 1)
                        nc.scalar.activation(qT[:, u * HALF:(u + 1) * HALF], bank_qp[u][:], ACT.Identity,
                                             bias=chip.weight("bq")).then_inc(q_sb, 1)
                for u in range(2):
                    act.wait_ge(negtop_ready, j * 2 + u + 1)
                    for t in range(4):
                        nc.scalar.activation(prob[:, 4 * u + t, :], bank_xs[u][:, t, :], ACT.Exp, scale=SCALE,
                                             bias=negtop[:, 4 * u + t:4 * u + t + 1],
                                             accum_out=total[:, 4 * u + t:4 * u + t + 1]).then_inc(prob_sb, 1)

        @block.gpsimd
        def _(pool):
            with pool.Fori(0, STEPS) as j:
                norm_rstd(chip, pool, j, mv_ready, Steps(pool, pool_steps, j, 1), rstd_ready)

        @block.vector
        def _(dve):
            with dve.Fori(0, STEPS) as j:
                steps = Steps(dve, dve_steps, j, 5)
                jn = (j + 1) % STEPS
                norm_stats(chip, steps, jn, mv_ready)
                for u in range(2):
                    dve.wait_ge(scores, j * 2 + u + 1)
                    steps.done(nc.vector.tensor_reduce(top[:, 4 * u:4 * u + 4], bank_xs[u][:], AX_X, ALU.max))
                    nc.vector.tensor_scalar(negtop[:, 4 * u:4 * u + 4], top[:, 4 * u:4 * u + 4], -SCALE, None,
                                            ALU.mult).then_inc(negtop_ready, 1)
                for u in range(2):
                    dve.wait_ge(probT_ps, j * 2 + u + 1)
                    nc.vector.tensor_copy(probT[:, u * HALF:(u + 1) * HALF], bank_qp[u][:]).then_inc(probT_sb, 1)
                for u in range(2):
                    dve.wait_ge(prob_sb, j * 8 + 4 * u + 4)
                    steps.done(nc.vector.reciprocal(share[:, 4 * u:4 * u + 4], total[:, 4 * u:4 * u + 4]))
                    dve.wait_ge(o_ps, j * 2 + u + 1)
                    for t in range(4):
                        last = nc.vector.scalar_tensor_tensor(
                            chip.x[:, ds(j * TPI + 4 * u + t, 1), :], bank_o[u][:, t, :], share[:, 4 * u + t:4 * u + t + 1],
                            chip.x[:, ds(j * TPI + 4 * u + t, 1), :], ALU.mult, ALU.add)
                    last.then_inc(x_done, 1)
                dve.wait_ge(x_done, j * 2 + 2)
                norm_rows(chip, dve, jn, j, rstd_ready, xn_ready)
                steps.close()


def stage_recurrence(chip):
    nc = chip.nc
    LOG_A_MIN, LOG_SUM_MIN = float(np.log(1e-7)), -80.0
    with ExitStack() as ctx:
        def sb(name, shape, dt=F32):
            return ctx.enter_context(nc.sbuf_tensor("b_" + name, shape, dt))

        def bank(name, shape):
            return ctx.enter_context(nc.psum_tensor("b_" + name, shape, F32))

        sem = semaphores(nc, ctx, "b_")

        hT = sb("hT", [P, 2, HALF])
        xc = sb("xc", [P, 2, HALF])
        r = sb("r", [P, 2, HALF])
        g = sb("g", [P, 2, HALF])
        run = sb("run", [P, 2, HALF])
        a2 = sb("a2", [P, 2, HALF])
        grow = sb("grow", [P, 2, HALF])
        decay = sb("decay", [P, 2, HALF])
        acc = sb("acc", [P, 2, HALF])
        sq = sb("sq", [P, 2, HALF])
        rs = sb("rs", [P, 2, HALF])
        fresh = sb("fresh", [P, HALF])
        rate = sb("rate", [P, LAYERS])
        rate8 = sb("rate8", [P, LAYERS])
        rate16 = sb("rate16", [P, LAYERS])
        rms_eps = sb("rms_eps", [P, 1])
        bank_r = [bank(f"r{u}", [P, HALF]) for u in range(2)]
        bank_i = [bank(f"i{u}", [P, HALF]) for u in range(2)]
        bank_y = [bank(f"y{u}", [P, HALF]) for u in range(2)]
        bank_m = [bank(f"m{u}", [P, HALF]) for u in range(2)]
        const, rate_e, rate_l, rate_done = sem("const"), sem("rate_e"), sem("rate_l"), sem("rate")
        xT_ps, hT_ready, xc_ready, gates_ps, gates_sb = (sem(n) for n in ("xT_ps", "hT", "xc", "gates_ps", "gates_sb"))
        a2_ready, clip_ready, ix_ready, ln_ready, t_ready, e_ready = (
            sem(n) for n in ("a2_s", "clip", "ix", "ln", "t", "e"))
        h_ready, y_ps, sq_ready, m_ps, var_ln, rs_ready = (sem(n) for n in ("h", "y_ps", "sq_s", "m_ps", "var_ln", "rs_s"))
        z_ready, zT_ps = sem("z"), sem("zT_ps")
        mv_ready, rstd_ready, xn_ready = sem("mv"), sem("rstd"), sem("xn")
        dve_steps, pool_steps = sem("dve"), sem("pool")
        block = ctx.enter_context(nc.Block())
        batches = lambda ap: ap.rearrange("p (b s) -> p b s", s=S)

        @block.tensor
        def _(pe):
            pe.wait_ge(const, 1)
            with pe.Fori(0, STEPS) as j:
                for u in range(2):
                    for t in range(4):
                        last = nc.tensor.transpose(bank_y[u][:, t * P:(t + 1) * P], chip.xn[:, 4 * u + t, :], chip.ident[:])
                    last.then_inc(xT_ps, 1)
                for l in range(LAYERS):
                    w = slice(l * D, (l + 1) * D)
                    for u in range(2):
                        n = 2 * l + u + 1
                        pe.wait_ge(xc_ready, j * 6 + n)
                        nc.tensor.matmul(bank_r[u][:], chip.weight("wrT")[:, w], xc[:, u, :], start=True, stop=True)
                        nc.tensor.matmul(bank_i[u][:], chip.weight("wiT")[:, w], xc[:, u, :],
                                         start=True, stop=True).then_inc(gates_ps, 1)
                    for u in range(2):
                        n = 2 * l + u + 1
                        pe.wait_ge(h_ready, j * 6 + n)
                        nc.tensor.matmul(bank_y[u][:], chip.weight("woT")[:, w], acc[:, u, :],
                                         start=True, stop=True).then_inc(y_ps, 1)
                    for u in range(2):
                        pe.wait_ge(sq_ready, j * 8 + (2 * l + u + 1))
                        nc.tensor.matmul(bank_m[u][:], chip.ones[:], sq[:, u, :], start=True, stop=True).then_inc(m_ps, 1)
                for u in range(2):
                    pe.wait_ge(sq_ready, j * 8 + (6 + u + 1))
                    nc.tensor.matmul(bank_m[u][:], chip.ones[:], sq[:, u, :], start=True, stop=True).then_inc(m_ps, 1)
                for u in range(2):
                    pe.wait_ge(z_ready, j * 2 + (u + 1))
                    for t in range(4):
                        last = nc.tensor.transpose(bank_r[u][:, t * P:(t + 1) * P], xc[:, u, t * P:(t + 1) * P], chip.ident[:])
                    last.then_inc(zT_ps, 1)
                pe.wait_ge(xn_ready, j + 1)

        @block.scalar
        def _(act):
            act.wait_ge(const, 1)
            nc.scalar.activation(rate[:], chip.weight("log_a"), ACT.Exp, scale=-1.0).then_inc(rate_e, 1)
            act.wait_ge(rate_e, 1)
            nc.scalar.activation(rate[:], rate[:], ACT.Ln, bias=1.0).then_inc(rate_l, 1)
            act.wait_ge(rate_done, 1)

            def mean_square(j, n, u, src):
                nc.scalar.activation(sq[:, u, :], src, ACT.Square).then_inc(sq_ready, 1)

            def root(j, n, u):
                act.wait_ge(m_ps, j * 8 + n)
                nc.scalar.activation(rs[:, u, :], bank_m[u][:], ACT.Ln, scale=1.0 / D, bias=rms_eps[:]).then_inc(var_ln, 1)
                act.wait_ge(var_ln, j * 8 + n)
                nc.scalar.activation(rs[:, u, :], rs[:, u, :], ACT.Exp, scale=-0.5).then_inc(rs_ready, 1)

            with act.Fori(0, STEPS) as j:
                for u in range(2):
                    act.wait_ge(xT_ps, j * 2 + u + 1)
                    nc.scalar.activation(hT[:, u, :], bank_y[u][:], ACT.Identity).then_inc(hT_ready, 1)
                for l in range(LAYERS):
                    for u in range(2):
                        n = 2 * l + u + 1
                        act.wait_ge(gates_ps, j * 6 + n)
                        nc.scalar.activation(r[:, u, :], bank_r[u][:], ACT.Sigmoid, bias=chip.weight("rb")[:, l:l + 1])
                        nc.scalar.activation(g[:, u, :], bank_i[u][:], ACT.Sigmoid,
                                             bias=chip.weight("ib")[:, l:l + 1]).then_inc(gates_sb, 1)
                    act.preload_act_table_set("natural_log_exp_and_others")
                    for u in range(2):
                        n = 2 * l + u + 1
                        act.wait_ge(gates_sb, j * 6 + n)
                        nc.scalar.activation(a2[:, u, :], r[:, u, :], ACT.Exp, scale=rate16[:, l:l + 1]).then_inc(a2_ready, 1)
                    for u in range(2):
                        n = 2 * l + u + 1
                        act.wait_ge(clip_ready, j * 6 + n)
                        nc.scalar.activation(a2[:, u, :], a2[:, u, :], ACT.Ln, scale=-1.0).then_inc(ln_ready, 1)
                        nc.scalar.activation(decay[:, u, :], run[:, u, :], ACT.Exp)
                    for u in range(2):
                        n = 2 * l + u + 1
                        act.wait_ge(t_ready, j * 6 + n)
                        nc.scalar.activation(grow[:, u, :], grow[:, u, :], ACT.Exp).then_inc(e_ready, 1)
                    for u in range(2):
                        n = 2 * l + u + 1
                        act.wait_ge(y_ps, j * 6 + n)
                        mean_square(j, n, u, bank_y[u][:])
                    for u in range(2):
                        root(j, 2 * l + u + 1, u)
                for u in range(2):
                    act.wait_ge(hT_ready, j * 8 + (6 + u + 1))
                    mean_square(j, 6 + u + 1, u, hT[:, u, :])
                for u in range(2):
                    root(j, 6 + u + 1, u)

        @block.gpsimd
        def _(pool):
            nc.gpsimd.memset(fresh[:], 1.0).then_inc(pool_steps, 1)
            nc.gpsimd.memset(rms_eps[:], RMS_EPS).then_inc(pool_steps, 1)
            pool.wait_ge(pool_steps, 2)
            nc.gpsimd.memset(batches(fresh[:])[:, :, 0], 0.0).then_inc(const, 1)
            with pool.Fori(0, STEPS) as j:
                for l in range(LAYERS):
                    for u in range(2):
                        n = 2 * l + u + 1
                        pool.wait_ge(gates_sb, j * 6 + n)
                        nc.gpsimd.tensor_tensor(g[:, u, :], g[:, u, :], xc[:, u, :], ALU.mult).then_inc(ix_ready, 1)
                norm_rstd(chip, pool, j, mv_ready, Steps(pool, pool_steps, j, 1, 2), rstd_ready)

        @block.vector
        def _(dve):
            dve.wait_ge(const, 1)
            dve.wait_ge(rate_l, 1)
            nc.vector.tensor_scalar(rate8[:], rate[:], -8.0, None, ALU.mult)
            nc.vector.tensor_scalar(rate16[:], rate[:], -16.0, None, ALU.mult).then_inc(rate_done, 1)
            dve.wait_ge(rate_done, 1)
            with dve.Fori(0, STEPS) as j:
                steps = Steps(dve, dve_steps, j, 35)
                for l in range(LAYERS):
                    tap = lambda k: chip.weight("cw")[:, l * TAPS + k:l * TAPS + k + 1]
                    for u in range(2):
                        dve.wait_ge(hT_ready, j * 8 + (2 * l + u + 1))
                        last = nc.vector.tensor_scalar(xc[:, u, :], hT[:, u, :], tap(TAPS - 1),
                                                       chip.weight("cb")[:, l:l + 1], ALU.mult, ALU.add)
                    steps.done(last)
                    for back in range(1, TAPS):
                        for u in range(2):
                            last = nc.vector.scalar_tensor_tensor(
                                batches(xc[:, u, :])[:, :, back:], batches(hT[:, u, :])[:, :, :S - back],
                                tap(TAPS - 1 - back), batches(xc[:, u, :])[:, :, back:], ALU.mult, ALU.add)
                            if back == TAPS - 1:
                                last.then_inc(xc_ready, 1)
                        if back < TAPS - 1:
                            steps.done(last)
                    for u in range(2):
                        n = 2 * l + u + 1
                        dve.wait_ge(a2_ready, j * 6 + n)
                        nc.vector.tensor_scalar(a2[:, u, :], a2[:, u, :], 1.0, -1e-6, ALU.subtract, ALU.min)
                        steps.done(nc.vector.tensor_scalar(r[:, u, :], r[:, u, :], rate8[:, l:l + 1], LOG_A_MIN,
                                                           ALU.mult, ALU.max))
                        steps.done(nc.vector.tensor_tensor_scan(run[:, u, :], fresh[:], r[:, u, :], 0.0, ALU.mult, ALU.add))
                        nc.vector.tensor_scalar(run[:, u, :], run[:, u, :], LOG_SUM_MIN, None, ALU.max).then_inc(clip_ready, 1)
                    for u in range(2):
                        n = 2 * l + u + 1
                        dve.wait_ge(ln_ready, j * 6 + n)
                        nc.vector.scalar_tensor_tensor(grow[:, u, :], a2[:, u, :], 0.5, run[:, u, :],
                                                       ALU.mult, ALU.subtract).then_inc(t_ready, 1)
                    for u in range(2):
                        n = 2 * l + u + 1
                        dve.wait_ge(e_ready, j * 6 + n)
                        dve.wait_ge(ix_ready, j * 6 + n)
                        steps.done(nc.vector.tensor_tensor(grow[:, u, :], grow[:, u, :], g[:, u, :], ALU.mult))
                        steps.done(nc.vector.tensor_tensor_scan(acc[:, u, :], fresh[:], grow[:, u, :], 0.0, ALU.mult, ALU.add))
                        nc.vector.tensor_tensor(acc[:, u, :], acc[:, u, :], decay[:, u, :], ALU.mult).then_inc(h_ready, 1)
                    for u in range(2):
                        dve.wait_ge(rs_ready, j * 8 + (2 * l + u + 1))
                        nc.vector.scalar_tensor_tensor(hT[:, u, :], bank_y[u][:], chip.weight("norm_w")[:, l:l + 1],
                                                       rs[:, u, :], ALU.mult, ALU.mult).then_inc(hT_ready, 1)
                jn = (j + 1) % STEPS
                norm_stats(chip, steps, jn, mv_ready)
                for u in range(2):
                    dve.wait_ge(rs_ready, j * 8 + (6 + u + 1))
                    nc.vector.scalar_tensor_tensor(xc[:, u, :], hT[:, u, :], chip.weight("norm_out"),
                                                   rs[:, u, :], ALU.mult, ALU.mult).then_inc(z_ready, 1)
                norm_rows(chip, dve, jn, j, rstd_ready, xn_ready)
                for u in range(2):
                    dve.wait_ge(zT_ps, j * 2 + u + 1)
                    rows = chip.x[:, ds(j * TPI + 4 * u, 4), :]
                    last = nc.vector.tensor_tensor(rows, bank_r[u][:].rearrange("p (t d) -> p t d", d=D), rows, ALU.add)
                steps.done(last)
                steps.close()


def stage_experts0(chip):
    nc = chip.nc
    SLOTS = E0 * CAP
    COLS = BPI * CAP
    M = I0 // P
    TE = TPI * E0
    with ExitStack() as ctx:
        def sb(name, shape, dt=F32):
            return ctx.enter_context(nc.sbuf_tensor("c0_" + name, shape, dt))

        def bank(name, shape):
            return ctx.enter_context(nc.psum_tensor("c0_" + name, shape, F32))

        sem = semaphores(nc, ctx, "c0_")

        xT = sb("xT", [P, N])
        top = sb("top", [P, TPI])
        shifted = sb("shifted", [P, TPI, E0])
        raised = sb("raised", [P, TPI, E0])
        total = sb("total", [P, TPI])
        share = sb("share", [P, TPI])
        aff_w = sb("aff", [P, P])
        aff = aff_w[:, 0:TE].rearrange("p (t e) -> p t e", e=E0)
        affT = sb("affT", [TE, P])
        best = sb("best", [TE, 2, 2, 8])
        left1 = sb("left1", [TE, P])
        left2 = sb("left2", [TE, P])
        chosen = sb("chosen", [TE, P])
        count = sb("count", [TE, P])
        key_w = sb("key", [P, P])
        key = key_w[0:TE, :]
        keyT = sb("keyT", [P, TE])
        fresh = sb("fresh", [TE, P])
        slot_i = sb("slot_i", [P, CAP], mybir.dt.int32)
        slot = sb("slot", [P, CAP])
        sel = sb("sel", [P, TE, CAP])
        selg = sb("selg", [P, TE, CAP])
        selT = sb("selT", [P, N])
        xe = sb("xe", [P, E0, BPI, CAP])
        silu = sb("silu", [P, 2, 2 * COLS])
        h = sb("h", [P, 2, 2 * COLS])
        yT = sb("yT", [P, BPI, E0, CAP])
        y = sb("y", [P, BPI, D])
        bank_x = [bank(f"x{u}", [P, HALF]) for u in range(2)]
        bank_g = [bank(f"g{u}", [P, HALF]) for u in range(2)]
        bank_u = [bank(f"u{u}", [P, HALF]) for u in range(2)]
        bank_y = [bank(f"y{u}", [P, HALF]) for u in range(2)]
        spread = [bank_g[0], bank_u[0], bank_g[1], bank_u[1]]
        const, made = sem("const"), sem("made")
        xT_ps, xT_sb, logits, shifted_ready, raised_ready, aff_ready = (
            sem(n) for n in ("xT_ps", "xT_sb", "logits", "shifted_s", "raised_s", "aff_s"))
        affT_ps, key_ready, keyT_ps, sel_ready, selg_ready = (sem(n) for n in ("affT_ps", "key_s", "keyT_ps", "sel_s", "selg_s"))
        xe_ps, xe_sb, gu_ps, silu_ready, h_ready, yT_ps, yT_sb = (
            sem(n) for n in ("xe_ps", "xe_sb", "gu_ps", "silu_s", "h_s", "yT_ps", "yT_sb"))
        selT_ps, selT_sb, y_ps, y_sb, out_ps, x_done = (sem(n) for n in ("selT_ps", "selT_sb", "y_ps", "y_sb", "out_ps", "x_done"))
        mv_ready, rstd_ready, xn_ready = sem("mv"), sem("rstd"), sem("xn")
        dve_steps, pool_steps = sem("dve"), sem("pool")
        block = ctx.enter_context(nc.Block())
        parts = [(e, m) for e in range(E0) for m in range(M // 2)]

        @block.tensor
        def _(pe):
            pe.wait_ge(chip.ffn0_in, 16 * 3)
            with pe.Fori(0, STEPS) as j:
                for u in range(2):
                    for t in range(4):
                        last = nc.tensor.transpose(bank_x[u][:, t * P:(t + 1) * P], chip.xn[:, 4 * u + t, :], chip.ident[:])
                    last.then_inc(xT_ps, 1)
                pe.wait_ge(xT_sb, j * 2 + 2)
                for t in range(TPI):
                    last = nc.tensor.matmul(bank_x[0][:, t * E0:(t + 1) * E0], xT[:, t * P:(t + 1) * P],
                                            chip.weight("router0"), start=True, stop=True)
                last.then_inc(logits, 1)
                pe.wait_ge(aff_ready, j + 1)
                nc.tensor.transpose(bank_x[1][:, 0:P], aff_w[:], chip.ident[:]).then_inc(affT_ps, 1)
                pe.wait_ge(key_ready, j + 1)
                nc.tensor.transpose(bank_x[0][:, 0:P], key_w[:], chip.ident[:]).then_inc(keyT_ps, 1)
                pe.wait_ge(sel_ready, j + 1)
                for q in range(4):
                    for n in range(4):
                        t, half = 4 * (q // 2) + n, slice(64 * (q % 2), 64 * (q % 2) + 64)
                        last = nc.tensor.matmul(spread[q][:, n * SLOTS:(n + 1) * SLOTS], chip.xn[half, t, :],
                                                sel[half, t * E0:(t + 1) * E0, :].rearrange("p e c -> p (e c)"),
                                                start=True, stop=True)
                    last.then_inc(xe_ps, 1)
                pe.wait_ge(selg_ready, j + 1)
                for u in range(2):
                    for t in range(4):
                        n = 4 * u + t
                        last = nc.tensor.transpose(bank_x[u][:, t * P:(t + 1) * P],
                                                   selg[:, n * E0:(n + 1) * E0, :].rearrange("p e c -> p (e c)"), chip.ident[:])
                    last.then_inc(selT_ps, 1)

                def answer(i):
                    e, m = parts[i]
                    pe.wait_ge(h_ready, j * len(parts) + i + 1)
                    if m == 0 and e >= 2:
                        pe.wait_ge(yT_sb, j * E0 + (e - 1))
                    for c in range(2):
                        n = 2 * m + c
                        last = nc.tensor.matmul(bank_y[e % 2][:, 0:COLS], chip.down0[:, e * M + n, :],
                                                h[:, i % 2, c * COLS:(c + 1) * COLS], start=(n == 0), stop=(n == M - 1))
                    if m == M // 2 - 1:
                        last.then_inc(yT_ps, 1)

                for i, (e, m) in enumerate(parts):
                    pe.wait_ge(xe_sb, j * 4 + 4)
                    if i >= 2:
                        pe.wait_ge(h_ready, j * len(parts) + i - 1)
                    tokens = xe[:, e, :, :].rearrange("p b c -> p (b c)")
                    for w, dst in ((chip.gate0, bank_g[i % 2]), (chip.up0, bank_u[i % 2])):
                        for c in range(2):
                            n = 2 * m + c
                            last = nc.tensor.matmul(dst[:, c * COLS:(c + 1) * COLS], w[:, e, n * P:(n + 1) * P], tokens,
                                                    start=True, stop=True)
                    last.then_inc(gu_ps, 1)
                    if i:
                        answer(i - 1)
                answer(len(parts) - 1)
                pe.wait_ge(yT_sb, j * E0 + E0)
                for q in range(4):
                    for n in range(4):
                        b = 4 * q + n
                        last = nc.tensor.transpose(spread[q][:, n * D:(n + 1) * D],
                                                   yT[:, b, :, :].rearrange("p e c -> p (e c)"), chip.ident[:])
                    last.then_inc(y_ps, 1)
                pe.wait_ge(selT_sb, j * 2 + 2)
                for u in range(2):
                    pe.wait_ge(y_sb, j * 4 + 2 * u + 2)
                    for t in range(4):
                        for g in range(2):
                            b = 2 * (4 * u + t) + g
                            last = nc.tensor.matmul(bank_y[u][64 * g:64 * g + 64, t * D:(t + 1) * D],
                                                    selT[:, b * S:(b + 1) * S], y[:, b, :], start=True, stop=True)
                    last.then_inc(out_ps, 1)
                pe.wait_ge(xn_ready, j + 1)

        @block.scalar
        def _(act):
            with act.Fori(0, STEPS) as j:
                for u in range(2):
                    act.wait_ge(xT_ps, j * 2 + u + 1)
                    nc.scalar.activation(xT[:, u * HALF:(u + 1) * HALF], bank_x[u][:], ACT.Identity).then_inc(xT_sb, 1)
                act.wait_ge(shifted_ready, j + 1)
                nc.scalar.activation(raised[:], shifted[:], ACT.Exp).then_inc(raised_ready, 1)
                for q in range(4):
                    act.wait_ge(xe_ps, j * 4 + q + 1)
                    to = xe[:].rearrange("p e (t g) c -> p e t g c", g=2)[:, :, 4 * (q // 2):4 * (q // 2) + 4, q % 2, :]
                    nc.scalar.activation(to.rearrange("p e t c -> p t e c"),
                                         spread[q][:].rearrange("p (t e c) -> p t e c", t=4, e=E0),
                                         ACT.Identity).then_inc(xe_sb, 1)
                for u in range(2):
                    act.wait_ge(selT_ps, j * 2 + u + 1)
                    nc.scalar.activation(selT[:, u * HALF:(u + 1) * HALF], bank_x[u][:], ACT.Identity).then_inc(selT_sb, 1)
                def copy_answers(e):
                    act.wait_ge(yT_ps, j * E0 + e + 1)
                    nc.scalar.activation(yT[:, :, e, :], bank_y[e % 2][:, 0:COLS].rearrange("p (b c) -> p b c", c=CAP),
                                         ACT.Identity).then_inc(yT_sb, 1)

                for i, (e, m) in enumerate(parts):
                    act.wait_ge(gu_ps, j * len(parts) + i + 1)
                    nc.scalar.activation(silu[:, i % 2, :], bank_g[i % 2][:], ACT.Silu).then_inc(silu_ready, 1)
                    if m == 1 and e:
                        copy_answers(e - 1)
                copy_answers(E0 - 1)
                for q in range(0, 4, 2):
                    act.wait_ge(y_ps, j * 4 + q + 1)
                    nc.scalar.activation(y[:, 4 * q:4 * q + 4, :].rearrange("p b d -> p (b d)"), spread[q][:],
                                         ACT.Identity).then_inc(y_sb, 1)
                    act.wait_ge(y_ps, j * 4 + q + 2)
                    nc.scalar.activation(y[:, 4 * q + 4:4 * q + 8, :].rearrange("p b d -> p (b d)"), spread[q + 1][:],
                                         ACT.Identity).then_inc(y_sb, 1)

        @block.gpsimd
        def _(pool):
            nc.gpsimd.iota(slot_i[:], [[1, CAP]], base=1, channel_multiplier=0).then_inc(made, 1)
            nc.gpsimd.memset(fresh[:], 1.0).then_inc(made, 1)
            nc.gpsimd.memset(aff_w[:], 0.0).then_inc(const, 1)
            nc.gpsimd.memset(key_w[:], 0.0).then_inc(const, 1)
            pool.wait_ge(made, 2)
            nc.gpsimd.tensor_copy(slot[:], slot_i[:]).then_inc(const, 1)
            nc.gpsimd.memset(fresh[:].rearrange("p (b s) -> p b s", s=S)[:, :, 0], 0.0).then_inc(const, 1)
            with pool.Fori(0, STEPS) as j:
                pool.wait_ge(sel_ready, j + 1)
                nc.gpsimd.tensor_tensor(selg[:], sel[:],
                                        aff_w[:, 0:TE].unsqueeze(2).broadcast_to([P, TE, CAP]),
                                        ALU.mult).then_inc(selg_ready, 1)
                norm_rstd(chip, pool, j, mv_ready, Steps(pool, pool_steps, j, 1), rstd_ready)

        @block.vector
        def _(dve):
            dve.wait_ge(const, 4)
            with dve.Fori(0, STEPS) as j:
                steps = Steps(dve, dve_steps, j, 12)
                scores = bank_x[0][:, 0:TE].rearrange("p (t e) -> p t e", e=E0)
                along = lambda ap: ap.unsqueeze(2).broadcast_to([P, TPI, E0])
                dve.wait_ge(logits, j + 1)
                steps.done(nc.vector.tensor_reduce(top[:], scores, AX_X, ALU.max))
                nc.vector.tensor_tensor(shifted[:], scores, along(top[:]), ALU.subtract).then_inc(shifted_ready, 1)
                dve.wait_ge(raised_ready, j + 1)
                steps.done(nc.vector.tensor_reduce(total[:], raised[:], AX_X, ALU.add))
                steps.done(nc.vector.reciprocal(share[:], total[:]))
                nc.vector.tensor_tensor(aff, raised[:], along(share[:]), ALU.mult).then_inc(aff_ready, 1)
                dve.wait_ge(affT_ps, j + 1)
                steps.done(nc.vector.tensor_copy(affT[:], bank_x[1][0:TE, 0:P]))
                src = affT
                for rnd, left in enumerate((left1, left2)):
                    nc.vector.tensor_copy(chip.spare[:], chip.stats[:, 0, 0:1])
                    for g in range(2):
                        last = nc.vector.max(best[:, rnd, g, :], src[:, g * S:(g + 1) * S])
                    steps.done(last)
                    nc.vector.tensor_copy(chip.spare[:], chip.stats[:, 0, 0:1])
                    for g in range(2):
                        last = nc.vector.match_replace(left[:, g * S:(g + 1) * S], best[:, rnd, g, :],
                                                       src[:, g * S:(g + 1) * S], -1.0)
                    steps.done(last)
                    src = left
                steps.done(nc.vector.tensor_scalar(chosen[:], left2[:], 0.0, None, ALU.is_lt))
                steps.done(nc.vector.tensor_tensor_scan(count[:], fresh[:], chosen[:], 0.0, ALU.mult, ALU.add))
                nc.vector.tensor_tensor(key, count[:], chosen[:], ALU.mult).then_inc(key_ready, 1)
                dve.wait_ge(keyT_ps, j + 1)
                steps.done(nc.vector.tensor_copy(keyT[:], bank_x[0][:, 0:TE]))
                if_free = nc.vector.tensor_tensor(sel[:], keyT[:].unsqueeze(2).broadcast_to([P, TE, CAP]),
                                                  slot[:].unsqueeze(1).broadcast_to([P, TE, CAP]), ALU.is_equal)
                if_free.then_inc(sel_ready, 1)
                jn = (j + 1) % STEPS
                norm_stats(chip, steps, jn, mv_ready)
                for i in range(len(parts)):
                    dve.wait_ge(silu_ready, j * len(parts) + i + 1)
                    nc.vector.tensor_tensor(h[:, i % 2, :], silu[:, i % 2, :], bank_u[i % 2][:], ALU.mult).then_inc(h_ready, 1)
                for u in range(2):
                    dve.wait_ge(out_ps, j * 2 + u + 1)
                    rows = chip.x[:, ds(j * TPI + 4 * u, 4), :]
                    nc.vector.tensor_tensor(rows, bank_y[u][:].rearrange("p (t d) -> p t d", d=D), rows,
                                            ALU.add).then_inc(x_done, 1)
                dve.wait_ge(x_done, j * 2 + 2)
                norm_rows(chip, dve, jn, j, rstd_ready, xn_ready)
                steps.close()


def stage_heads(chip, ctxT_dram, mask_dram, fetch):
    nc = chip.nc
    PAIRS, UP = HEADS // 2, 4
    UNITS = BPI * PAIRS // UP
    VW = HD + 1
    SCALE = float(1.0 / np.sqrt(D))
    with ExitStack() as ctx:
        def sb(name, shape, dt=F32):
            return ctx.enter_context(nc.sbuf_tensor("d_" + name, shape, dt))

        sem = semaphores(nc, ctx, "d_")

        ctx_t = sb("ctx_t", [P, BPI * KV])
        mask_i = sb("mask_i", [P, KV], mybir.dt.int32)
        mask_add = sb("mask_add", [P, UP, KV], BF16)
        ident_b = sb("ident_b", [P, P], BF16)
        own = sb("own", [P, HEADS])
        xT = sb("xT", [P, N])
        qT = sb("qT", [P, N])
        qd = sb("qd", [P, BPI, HEADS, S])
        kT = sb("kT", [P, BPI * KV])
        v = sb("v", [P, BPI, HEADS, VW])
        top = sb("top", [P, UNITS, UP])
        negtop = sb("negtop", [P, UNITS, UP])
        prob = sb("prob", [P, 3, UP, KV])
        probT = sb("probT", [P, 2, UP * P])
        share = sb("share", [P, 2, 2, PAIRS])
        z = sb("z", [P, TPI, PAIRS, 2, HD])
        zT = sb("zT", [P, N])
        bk = [ctx.enter_context(nc.psum_tensor(f"d_bk{i}", [P, HALF], F32)) for i in range(8)]
        bank_t, bank_o, bank_e = bk[0:2], bk[2:4], bk[4:7]
        const, const2, mask_in, mask_ready = sem("const"), sem("const2"), sem("mask_in"), sem("mask")
        ctx_in, xT_ps, xT_sb, k_ps, k_sb, q_ps, q_sb, v_ps, v_sb = (
            sem(n) for n in ("ctx_in", "xT_ps", "xT_sb", "k_ps", "k_sb", "q_ps", "q_sb", "v_ps", "v_sb"))
        qd_pool, qd_dve, energy, negtop_ready, prob_ready, probT_ps, probT_sb, o_ps = (
            sem(n) for n in ("qd_pool", "qd_dve", "energy", "negtop_s", "prob_s", "probT_ps", "probT_sb", "o_ps"))
        z_ready, zT_ps, zT_sb, out_ps, x_done = (sem(n) for n in ("z_s", "zT_ps", "zT_sb", "out_ps", "x_done"))
        mv_ready, rstd_ready, xn_ready = sem("mv"), sem("rstd"), sem("xn")
        dve_steps, pool_steps = sem("dve"), sem("pool")
        block = ctx.enter_context(nc.Block())

        @block.sync
        def _(sp):
            for g in range(2):
                sp.dma_start(mask_i[64 * g:64 * g + 64, :], mask_dram).then_inc(mask_in, 16)
            sp.dma_start(ctx_t[:], ctxT_dram[:, 0:BPI * KV]).then_inc(ctx_in, 16)
            with sp.Fori(1, STEPS) as j:
                sp.wait_ge(v_ps, j * 4)
                sp.dma_start(ctx_t[:], ctxT_dram[:, ds(j * (BPI * KV), BPI * KV)]).then_inc(ctx_in, 16)
            fetch(sp)

        @block.tensor
        def _(pe):
            pe.wait_ge(const, 1)
            pe.wait_ge(mask_ready, 2)
            with pe.Fori(0, STEPS) as j:
                for u in range(2):
                    for t in range(4):
                        last = nc.tensor.transpose(bk[u][:, t * P:(t + 1) * P], chip.xn[:, 4 * u + t, :], chip.ident[:])
                    last.then_inc(xT_ps, 1)
                pe.wait_ge(ctx_in, j * 16 + 16)
                for c in range(4):
                    nc.tensor.matmul(bk[2 + c][:], chip.weight("k_bd"), ctx_t[:, c * HALF:(c + 1) * HALF],
                                     start=True, stop=True).then_inc(k_ps, 1)
                for u in range(2):
                    pe.wait_ge(xT_sb, j * 2 + u + 1)
                    nc.tensor.matmul(bk[6 + u][:], chip.weight("q_bd"), xT[:, u * HALF:(u + 1) * HALF],
                                     start=True, stop=True).then_inc(q_ps, 1)
                for c in range(4):
                    if c >= 2:
                        pe.wait_ge(k_sb, j * 4 + (c - 1))
                    for n in range(4):
                        b = 4 * c + n
                        last = nc.tensor.matmul(bk[c][:, n * D:(n + 1) * D], ctx_t[:, b * KV:(b + 1) * KV],
                                                chip.weight("v_bd"), start=True, stop=True)
                    last.then_inc(v_ps, 1)
                pe.wait_ge(k_sb, j * 4 + 4)
                pe.wait_ge(v_sb, j * 4 + 4)
                pe.wait_ge(q_sb, j * 2 + 2)
                for s in range(UNITS + 3):
                    if s < UNITS:
                        b, g = s // 2, s % 2
                        if s % (UNITS // 2) == 0:
                            pe.wait_ge(qd_pool, j * 2 + (s // (UNITS // 2) + 1))
                            pe.wait_ge(qd_dve, j * 2 + (s // (UNITS // 2) + 1))
                        nc.tensor.matmul(bank_e[s % 3][:], ident_b[:], mask_add[:].rearrange("p i k -> p (i k)"),
                                         start=True, stop=False, skip_group_check=True)
                        for i in range(UP):
                            h = 2 * (UP * g + i)
                            last = nc.tensor.matmul(bank_e[s % 3][:, i * KV:(i + 1) * KV],
                                                    qd[:, b, h:h + 2, :].rearrange("p h q -> p (h q)"),
                                                    kT[:, b * KV:(b + 1) * KV], start=False, stop=(i == UP - 1),
                                                    skip_group_check=True)
                        last.then_inc(energy, 1)
                    if 2 <= s < UNITS + 2:
                        s1 = s - 2
                        pe.wait_ge(prob_ready, j * UNITS + s1 + 1)
                        for i in range(UP):
                            last = nc.tensor.transpose(bank_t[s1 % 2][:, i * P:(i + 1) * P], prob[:, s1 % 3, i, :], chip.ident[:])
                        last.then_inc(probT_ps, 1)
                    if s >= 3:
                        s2 = s - 3
                        b, g = s2 // 2, s2 % 2
                        pe.wait_ge(probT_sb, j * UNITS + s2 + 1)
                        if s2 % 4 == 0 and s2 >= 8:
                            pe.wait_ge(z_ready, j * TPI + (s2 // 4 - 1))
                        for i in range(UP):
                            at = (b % 2) * PAIRS * 2 * VW + (UP * g + i) * 2 * VW
                            h = 2 * (UP * g + i)
                            last = nc.tensor.matmul(bank_o[(b // 2) % 2][:, at:at + 2 * VW], probT[:, s2 % 2, i * P:(i + 1) * P],
                                                    v[:, b, h:h + 2, :].rearrange("p h f -> p (h f)"), start=True, stop=True)
                        if s2 % 4 == 3:
                            last.then_inc(o_ps, 1)
                for u in range(2):
                    pe.wait_ge(z_ready, j * TPI + 4 * u + 4)
                    for t in range(4):
                        last = nc.tensor.transpose(bk[4 + u][:, t * P:(t + 1) * P],
                                                   z[:, 4 * u + t, :, :, :].rearrange("p a h f -> p (a h f)"), chip.ident[:])
                    last.then_inc(zT_ps, 1)
                for u in range(2):
                    pe.wait_ge(zT_sb, j * 2 + u + 1)
                    for t in range(4):
                        n = 4 * u + t
                        last = nc.tensor.matmul(bk[6 + u][:, t * D:(t + 1) * D], zT[:, n * P:(n + 1) * P],
                                                chip.weight("fc"), start=True, stop=True)
                    last.then_inc(out_ps, 1)
                pe.wait_ge(xn_ready, j + 1)

        @block.scalar
        def _(act):
            with act.Fori(0, STEPS) as j:
                for u in range(2):
                    act.wait_ge(xT_ps, j * 2 + u + 1)
                    nc.scalar.activation(xT[:, u * HALF:(u + 1) * HALF], bk[u][:], ACT.Identity).then_inc(xT_sb, 1)
                for c in range(2):
                    act.wait_ge(k_ps, j * 4 + c + 1)
                    nc.scalar.activation(kT[:, c * HALF:(c + 1) * HALF], bk[2 + c][:], ACT.Identity).then_inc(k_sb, 1)
                for u in range(2):
                    act.wait_ge(q_ps, j * 2 + u + 1)
                    nc.scalar.activation(qT[:, u * HALF:(u + 1) * HALF], bk[6 + u][:], ACT.Identity, scale=SCALE).then_inc(q_sb, 1)
                for c in range(2, 4):
                    act.wait_ge(k_ps, j * 4 + c + 1)
                    nc.scalar.activation(kT[:, c * HALF:(c + 1) * HALF], bk[2 + c][:], ACT.Identity).then_inc(k_sb, 1)
                for s in range(UNITS):
                    act.wait_ge(negtop_ready, j * UNITS + s + 1)
                    for i in range(UP):
                        last = nc.scalar.activation(prob[:, s % 3, i, :], bank_e[s % 3][:, i * KV:(i + 1) * KV], ACT.Exp,
                                                    bias=negtop[:, s, i:i + 1])
                    last.then_inc(prob_ready, 1)
                for u in range(2):
                    act.wait_ge(zT_ps, j * 2 + u + 1)
                    nc.scalar.activation(zT[:, u * HALF:(u + 1) * HALF], bk[4 + u][:], ACT.Identity).then_inc(zT_sb, 1)

        def spread_heads(engine, quarters, u, done):
            for n, c in enumerate(quarters):
                rows, heads = slice(32 * c, 32 * c + 32), slice(4 * c, 4 * c + 4)
                for i in range(4):
                    h = 4 * c + i
                    to = qd[rows, 8 * u:8 * u + 8, h, :]
                    of = qT[rows, u * HALF:(u + 1) * HALF].rearrange("p (b q) -> p b q", q=S)
                    if engine is nc.gpsimd:
                        last = engine.tensor_tensor(to, of, own[rows, h:h + 1].unsqueeze(2).broadcast_to([32, 8, S]), ALU.mult)
                    else:
                        last = engine.tensor_scalar(to, of, own[rows, h:h + 1], None, ALU.mult)
            last.then_inc(done, 1)

        @block.gpsimd
        def _(pool):
            nc.gpsimd.memset(own[:], 1.0).then_inc(const2, 1)
            nc.gpsimd.memset(qd[:, 0:8, :, :], 0.0).then_inc(const2, 1)
            nc.gpsimd.memset(v[:], 1.0).then_inc(const2, 1)
            pool.wait_ge(const2, 3)
            nc.gpsimd.affine_select(out=own[:], in_=own[:], compare_op=ALU.is_ge, fill=0.0, base=0,
                                    pattern=[[-HD, HEADS]], channel_multiplier=1).then_inc(const2, 1)
            pool.wait_ge(const2, 4)
            nc.gpsimd.affine_select(out=own[:], in_=own[:], compare_op=ALU.is_ge, fill=0.0, base=HD - 1,
                                    pattern=[[HD, HEADS]], channel_multiplier=-1).then_inc(const2, 1)
            pool.wait_ge(const2, 5)
            nc.gpsimd.tensor_copy(ident_b[:], chip.ident[:]).then_inc(const, 1)
            pool.wait_ge(mask_ready, 1)
            with pool.Fori(0, STEPS) as j:
                for u in range(2):
                    pool.wait_ge(q_sb, j * 2 + u + 1)
                    spread_heads(nc.gpsimd, (0,), u, qd_pool)
                norm_rstd(chip, pool, j, mv_ready, Steps(pool, pool_steps, j, 1), rstd_ready)

        @block.vector
        def _(dve):
            nc.vector.memset(qd[:, 8:16, :, :], 0.0)
            dve.wait_ge(mask_in, 32)
            nc.vector.tensor_scalar(mask_add[:, 0, :], mask_i[:], 0.0, -1e20 * SCALE, ALU.is_equal, ALU.mult).then_inc(mask_ready, 1)
            dve.wait_ge(mask_ready, 1)
            nc.vector.tensor_copy(mask_add[:, 1:UP, :], mask_add[:, 0, :].unsqueeze(1).broadcast_to([P, UP - 1, KV])).then_inc(mask_ready, 1)
            dve.wait_ge(const, 1)
            with dve.Fori(0, STEPS) as j:
                steps = Steps(dve, dve_steps, j, UNITS + TPI + 1)
                for u in range(2):
                    dve.wait_ge(q_sb, j * 2 + u + 1)
                    spread_heads(nc.vector, (1, 2, 3), u, qd_dve)
                for c in range(4):
                    dve.wait_ge(v_ps, j * 4 + c + 1)
                    nc.vector.tensor_copy(v[:, 4 * c:4 * c + 4, :, 0:HD].rearrange("p b h f -> p (b h) f"),
                                          bk[c][:].rearrange("p (a f) -> p a f", f=HD)).then_inc(v_sb, 1)
                jn = (j + 1) % STEPS
                norm_stats(chip, steps, jn, mv_ready)
                for s in range(UNITS + 4):
                    if s < UNITS:
                        dve.wait_ge(energy, j * UNITS + s + 1)
                        steps.done(nc.vector.tensor_reduce(top[:, s, :], bank_e[s % 3][:].rearrange("p (i k) -> p i k", k=KV),
                                                           AX_X, ALU.max))
                        nc.vector.tensor_scalar(negtop[:, s, :], top[:, s, :], -1.0, None, ALU.mult).then_inc(negtop_ready, 1)
                    if 2 <= s < UNITS + 2:
                        s1 = s - 2
                        dve.wait_ge(probT_ps, j * UNITS + s1 + 1)
                        nc.vector.tensor_copy(probT[:, s1 % 2, :], bank_t[s1 % 2][:]).then_inc(probT_sb, 1)
                    if s >= 4 and s % 4 == 3:
                        t = s // 4 - 1
                        dve.wait_ge(o_ps, j * TPI + t + 1)
                        o = bank_o[t % 2][:, 0:2 * PAIRS * 2 * VW].rearrange("p (b a v) -> p b a v", b=2, a=PAIRS)
                        for h in range(2):
                            rows = slice(64 * h, 64 * h + 64)
                            last = nc.vector.reciprocal(share[rows, t % 2, :, :], o[rows, :, :, h * VW + HD])
                        steps.done(last)
                        for h in range(2):
                            rows = slice(64 * h, 64 * h + 64)
                            for g in range(2):
                                last = nc.vector.tensor_tensor(
                                    z[64 * g:64 * g + 64, t, :, h, :], o[rows, g, :, h * VW:h * VW + HD],
                                    share[rows, t % 2, g, :].unsqueeze(2).broadcast_to([64, PAIRS, HD]), ALU.mult)
                        last.then_inc(z_ready, 1)
                for u in range(2):
                    dve.wait_ge(out_ps, j * 2 + u + 1)
                    rows = chip.x[:, ds(j * TPI + 4 * u, 4), :]
                    nc.vector.tensor_tensor(rows, bk[6 + u][:].rearrange("p (t d) -> p t d", d=D), rows,
                                            ALU.add).then_inc(x_done, 1)
                dve.wait_ge(x_done, j * 2 + 2)
                norm_rows(chip, dve, jn, j, rstd_ready, xn_ready)
                steps.close()


def stage_ssm(chip, b_out_dram):
    nc = chip.nc
    C = CH // P
    with ExitStack() as ctx:
        def sb(name, shape, dt=F32):
            return ctx.enter_context(nc.sbuf_tensor("e_" + name, shape, dt))

        sem = semaphores(nc, ctx, "e_")

        xi = sb("xi", [P, TPI, D])
        stats = sb("stats", [P, TPI, 6])
        mv = sb("mv", [P, TPI, 2])
        ve = sb("ve", [P, TPI])
        rstd = sb("rstd", [P, TPI])
        xT = sb("xT", [P, 2, HALF])
        xp = sb("xp", [P, 2, C, HALF])
        xc = sb("xc", [P, 2, C, HALF])
        gate = sb("gate", [P, 2, C, HALF])
        sd = sb("sd", [P, 2, C, HALF])
        y = sb("y", [P, 2, C, HALF])
        keep = sb("keep", [P, C, HALF])
        fresh = sb("fresh", [P, HALF])
        delta = sb("delta", [P, C])
        ab = sb("ab", [P, C * SN])
        coef = sb("coef", [P, C])
        bias = sb("bias", [P, 4, D])
        bk = [[ctx.enter_context(nc.psum_tensor(f"e_bk{u}{i}", [P, HALF], F32)) for i in range(4)] for u in range(2)]
        const, delta_a, coef_a, bias_in, keep_ready = sem("const"), sem("delta_a"), sem("coef_a"), sem("bias_in"), sem("keep_s")
        xT_ps, xT_sb, xp_ps, xp_sb, gate_ps, gate_sb, xc_ready, xs_ready = (
            sem(n) for n in ("xT_ps", "xT_sb", "xp_ps", "xp_sb", "gate_ps", "gate_sb", "xc_s", "xs_s"))
        cd_ps, sd_ready, y_ready, out_ps, x_done = (sem(n) for n in ("cd_ps", "sd_s", "y_s", "out_ps", "x_done"))
        mv_ready, rstd_ready, xn_ready = sem("mv_s"), sem("rstd_s"), sem("xn_s")
        mv2_ready, rstd2_ready, xi_ready = sem("mv2"), sem("rstd2"), sem("xi_s")
        dve_steps, pool_steps, first_steps = sem("dve"), sem("pool"), sem("first")
        block = ctx.enter_context(nc.Block())
        batches = lambda ap: ap.rearrange("p (b s) -> p b s", s=S)

        def inner_stats(steps):
            for t in range(TPI):
                last = nc.vector.bn_stats(stats[:, t, :], chip.xn[:, t, :])
            steps.done(last)
            nc.vector.tensor_copy(chip.spare[:], stats[:, 0, 0:1])
            for t in range(TPI):
                last = nc.vector.bn_aggr(mv[:, t, :], stats[:, t, :])
            last.then_inc(mv2_ready, 1)

        def inner_rows():
            for t in range(TPI):
                last = nc.vector.tensor_scalar(xi[:, t, :], chip.xn[:, t, :], mv[:, t, 0:1], rstd[:, t:t + 1],
                                               ALU.subtract, ALU.mult)
            last.then_inc(xi_ready, 1)

        def inner_rstd(pool, steps):
            steps.done(nc.gpsimd.tensor_tensor(ve[:], mv[:, :, 1], chip.eps[:], ALU.add))
            nc.gpsimd.tensor_tensor(rstd[:], ve[:], chip.neghalf[:], ALU.pow).then_inc(rstd2_ready, 1)

        @block.sync
        def _(sp):
            sp.wait_ge(const, 1)
            for t in range(4):
                sp.dma_start(bias[0:1, t, :], b_out_dram).then_inc(bias_in, 16)

        @block.tensor
        def _(pe):
            pe.wait_ge(bias_in, 64)
            with pe.Fori(0, STEPS) as j:
                pe.wait_ge(xi_ready, j + 1)
                for u in range(2):
                    for t in range(4):
                        last = nc.tensor.transpose(bk[u][0][:, t * P:(t + 1) * P], xi[:, 4 * u + t, :], chip.ident[:])
                    last.then_inc(xT_ps, 1)
                for u in range(2):
                    pe.wait_ge(xT_sb, j * 2 + u + 1)
                    for c in range(2 * C):
                        nc.tensor.matmul(bk[u][(1 + c) % 4][:], chip.weight("w_inT")[:, c * P:(c + 1) * P], xT[:, u, :],
                                         start=True, stop=True).then_inc(xp_ps if c < C else gate_ps, 1)
                for u in range(2):
                    pe.wait_ge(xs_ready, j * 4 + 2 * u + 2)
                    pe.wait_ge(gate_sb, j * 4 + 2 * u + 2)
                    for n, w in enumerate(("w_cT", "w_dT")):
                        for f in range(C):
                            for k in range(C):
                                last = nc.tensor.matmul(bk[u][(1 + 2 * n + f) % 4][:],
                                                        chip.weight(w)[:, k * CH + f * P:k * CH + (f + 1) * P],
                                                        xc[:, u, k, :], start=(k == 0), stop=(k == C - 1))
                    last.then_inc(cd_ps, 1)
                for u in range(2):
                    pe.wait_ge(y_ready, j * 2 + u + 1)
                    nc.tensor.matmul(bk[u][1][:], chip.ones[:], bias[:].rearrange("p t d -> p (t d)"),
                                     start=True, stop=False, skip_group_check=True)
                    for t in range(4):
                        for c in range(C):
                            last = nc.tensor.matmul(bk[u][1][:, t * D:(t + 1) * D], y[:, u, c, t * P:(t + 1) * P],
                                                    chip.weight("w_outT")[:, c * D:(c + 1) * D], start=False,
                                                    stop=(t == 3 and c == C - 1), skip_group_check=True)
                    last.then_inc(out_ps, 1)

        @block.scalar
        def _(act):
            nc.scalar.activation(delta[:], chip.weight("log_delta"), ACT.Exp).then_inc(delta_a, 1)
            act.wait_ge(delta_a, 1)
            nc.scalar.activation(delta[:], delta[:], ACT.Ln, bias=1.0).then_inc(delta_a, 1)
            act.wait_ge(delta_a, 2)
            nc.scalar.activation(delta[:], delta[:], ACT.Exp, scale=-1.0).then_inc(delta_a, 1)
            with act.Fori(0, STEPS) as j:
                for u in range(2):
                    act.wait_ge(xT_ps, j * 2 + u + 1)
                    nc.scalar.activation(xT[:, u, :], bk[u][0][:], ACT.Identity, scale=chip.weight("in_g"),
                                         bias=chip.weight("in_b")).then_inc(xT_sb, 1)
                for u in range(2):
                    for c in range(C):
                        act.wait_ge(xp_ps, j * 4 + 2 * u + c + 1)
                        nc.scalar.activation(xp[:, u, c, :], bk[u][1 + c][:], ACT.Identity,
                                             bias=chip.weight("b_in")[:, c:c + 1]).then_inc(xp_sb, 1)
                for u in range(2):
                    for c in range(C):
                        act.wait_ge(gate_ps, j * 4 + 2 * u + c + 1)
                        nc.scalar.activation(gate[:, u, c, :], bk[u][(3 + c) % 4][:], ACT.Sigmoid,
                                             bias=chip.weight("b_in")[:, C + c:C + c + 1]).then_inc(gate_sb, 1)
                for u in range(2):
                    for c in range(C):
                        act.wait_ge(xc_ready, j * 4 + 2 * u + c + 1)
                        nc.scalar.activation(xc[:, u, c, :], xc[:, u, c, :], ACT.Silu).then_inc(xs_ready, 1)
                for u in range(2):
                    act.wait_ge(cd_ps, j * 2 + u + 1)
                    for c in range(C):
                        nc.scalar.activation(sd[:, u, c, :], bk[u][(3 + c) % 4][:], ACT.Sigmoid,
                                             bias=chip.weight("b_d")[:, c:c + 1]).then_inc(sd_ready, 1)

        @block.gpsimd
        def _(pool):
            nc.gpsimd.memset(bias[:], 0.0).then_inc(const, 1)
            nc.gpsimd.memset(fresh[:], 1.0).then_inc(pool_steps, 1)
            pool.wait_ge(pool_steps, 1)
            nc.gpsimd.memset(batches(fresh[:])[:, :, 0], 0.0).then_inc(const, 1)
            steps = Steps(pool, pool_steps, base=1)
            pool.wait_ge(mv2_ready, 1)
            inner_rstd(pool, steps)
            with pool.Fori(0, STEPS) as j:
                steps = Steps(pool, pool_steps, j, 2, base=2)
                norm_rstd(chip, pool, j, mv_ready, steps, rstd_ready)
                pool.wait_ge(mv2_ready, j + 2)
                inner_rstd(pool, steps)

        @block.vector
        def _(dve):
            steps = Steps(dve, first_steps)
            dve.wait_ge(delta_a, 3)
            dve.wait_ge(const, 2)
            for c in range(C):
                nc.vector.tensor_scalar(keep[:, c, :], fresh[:], delta[:, c:c + 1], None, ALU.mult)
            steps.done(nc.vector.tensor_tensor(ab[:], chip.weight("ssm_A"), chip.weight("ssm_B"), ALU.mult))
            nc.vector.tensor_reduce(coef[:], ab[:].rearrange("p (c n) -> p c n", n=SN), AX_X, ALU.add)
            inner_stats(steps)
            dve.wait_ge(rstd2_ready, 1)
            inner_rows()
            with dve.Fori(0, STEPS) as j:
                steps = Steps(dve, dve_steps, j, 12)
                jn = (j + 1) % STEPS
                rows = chip.x[:, ds(j * TPI, TPI), :]
                nc.vector.tensor_tensor(rows, chip.xn[:], rows, ALU.add)
                for u in range(2):
                    tap = lambda c, k: chip.weight("conv_w")[:, c * TAPS + k:c * TAPS + k + 1]
                    for c in range(C):
                        dve.wait_ge(xp_sb, j * 4 + 2 * u + c + 1)
                        last = nc.vector.tensor_scalar(xc[:, u, c, :], xp[:, u, c, :], tap(c, TAPS - 1),
                                                       chip.weight("conv_b")[:, c:c + 1], ALU.mult, ALU.add)
                    steps.done(last)
                    for back in range(1, TAPS):
                        for c in range(C):
                            last = nc.vector.scalar_tensor_tensor(
                                batches(xc[:, u, c, :])[:, :, back:], batches(xp[:, u, c, :])[:, :, :S - back],
                                tap(c, TAPS - 1 - back), batches(xc[:, u, c, :])[:, :, back:], ALU.mult, ALU.add)
                            if back == TAPS - 1:
                                last.then_inc(xc_ready, 1)
                        if back < TAPS - 1:
                            steps.done(last)
                norm_stats(chip, steps, jn, mv_ready)
                for u in range(2):
                    for c in range(C):
                        dve.wait_ge(sd_ready, j * 4 + 2 * u + c + 1)
                        last = nc.vector.scalar_tensor_tensor(sd[:, u, c, :], bk[u][1 + c][:], chip.weight("b_c")[:, c:c + 1],
                                                              sd[:, u, c, :], ALU.add, ALU.mult)
                    steps.done(last)
                    for c in range(C):
                        last = nc.vector.tensor_tensor_scan(y[:, u, c, :], keep[:, c, :], sd[:, u, c, :], 0.0, ALU.mult, ALU.add)
                    steps.done(last)
                    for c in range(C):
                        last = nc.vector.scalar_tensor_tensor(y[:, u, c, :], y[:, u, c, :], coef[:, c:c + 1], gate[:, u, c, :],
                                                              ALU.mult, ALU.mult)
                    last.then_inc(y_ready, 1)
                for u in range(2):
                    dve.wait_ge(out_ps, j * 2 + u + 1)
                    rows = chip.x[:, ds(j * TPI + 4 * u, 4), :]
                    nc.vector.tensor_tensor(rows, bk[u][1][:].rearrange("p (t d) -> p t d", d=D), rows, ALU.add).then_inc(x_done, 1)
                dve.wait_ge(x_done, j * 2 + 2)
                norm_rows(chip, dve, jn, j, rstd_ready, xn_ready)
                dve.wait_ge(xn_ready, j + 1)
                inner_stats(steps)
                dve.wait_ge(rstd2_ready, j + 2)
                inner_rows()
                steps.close()


def stage_experts1(chip, router_b_dram, b2_dram):
    nc = chip.nc
    M = I1 // P
    TE = TPI * E1
    BIG = 1e30
    with ExitStack() as ctx:
        def sb(name, shape, dt=F32):
            return ctx.enter_context(nc.sbuf_tensor("f_" + name, shape, dt))

        def bank(name, shape):
            return ctx.enter_context(nc.psum_tensor("f_" + name, shape, F32))

        sem = semaphores(nc, ctx, "f_")

        xi = sb("xi", [P, TPI, D])
        stats = sb("stats", [P, TPI, 6])
        mv = sb("mv", [P, TPI, 2])
        ve = sb("ve", [P, TPI])
        rstd = sb("rstd", [P, TPI])
        xT = sb("xT", [P, N])
        rw = sb("rw", [P, E1])
        rn_b = sb("rn_b", [P, P])
        rb_row = sb("rb_row", [P, E1])
        rb = sb("rb", [P, E1])
        b1 = sb("b1", [P, E1 * M])
        b2 = sb("b2", [P, TPI, D])
        logit = sb("logit", [P, TPI, E1])
        best = sb("best", [P, TPI, 8])
        two = sb("two", [P, TPI, 8])
        left = sb("left", [P, TPI, E1])
        diff = sb("diff", [P, TPI, E1])
        raised = sb("raised", [P, TPI, E1])
        total = sb("total", [P, TPI])
        share = sb("share", [P, TPI])
        comb_w = sb("comb", [P, P])
        comb = comb_w[:, 0:TE].rearrange("p (t e) -> p t e", e=E1)
        combT = sb("combT", [P, P])
        h = sb("h", [P, 2, M, HALF])
        bank_x = [bank(f"x{u}", [P, HALF]) for u in range(2)]
        bank_h = [bank(f"h{m}", [P, HALF]) for m in range(M)]
        bank_y = [bank(f"y{u}", [P, 4, D]) for u in range(2)]
        const, bias_in, rn_ready, bias_ps, w1_ready, two_set = (
            sem(n) for n in ("const", "bias_in", "rn_s", "bias_ps", "w1_s", "two_s"))
        xT_ps, xT_sb, logits, diff_ready, raised_ready, comb_ready, combT_ps, combT_sb, b2_ps, b2_done = (
            sem(n) for n in ("xT_ps", "xT_sb", "logits", "diff_s", "raised_s", "comb_s", "combT_ps", "combT_sb", "b2_ps", "b2_done"))
        h_ps, h_ready, y_ps, x_done = (sem(n) for n in ("h_ps", "h_s", "y_ps", "x_done"))
        mv_ready, rstd_ready, xn_ready = sem("mv_s"), sem("rstd_s"), sem("xn_s")
        mv2_ready, rstd2_ready, xi_ready = sem("mv2"), sem("rstd2"), sem("xi_s")
        dve_steps, pool_steps, first_steps = sem("dve"), sem("pool"), sem("first")
        block = ctx.enter_context(nc.Block())
        units = [(e, u) for e in range(E1) for u in range(2)]
        U = len(units)

        def inner_stats(steps):
            for t in range(TPI):
                last = nc.vector.bn_stats(stats[:, t, :], chip.xn[:, t, :])
            steps.done(last)
            nc.vector.tensor_copy(chip.spare[:], stats[:, 0, 0:1])
            for t in range(TPI):
                last = nc.vector.bn_aggr(mv[:, t, :], stats[:, t, :])
            last.then_inc(mv2_ready, 1)

        def inner_rows():
            for t in range(TPI):
                last = nc.vector.tensor_scalar(xi[:, t, :], chip.xn[:, t, :], mv[:, t, 0:1], rstd[:, t:t + 1],
                                               ALU.subtract, ALU.mult)
            last.then_inc(xi_ready, 1)

        def inner_rstd(pool, steps):
            steps.done(nc.gpsimd.tensor_tensor(ve[:], mv[:, :, 1], chip.eps[:], ALU.add))
            nc.gpsimd.tensor_tensor(rstd[:], ve[:], chip.neghalf[:], ALU.pow).then_inc(rstd2_ready, 1)

        @block.sync
        def _(sp):
            sp.wait_ge(const, 3)
            for t in range(TPI):
                sp.dma_start(b2[E1 * t:E1 * t + E1, t, :], b2_dram).then_inc(bias_in, 16)
            sp.dma_start(rb_row[0:1, :], router_b_dram).then_inc(bias_in, 16)

        @block.tensor
        def _(pe):
            pe.wait_ge(chip.ffn1_in, 32)
            for e in range(E1):
                for m in range(M):
                    nc.tensor.matmul(bank_x[0][:, e * M + m:e * M + m + 1], chip.w1[:, e, m * P:(m + 1) * P],
                                     chip.weight("ln_bT")[:, e:e + 1], start=True, stop=True)
            pe.wait_ge(rn_ready, 1)
            pe.wait_ge(bias_in, 16 * (TPI + 1))
            nc.tensor.matmul(bank_x[1][:, 0:E1], rn_b[:], chip.weight("router1"), start=True, stop=False)
            nc.tensor.matmul(bank_x[1][:, 0:E1], chip.ones[:], rb_row[:], start=False, stop=True).then_inc(bias_ps, 1)
            pe.wait_ge(w1_ready, 1)
            with pe.Fori(0, STEPS) as j:
                pe.wait_ge(xi_ready, j + 1)
                for u in range(2):
                    for t in range(4):
                        last = nc.tensor.transpose(bank_x[u][:, t * P:(t + 1) * P], xi[:, 4 * u + t, :], chip.ident[:])
                    last.then_inc(xT_ps, 1)
                pe.wait_ge(xT_sb, j * 2 + 2)
                for t in range(TPI):
                    last = nc.tensor.matmul(bank_x[0][:, t * E1:(t + 1) * E1], xT[:, t * P:(t + 1) * P], rw[:],
                                            start=True, stop=True)
                last.then_inc(logits, 1)

                def up(k):
                    e, u = units[k]
                    for m in range(M):
                        if k:
                            pe.wait_ge(h_ready, j * (U * M) + ((k - 1) * M + m + 1))
                        nc.tensor.matmul(bank_h[m][:], chip.w1[:, e, m * P:(m + 1) * P], xT[:, u * HALF:(u + 1) * HALF],
                                         start=True, stop=True).then_inc(h_ps, 1)

                def down(k):
                    e, u = units[k]
                    pe.wait_ge(h_ready, j * (U * M) + (k + 1) * M)
                    if k:
                        pe.wait_ge(x_done, j * U + max(k - 1, 1))
                    for t in range(4):
                        for m in range(M):
                            last = nc.tensor.matmul(bank_y[k % 2][:, t, :], h[:, k % 2, m, t * P:(t + 1) * P],
                                                    chip.w2[:, e * M + m, :], start=(m == 0), stop=(m == M - 1))
                    last.then_inc(y_ps, 1)

                up(0)
                for k in range(1, U):
                    up(k)
                    if k == 2:
                        pe.wait_ge(comb_ready, j + 1)
                        nc.tensor.transpose(bank_x[1][:, 0:P], comb_w[:], chip.ident[:]).then_inc(combT_ps, 1)
                    if k == 3:
                        pe.wait_ge(combT_sb, j + 1)
                        for u in range(2):
                            nc.tensor.matmul(bank_x[u][:], combT[:], b2[:, 4 * u:4 * u + 4, :].rearrange("p t d -> p (t d)"),
                                             start=True, stop=True).then_inc(b2_ps, 1)
                    down(k - 1)
                down(U - 1)
                pe.wait_ge(b2_done, j * 2 + 2)
                pe.wait_ge(x_done, j * U + U - 1)

        @block.scalar
        def _(act):
            with act.Fori(0, STEPS) as j:
                for u in range(2):
                    act.wait_ge(xT_ps, j * 2 + u + 1)
                    nc.scalar.activation(xT[:, u * HALF:(u + 1) * HALF], bank_x[u][:], ACT.Identity).then_inc(xT_sb, 1)
                act.wait_ge(diff_ready, j + 1)
                nc.scalar.activation(raised[:], diff[:], ACT.Exp).then_inc(raised_ready, 1)
                for k, (e, u) in enumerate(units):
                    if k == 3:
                        act.wait_ge(combT_ps, j + 1)
                        nc.scalar.activation(combT[:], bank_x[1][:, 0:P], ACT.Identity).then_inc(combT_sb, 1)
                    for m in range(M):
                        act.wait_ge(h_ps, j * (U * M) + (k * M + m + 1))
                        nc.scalar.activation(h[:, k % 2, m, :], bank_h[m][:], ACT.Gelu,
                                             bias=b1[:, e * M + m:e * M + m + 1]).then_inc(h_ready, 1)

        @block.gpsimd
        def _(pool):
            nc.gpsimd.memset(b2[:], 0.0).then_inc(const, 1)
            nc.gpsimd.memset(rb_row[:], 0.0).then_inc(const, 1)
            nc.gpsimd.memset(comb_w[:], 0.0).then_inc(const, 1)
            nc.gpsimd.memset(two[:], BIG).then_inc(two_set, 1)
            steps = Steps(pool, pool_steps)
            pool.wait_ge(mv2_ready, 1)
            inner_rstd(pool, steps)
            with pool.Fori(0, STEPS) as j:
                steps = Steps(pool, pool_steps, j, 2, base=1)
                norm_rstd(chip, pool, j, mv_ready, steps, rstd_ready)
                pool.wait_ge(mv2_ready, j + 2)
                inner_rstd(pool, steps)

        @block.vector
        def _(dve):
            steps = Steps(dve, first_steps)
            inner_stats(steps)
            dve.wait_ge(rstd2_ready, 1)
            inner_rows()
            nc.vector.tensor_scalar(rw[:], chip.weight("router1"), chip.weight("rn_g"), None, ALU.mult)
            nc.vector.tensor_scalar(rn_b[:], chip.ones[:], chip.weight("rn_b"), None, ALU.mult).then_inc(rn_ready, 1)
            dve.wait_ge(bias_ps, 1)
            nc.vector.tensor_tensor(b1[:], bank_x[0][:, 0:E1 * M], chip.weight("b1"), ALU.add)
            nc.vector.tensor_copy(rb[:], bank_x[1][:, 0:E1])
            for e in range(E1):
                last = nc.vector.tensor_scalar(chip.w1[:, e, :], chip.w1[:, e, :], chip.weight("ln_gT")[:, e:e + 1], None, ALU.mult)
            last.then_inc(w1_ready, 1)
            dve.wait_ge(w1_ready, 1)
            dve.wait_ge(two_set, 1)
            dve.wait_ge(const, 3)
            with dve.Fori(0, STEPS) as j:
                steps = Steps(dve, dve_steps, j, 10)
                along = lambda ap: ap.unsqueeze(2).broadcast_to([P, TPI, E1])
                dve.wait_ge(logits, j + 1)
                steps.done(nc.vector.tensor_tensor(logit[:], bank_x[0][:, 0:TE].rearrange("p (t e) -> p t e", e=E1),
                                                   rb[:].unsqueeze(1).broadcast_to([P, TPI, E1]), ALU.add))
                nc.vector.tensor_copy(chip.spare[:], stats[:, 0, 0:1])
                for t in range(TPI):
                    last = nc.vector.max(best[:, t, :], logit[:, t, :])
                steps.done(last)
                nc.vector.tensor_tensor(diff[:], logit[:], along(best[:, :, 0]), ALU.subtract).then_inc(diff_ready, 1)
                steps.done(nc.vector.tensor_copy(two[:, :, 0:2], best[:, :, 0:2]))
                nc.vector.tensor_copy(chip.spare[:], stats[:, 0, 0:1])
                for t in range(TPI):
                    last = nc.vector.match_replace(left[:, t, :], two[:, t, :], logit[:, t, :], -BIG)
                steps.done(last)
                steps.done(nc.vector.tensor_scalar(left[:], left[:], -BIG, None, ALU.is_equal))
                dve.wait_ge(raised_ready, j + 1)
                steps.done(nc.vector.tensor_tensor(left[:], left[:], raised[:], ALU.mult))
                steps.done(nc.vector.tensor_reduce(total[:], left[:], AX_X, ALU.add))
                steps.done(nc.vector.reciprocal(share[:], total[:]))
                nc.vector.tensor_tensor(comb, left[:], along(share[:]), ALU.mult).then_inc(comb_ready, 1)
                dve.wait_ge(comb_ready, j + 1)
                jn = (j + 1) % STEPS
                for k, (e, u) in enumerate(units):
                    if k == 2:
                        dve.wait_ge(x_done, j * U + 2)
                        for v in range(2):
                            dve.wait_ge(b2_ps, j * 2 + v + 1)
                            rows = chip.x[:, ds(j * TPI + 4 * v, 4), :]
                            nc.vector.tensor_tensor(rows, bank_x[v][:].rearrange("p (t d) -> p t d", d=D), rows,
                                                    ALU.add).then_inc(b2_done, 1)
                        dve.wait_ge(b2_done, j * 2 + 2)
                    if k == 3:
                        norm_stats(chip, steps, jn, mv_ready)
                    if k == 4:
                        norm_rows(chip, dve, jn, j, rstd_ready, xn_ready)
                        dve.wait_ge(xn_ready, j + 1)
                        inner_stats(steps)
                    if k == 5:
                        dve.wait_ge(rstd2_ready, j + 2)
                        inner_rows()
                    dve.wait_ge(y_ps, j * U + (k + 1))
                    if k >= 2:
                        dve.wait_ge(x_done, j * U + (k - 1))
                    for t in range(4):
                        row = chip.x[:, ds(j * TPI + 4 * u + t, 1), :]
                        at = (4 * u + t) * E1 + e
                        last = nc.vector.scalar_tensor_tensor(row, bank_y[k % 2][:, t, :], comb_w[:, at:at + 1], row,
                                                              ALU.mult, ALU.add)
                    last.then_inc(x_done, 1)
                steps.close()


def stage_store(chip, out_dram):
    nc = chip.nc
    with ExitStack() as ctx:
        stored = ctx.enter_context(nc.semaphore("st_out"))
        block = ctx.enter_context(nc.Block())

        @block.sync
        def _(sp):
            o = out_dram.rearrange("(t p) d -> p t d", p=P)
            for n in range(STEPS):
                sp.dma_start(o[:, n * TPI:(n + 1) * TPI, :], chip.x[:, n * TPI:(n + 1) * TPI, :]).then_inc(stored, 16)
            sp.wait_ge(stored, 16 * STEPS)


def build(nc, a, stages="ABCDEF"):
    with ExitStack() as ctx:
        chip = Chip(nc, ctx)
        first = lambda sp: fetch_ffn0(chip, sp, a["ffn0_gate"], a["ffn0_up"], a["ffn0_down"])
        second = lambda sp: fetch_ffn1(chip, sp, a["ffn1_w1"], a["ffn1_w2"])
        with ExitStack() as early:
            chip.place_ffn0(early)
            stage_load(chip, a["x"], a["pack"], None if "A" in stages else first if "C" in stages else second if "D" not in stages else None)
            if "A" in stages:
                stage_cross0(chip, a["ctx"], a["ctxT"], first)
            if "B" in stages:
                stage_recurrence(chip)
            if "C" in stages:
                stage_experts0(chip)
        if "D" in stages:
            stage_heads(chip, a["ctxT"], a["mask"], second)
        if "E" in stages:
            stage_ssm(chip, a["b_out"])
        if "F" in stages:
            stage_experts1(chip, a["router_b"], a["b2"])
        stage_store(chip, a["out"])


def lay_out(v):
    f = lambda name: np.asarray(v[name])
    cols = lambda a: np.ascontiguousarray(a.reshape(-1, P).T)
    wide = lambda a: np.concatenate(list(a), axis=1)
    rows = lambda a: wide(a.reshape(-1, P, a.shape[-1]))

    def heads(a):
        w = np.zeros((D, D), a.dtype)
        for h in range(HEADS):
            w[h * HD:(h + 1) * HD, h * HD:(h + 1) * HD] = a
        return w

    l0, l1, f1 = "L0_attn_", "L1_attn_", "L1_ffn_"
    part = {
        "wqT": f("L0_xattn_Wq").T, "wkT": f("L0_xattn_Wk").T, "bq": cols(f("L0_xattn_bq")), "bk": cols(f("L0_xattn_bk")),
        "wrT": wide(f(l0 + "wr_w").transpose(0, 2, 1)), "wiT": wide(f(l0 + "wi_w").transpose(0, 2, 1)),
        "woT": wide(f(l0 + "wo_w").transpose(0, 2, 1)), "cw": wide(f(l0 + "conv_w")),
        "cb": f(l0 + "conv_b").T, "rb": f(l0 + "wr_b").T, "ib": f(l0 + "wi_b").T, "log_a": f(l0 + "log_a").T,
        "norm_w": f(l0 + "norm_w").T, "norm_out": cols(f(l0 + "norm_out_w")),
        "router0": f("L0_ffn_gate_w").T,
        "q_bd": heads(f("L1_xattn_queries_weight")), "k_bd": heads(f("L1_xattn_keys_weight")),
        "v_bd": heads(f("L1_xattn_values_weight")), "fc": f("L1_xattn_fc_weight"),
        "in_g": cols(f(l1 + "ln_g")), "in_b": cols(f(l1 + "ln_b")), "w_inT": f(l1 + "W_in").T,
        "b_in": cols(f(l1 + "b_in")), "conv_w": rows(f(l1 + "conv_w")[:, 0, :]), "conv_b": cols(f(l1 + "conv_b")),
        "ssm_A": rows(f(l1 + "A")), "ssm_B": rows(f(l1 + "Bm")), "w_cT": rows(f(l1 + "W_c").T),
        "w_dT": rows(f(l1 + "W_d").T), "b_c": cols(f(l1 + "b_c")), "b_d": cols(f(l1 + "b_d")),
        "log_delta": cols(f(l1 + "log_delta")), "w_outT": rows(f(l1 + "W_out").T),
        "rn_g": cols(f(f1 + "rn_g")), "rn_b": cols(f(f1 + "rn_b")), "router1": f(f1 + "router_w").T,
        "ln_gT": f(f1 + "ln_g").T, "ln_bT": f(f1 + "ln_b").T, "b1": cols(f(f1 + "b1")),
            }
    return {
        "x": f("x").reshape(B * S, D),
        "pack": np.concatenate([part[name] for name, _ in PACK], axis=1),
        "ctx": f("ctx_1024").transpose(1, 0, 2).reshape(KV, B * D),
        "ctxT": f("ctx_1024").transpose(2, 0, 1).reshape(D, B * KV),
        "mask": f("mask_1x1xSxS2_ik0").reshape(S, KV),
        "ffn0_gate": f("L0_ffn_w_gate").transpose(2, 0, 1), "ffn0_up": f("L0_ffn_w_up").transpose(2, 0, 1),
        "ffn0_down": f("L0_ffn_w_down").transpose(0, 2, 1).reshape(E0 * I0 // P, P, D).transpose(1, 0, 2),
        "ffn1_w1": f("L1_ffn_w1").transpose(1, 0, 2), "ffn1_w2": f("L1_ffn_w2").reshape(E1 * I1 // P, P, D).transpose(1, 0, 2),
        "b_out": f(l1 + "b_out").reshape(1, D), "router_b": f(f1 + "router_b").reshape(1, E1),
        "b2": f(f1 + "b2"),
    }


def kernel(**inputs):
    import concourse.bacc as bacc
    from concourse.bass_utils import run_bass_kernel_spmd

    nc = bacc.Bacc("TRN2", target_bir_lowering=False, num_devices=1)
    arrays, aps = {}, {}
    for name, a in lay_out(inputs).items():
        a = np.ascontiguousarray(a)
        arrays[name] = a
        aps[name] = nc.dram_tensor(name, a.shape, mybir.dt.from_np(a.dtype), kind="ExternalInput").ap()
    aps["out"] = nc.dram_tensor("out", (B * S, D), F32, kind="ExternalOutput").ap()
    build(nc, aps)
    r = run_bass_kernel_spmd(nc, [arrays], core_ids=[0])
    return np.asarray(r.results[0]["out"]).reshape(B, S, D)
```

```python
from contextlib import ExitStack

import numpy as np

import concourse.bass as bass
from concourse import mybir

F32 = mybir.dt.float32
BF16 = mybir.dt.bfloat16
ALU = mybir.AluOpType
ACT = mybir.ActivationFunctionType
AX_X = mybir.AxisListType.X
ds = bass.ds

P = 128
D = 128
B, S, KV = 64, 64, 128
TILES = B * S // P
TPI = 8
BPI = 2 * TPI
N = TPI * P
STEPS = TILES // TPI
HALF = N // 2
LN_EPS = 1e-5
RMS_EPS = 1e-6
LAYERS, TAPS = 3, 4
E0, CAP, I0 = 8, S // 8 * 2, 512
HEADS, HD = 16, 8
CH, SN = 256, 16
E1, I1 = 8, 512

PACK = [
    ("wqT", D), ("wkT", D), ("bq", 1), ("bk", 1),
    ("wrT", LAYERS * D), ("wiT", LAYERS * D), ("woT", LAYERS * D), ("cw", LAYERS * TAPS), ("cb", LAYERS),
    ("rb", LAYERS), ("ib", LAYERS), ("log_a", LAYERS), ("norm_w", LAYERS), ("norm_out", 1),
    ("router0", E0),
    ("q_bd", D), ("k_bd", D), ("v_bd", D), ("fc", D),
    ("in_g", 1), ("in_b", 1), ("w_inT", 2 * CH), ("b_in", 4), ("conv_w", 2 * TAPS), ("conv_b", 2),
    ("ssm_A", 2 * SN), ("ssm_B", 2 * SN), ("w_cT", 2 * CH), ("w_dT", 2 * CH), ("b_c", 2), ("b_d", 2),
    ("log_delta", 2), ("w_outT", 2 * D),
    ("rn_g", 1), ("rn_b", 1), ("router1", E1), ("ln_gT", E1), ("ln_bT", E1), ("b1", E1 * 4),
]
AT, _at = {}, 0
for _name, _w in PACK:
    AT[_name] = (_at, _at + _w)
    _at += _w
PACKED = _at


def semaphores(nc, ctx, prefix):
    taken = []

    def give_back():
        nc.clear_and_free_semaphores(taken)
        nc.all_engine_barrier()

    ctx.callback(give_back)

    def sem(name):
        taken.append(nc.alloc_semaphore(prefix + name))
        return taken[-1]

    return sem


class Steps:

    def __init__(self, eng, sem, j=0, per=0, base=0):
        self.eng, self.sem, self.j, self.per, self.base, self.k = eng, sem, j, per, base, 0

    def done(self, ins):
        self.k += 1
        ins.then_inc(self.sem, 1)
        self.eng.wait_ge(self.sem, self.j * self.per + (self.base + self.k))

    def close(self):
        assert self.k == self.per, (self.k, self.per)


class Chip:

    def __init__(self, nc, ctx):
        self.nc = nc

        def sb(name, shape, dt=F32):
            return ctx.enter_context(nc.sbuf_tensor("c_" + name, shape, dt))

        self.x = sb("x", [P, TILES, D])
        self.xn = sb("xn", [P, TPI, D])
        self.stats = sb("stats", [P, TPI, 6])
        self.mv = sb("mv", [P, TPI, 2])
        self.ve = sb("ve", [P, TPI])
        self.rstd = sb("rstd", [P, TPI])
        self.spare = sb("spare", [P, 1])
        self.eps = sb("eps", [P, TPI])
        self.neghalf = sb("neghalf", [P, TPI])
        self.w = sb("w", [P, PACKED])
        self.ident = sb("ident", [P, P])
        self.ones = sb("ones", [P, P])
        self.ffn0_in = ctx.enter_context(nc.semaphore("ffn0_in"))
        self.ffn1_in = ctx.enter_context(nc.semaphore("ffn1_in"))

    def place_ffn0(self, ctx):
        sb = lambda name, shape: ctx.enter_context(self.nc.sbuf_tensor("c_" + name, shape, F32))
        self.gate0 = sb("gate0", [P, E0, I0])
        self.up0 = sb("up0", [P, E0, I0])
        self.down0 = sb("down0", [P, E0 * I0 // P, D])

    def place_ffn1(self, ctx):
        sb = lambda name, shape: ctx.enter_context(self.nc.sbuf_tensor("c_" + name, shape, F32))
        self.w1 = sb("w1", [P, E1, I1])
        self.w2 = sb("w2", [P, E1 * I1 // P, D])

    def weight(self, name, rows=P):
        a, b = AT[name]
        return self.w[0:rows, a:b]



def norm_stats(chip, steps, jn, mv_ready):
    nc = chip.nc
    for t in range(TPI):
        last = nc.vector.bn_stats(chip.stats[:, t, :], chip.x[:, ds(jn * TPI + t, 1), :])
    steps.done(last)
    nc.vector.tensor_copy(chip.spare[:], chip.stats[:, 0, 0:1])
    for t in range(TPI):
        last = nc.vector.bn_aggr(chip.mv[:, t, :], chip.stats[:, t, :])
    last.then_inc(mv_ready, 1)


def norm_rstd(chip, pool, j, mv_ready, pool_steps, rstd_ready):
    nc = chip.nc
    pool.wait_ge(mv_ready, j + 1)
    pool_steps.done(nc.gpsimd.tensor_tensor(chip.ve[:], chip.mv[:, :, 1], chip.eps[:], ALU.add))
    nc.gpsimd.tensor_tensor(chip.rstd[:], chip.ve[:], chip.neghalf[:], ALU.pow).then_inc(rstd_ready, 1)


def norm_rows(chip, dve, jn, j, rstd_ready, xn_ready, xn=None):
    nc = chip.nc
    xn = chip.xn if xn is None else xn
    dve.wait_ge(rstd_ready, j + 1)
    for t in range(TPI):
        last = nc.vector.tensor_scalar(xn[:, t, :], chip.x[:, ds(jn * TPI + t, 1), :], chip.mv[:, t, 0:1],
                                       chip.rstd[:, t:t + 1], ALU.subtract, ALU.mult)
    last.then_inc(xn_ready, 1)


def fetch_ffn0(chip, sp, gate, up, down):
    for dst, src in ((chip.gate0, gate), (chip.up0, up), (chip.down0, down)):
        sp.dma_start(dst[:], src).then_inc(chip.ffn0_in, 16)


def fetch_ffn1(chip, sp, w1, w2):
    for dst, src in ((chip.w1, w1), (chip.w2, w2)):
        sp.dma_start(dst[:], src).then_inc(chip.ffn1_in, 16)


def stage_load(chip, x_dram, pack_dram, fetch=None):
    nc = chip.nc
    with ExitStack() as ctx:
        sem = semaphores(nc, ctx, "")
        x_in, x_first, w_in = sem("ld_x"), sem("ld_x0"), sem("ld_w")
        made, mv_ready, rstd_ready, xn_ready = sem("ld_made"), sem("ld_mv"), sem("ld_rstd"), sem("ld_xn")
        dve_steps, pool_steps = sem("ld_dve"), sem("ld_pool")
        block = ctx.enter_context(nc.Block())

        @block.sync
        def _(sp):
            xr = x_dram.rearrange("(t p) d -> p t d", p=P)
            sp.dma_start(chip.x[:, 0:TPI, :], xr[:, 0:TPI, :]).then_inc(x_first, 16)
            for n in range(1, STEPS):
                sp.dma_start(chip.x[:, n * TPI:(n + 1) * TPI, :], xr[:, n * TPI:(n + 1) * TPI, :]).then_inc(x_in, 16)
            if fetch:
                fetch(sp)
            sp.wait_ge(x_in, 16 * (STEPS - 1))

        @block.scalar
        def _(act):
            act.dma_start(chip.w[:], pack_dram).then_inc(w_in, 16)
            act.wait_ge(w_in, 16)

        @block.gpsimd
        def _(pool):
            nc.gpsimd.memset(chip.neghalf[:], -0.5).then_inc(made, 1)
            nc.gpsimd.memset(chip.ones[:], 1.0).then_inc(made, 1)
            nc.gpsimd.memset(chip.eps[:], LN_EPS).then_inc(made, 1)
            nc.gpsimd.memset(chip.ident[:], 0.0).then_inc(made, 1)
            pool.wait_ge(made, 4)
            nc.gpsimd.affine_select(out=chip.ident[:], in_=chip.ident[:], compare_op=ALU.not_equal, fill=1.0,
                                    base=0, pattern=[[-1, P]], channel_multiplier=1).then_inc(made, 1)
            norm_rstd(chip, pool, 0, mv_ready, Steps(pool, pool_steps), rstd_ready)

        @block.vector
        def _(dve):
            dve.wait_ge(x_first, 16)
            steps = Steps(dve, dve_steps)
            norm_stats(chip, steps, 0, mv_ready)
            norm_rows(chip, dve, 0, 0, rstd_ready, xn_ready)


def stage_cross0(chip, ctx_dram, ctxT_dram, fetch):
    nc = chip.nc
    SCALE = 1.0 / 32.0
    with ExitStack() as ctx:
        def sb(name, shape, dt=F32):
            return ctx.enter_context(nc.sbuf_tensor("a_" + name, shape, dt))

        def bank(name, shape):
            return ctx.enter_context(nc.psum_tensor("a_" + name, shape, F32))

        sem = semaphores(nc, ctx, "a_")

        ctx_n = sb("ctx_n", [P, BPI, D])
        ctx_t = sb("ctx_t", [P, BPI * KV])
        xT = sb("xT", [P, N])
        qT = sb("qT", [P, N])
        kT = sb("kT", [P, BPI * KV])
        prob = sb("prob", [P, TPI, KV])
        probT = sb("probT", [P, N])
        top = sb("top", [P, TPI])
        negtop = sb("negtop", [P, TPI])
        total = sb("total", [P, TPI])
        share = sb("share", [P, TPI])
        bank_xs = [bank(f"xs{u}", [P, 4, KV]) for u in range(2)]
        bank_qp = [bank(f"qp{u}", [P, HALF]) for u in range(2)]
        bank_k = [bank(f"k{u}", [P, HALF]) for u in range(2)]
        bank_o = [bank(f"o{u}", [P, 4, D]) for u in range(2)]
        ctxT_in, ctx_in = sem("ctxT_in"), sem("ctx_in")
        xT_ps, xT_sb, q_ps, q_sb, k_ps, k_sb = (sem(n) for n in ("xT_ps", "xT_sb", "q_ps", "q_sb", "k_ps", "k_sb"))
        scores, negtop_ready, prob_sb, probT_ps, probT_sb = (
            sem(n) for n in ("scores", "negtop", "prob_sb", "probT_ps", "probT_sb"))
        o_ps, x_done = sem("o_ps"), sem("x_done")
        mv_ready, rstd_ready, xn_ready = sem("mv"), sem("rstd"), sem("xn")
        dve_steps, pool_steps = sem("dve"), sem("pool")
        block = ctx.enter_context(nc.Block())

        @block.sync
        def _(sp):
            flat = ctx_n[:].rearrange("k b d -> k (b d)")
            sp.dma_start(ctx_t[:], ctxT_dram[:, 0:BPI * KV]).then_inc(ctxT_in, 16)
            sp.dma_start(flat, ctx_dram[:, 0:BPI * D]).then_inc(ctx_in, 16)
            with sp.Fori(1, STEPS) as j:
                sp.wait_ge(k_ps, j * 4)
                sp.dma_start(ctx_t[:], ctxT_dram[:, ds(j * (BPI * KV), BPI * KV)]).then_inc(ctxT_in, 16)
                sp.wait_ge(o_ps, j * 2)
                sp.dma_start(flat, ctx_dram[:, ds(j * (BPI * D), BPI * D)]).then_inc(ctx_in, 16)
            fetch(sp)

        @block.tensor
        def _(pe):
            with pe.Fori(0, STEPS) as j:
                for u in range(2):
                    for t in range(4):
                        last = nc.tensor.transpose(bank_xs[u][:, t, :], chip.xn[:, 4 * u + t, :], chip.ident[:])
                    last.then_inc(xT_ps, 1)
                pe.wait_ge(ctxT_in, j * 16 + 16)
                for c in range(4):
                    if c >= 2:
                        pe.wait_ge(k_sb, j * 4 + (c - 1))
                    nc.tensor.matmul(bank_k[c % 2][:], chip.weight("wkT"), ctx_t[:, c * HALF:(c + 1) * HALF],
                                     start=True, stop=True).then_inc(k_ps, 1)
                for u in range(2):
                    pe.wait_ge(xT_sb, j * 2 + u + 1)
                    nc.tensor.matmul(bank_qp[u][:], chip.weight("wqT"), xT[:, u * HALF:(u + 1) * HALF],
                                     start=True, stop=True).then_inc(q_ps, 1)
                for u in range(2):
                    pe.wait_ge(q_sb, j * 2 + u + 1)
                    pe.wait_ge(k_sb, j * 4 + 2 * u + 2)
                    for t in range(4):
                        for h in range(2):
                            b = 2 * (4 * u + t) + h
                            last = nc.tensor.matmul(bank_xs[u][64 * h:64 * h + 64, t, :], qT[:, b * S:(b + 1) * S],
                                                    kT[:, b * KV:(b + 1) * KV], start=True, stop=True)
                    last.then_inc(scores, 1)
                for u in range(2):
                    for t in range(4):
                        pe.wait_ge(prob_sb, j * 8 + 4 * u + t + 1)
                        last = nc.tensor.transpose(bank_qp[u][:, t * P:(t + 1) * P], prob[:, 4 * u + t, :], chip.ident[:])
                    last.then_inc(probT_ps, 1)
                pe.wait_ge(ctx_in, j * 16 + 16)
                for u in range(2):
                    pe.wait_ge(probT_sb, j * 2 + u + 1)
                    for t in range(4):
                        for h in range(2):
                            b = 2 * (4 * u + t) + h
                            last = nc.tensor.matmul(bank_o[u][64 * h:64 * h + 64, t, :], probT[:, b * S:(b + 1) * S],
                                                    ctx_n[:, b, :], start=True, stop=True)
                    last.then_inc(o_ps, 1)
                pe.wait_ge(xn_ready, j + 1)

        @block.scalar
        def _(act):
            with act.Fori(0, STEPS) as j:
                for u in range(2):
                    act.wait_ge(xT_ps, j * 2 + u + 1)
                    nc.scalar.activation(xT[:, u * HALF:(u + 1) * HALF], bank_xs[u][:].rearrange("p t k -> p (t k)"),
                                         ACT.Identity).then_inc(xT_sb, 1)
                for c in range(4):
                    act.wait_ge(k_ps, j * 4 + c + 1)
                    nc.scalar.activation(kT[:, c * HALF:(c + 1) * HALF], bank_k[c % 2][:], ACT.Identity,
                                         bias=chip.weight("bk")).then_inc(k_sb, 1)
                    if c % 2:
                        u = c // 2
                        act.wait_ge(q_ps, j * 2 + u + 1)
                        nc.scalar.activation(qT[:, u * HALF:(u + 1) * HALF], bank_qp[u][:], ACT.Identity,
                                             bias=chip.weight("bq")).then_inc(q_sb, 1)
                for u in range(2):
                    act.wait_ge(negtop_ready, j * 2 + u + 1)
                    for t in range(4):
                        nc.scalar.activation(prob[:, 4 * u + t, :], bank_xs[u][:, t, :], ACT.Exp, scale=SCALE,
                                             bias=negtop[:, 4 * u + t:4 * u + t + 1],
                                             accum_out=total[:, 4 * u + t:4 * u + t + 1]).then_inc(prob_sb, 1)

        @block.gpsimd
        def _(pool):
            with pool.Fori(0, STEPS) as j:
                norm_rstd(chip, pool, j, mv_ready, Steps(pool, pool_steps, j, 1), rstd_ready)

        @block.vector
        def _(dve):
            with dve.Fori(0, STEPS) as j:
                steps = Steps(dve, dve_steps, j, 5)
                jn = (j + 1) % STEPS
                norm_stats(chip, steps, jn, mv_ready)
                for u in range(2):
                    dve.wait_ge(scores, j * 2 + u + 1)
                    steps.done(nc.vector.tensor_reduce(top[:, 4 * u:4 * u + 4], bank_xs[u][:], AX_X, ALU.max))
                    nc.vector.tensor_scalar(negtop[:, 4 * u:4 * u + 4], top[:, 4 * u:4 * u + 4], -SCALE, None,
                                            ALU.mult).then_inc(negtop_ready, 1)
                for u in range(2):
                    dve.wait_ge(probT_ps, j * 2 + u + 1)
                    nc.vector.tensor_copy(probT[:, u * HALF:(u + 1) * HALF], bank_qp[u][:]).then_inc(probT_sb, 1)
                for u in range(2):
                    dve.wait_ge(prob_sb, j * 8 + 4 * u + 4)
                    steps.done(nc.vector.reciprocal(share[:, 4 * u:4 * u + 4], total[:, 4 * u:4 * u + 4]))
                    dve.wait_ge(o_ps, j * 2 + u + 1)
                    for t in range(4):
                        last = nc.vector.scalar_tensor_tensor(
                            chip.x[:, ds(j * TPI + 4 * u + t, 1), :], bank_o[u][:, t, :], share[:, 4 * u + t:4 * u + t + 1],
                            chip.x[:, ds(j * TPI + 4 * u + t, 1), :], ALU.mult, ALU.add)
                    last.then_inc(x_done, 1)
                dve.wait_ge(x_done, j * 2 + 2)
                norm_rows(chip, dve, jn, j, rstd_ready, xn_ready)
                steps.close()


def stage_recurrence(chip):
    nc = chip.nc
    LOG_A_MIN, LOG_SUM_MIN = float(np.log(1e-7)), -80.0
    STREAMS = 4
    PASSES = TILES * P // (STREAMS * HALF)
    CHAIN = {"conv": 4.6, "xc": 1.0, "gates": 5.7, "sigmoid": 1.4, "a2": 3.0, "decay": 3.8,
             "log": 3.4, "growlog": 0.8, "grow": 0.8, "h": 7.5, "y": 0.6, "square": 0.5, "mean": 1.7, "rs": 1.8, "norm": 0.5}
    STEPS_OF = ([("in", 0, 1.0), ("inT", 0, 1.0)] + [(what, l, CHAIN[what]) for l in range(LAYERS) for what in CHAIN]
                + [(what, LAYERS, CHAIN[what]) for what in ("square", "mean", "rs")]
                + [("z", 0, 1.0), ("zT", 0, 1.5), ("add", 0, 1.2)])
    LAG = 18.0

    DVE_CONV = (0, 2)
    CONVS = len({u // 2 for u in DVE_CONV})

    def order():
        all_steps = []
        for pair in ((0, 1), (2, 3)):
            start = LAG * (pair[0] // 2)
            for what, l, length in STEPS_OF:
                all_steps.append((start, pair, what, l))
                start += length
        for _, pair, what, l in sorted(all_steps):
            yield what, l, pair

    with ExitStack() as ctx:
        def sb(name, shape, dt=F32):
            return ctx.enter_context(nc.sbuf_tensor("b_" + name, shape, dt))

        def bank(name):
            return [ctx.enter_context(nc.psum_tensor(f"b_{name}{u}", [P, HALF], F32)) for u in range(STREAMS)]

        sem = semaphores(nc, ctx, "b_")
        per_stream = lambda name: [sem(f"{name}{u}") for u in range(STREAMS)]

        def wide(name):
            return sb(name, [P, STREAMS, HALF])

        hT = wide("hT")
        xc = wide("xc")
        r = wide("r")
        g = wide("g")
        run = wide("run")
        a2 = wide("a2")
        grow = wide("grow")
        decay = wide("decay")
        acc = r
        sq = r
        rs = a2
        xn2 = sb("xn2", [P, TPI, D])
        tap = sb("tap", [P, LAYERS * TAPS, P])
        fresh = sb("fresh", [P, HALF])
        rate = sb("rate", [P, LAYERS])
        rate8 = sb("rate8", [P, LAYERS])
        rate16 = sb("rate16", [P, LAYERS])
        rms_eps = sb("rms_eps", [P, 1])
        bank_c, bank_y = bank("c"), bank("y")
        const, taps_ready, rate_e, rate_l, rate_done = (sem(n) for n in ("const", "taps", "rate_e", "rate_l", "rate"))
        (xT_ps, hT_ready, conv_ps, xc_ready, gates_ps, gates_sb, a2_ready, clip_ready, ix_ready, ln_ready, t_ready, e_ready,
         h_ready, y_ps, sq_ready, m_ps, var_ln, rs_ready, z_ready, zT_ps, x_done) = (per_stream(n) for n in (
             "xT_ps", "hT", "conv_ps", "xc", "gates_ps", "gates_sb", "a2_s", "clip", "ix", "ln", "t", "e",
             "h", "y_ps", "sq_s", "m_ps", "var_ln", "rs_s", "z", "zT_ps", "x_done"))
        mv_ready, rstd_ready, xn_ready = sem("mv"), sem("rstd"), sem("xn")
        dve_steps, pool_steps = sem("dve"), sem("pool")
        block = ctx.enter_context(nc.Block())
        batches = lambda ap: ap.rearrange("p (b s) -> p b s", s=S)

        @block.tensor
        def _(pe):
            pe.wait_ge(const, 1)
            pe.wait_ge(taps_ready, 1)
            pe.wait_ge(xn_ready, 1)
            with pe.Fori(0, PASSES) as j:
                for what, l, pair in order():
                    w = slice(l * D, (l + 1) * D)
                    for u in pair:
                        if what == "in":
                            rows = (chip.xn, xn2)[u // 2]
                            for t in range(4):
                                last = nc.tensor.transpose(bank_y[u][:, t * P:(t + 1) * P], rows[:, 4 * (u % 2) + t, :], chip.ident[:])
                            last.then_inc(xT_ps[u], 1)
                        elif what == "conv" and u not in DVE_CONV:
                            pe.wait_ge(hT_ready[u], j * 4 + (l + 1))
                            nc.tensor.matmul(bank_c[u][:], tap[:, l * TAPS + TAPS - 1, :], hT[:, u, :], start=True, stop=False,
                                             skip_group_check=True)
                            for back in range(1, TAPS):
                                last = nc.tensor.matmul(batches(bank_c[u][:])[:, :, back:], tap[:, l * TAPS + TAPS - 1 - back, :],
                                                        batches(hT[:, u, :])[:, :, :S - back], start=False, stop=(back == TAPS - 1),
                                                        skip_group_check=True)
                            last.then_inc(conv_ps[u], 1)
                        elif what == "gates":
                            pe.wait_ge(xc_ready[u], j * 3 + (l + 1))
                            nc.tensor.matmul(bank_c[u][:], chip.weight("wrT")[:, w], xc[:, u, :], start=True, stop=True)
                            nc.tensor.matmul(bank_y[u][:], chip.weight("wiT")[:, w], xc[:, u, :],
                                             start=True, stop=True).then_inc(gates_ps[u], 1)
                        elif what == "y":
                            pe.wait_ge(h_ready[u], j * 3 + (l + 1))
                            nc.tensor.matmul(bank_y[u][:], chip.weight("woT")[:, w], acc[:, u, :],
                                             start=True, stop=True).then_inc(y_ps[u], 1)
                        elif what == "mean":
                            pe.wait_ge(sq_ready[u], j * 4 + (l + 1))
                            nc.tensor.matmul(bank_c[u][:], chip.ones[:], sq[:, u, :], start=True, stop=True).then_inc(m_ps[u], 1)
                        elif what == "zT":
                            pe.wait_ge(z_ready[u], j + 1)
                            for t in range(4):
                                last = nc.tensor.transpose(bank_c[u][:, t * P:(t + 1) * P], xc[:, u, t * P:(t + 1) * P], chip.ident[:])
                            last.then_inc(zT_ps[u], 1)
                pe.wait_ge(xn_ready, j * 2 + 3)
                for u in range(STREAMS):
                    pe.wait_ge(x_done[u], j + 1)

        @block.scalar
        def _(act):
            act.wait_ge(const, 1)
            nc.scalar.activation(rate[:], chip.weight("log_a"), ACT.Exp, scale=-1.0).then_inc(rate_e, 1)
            act.wait_ge(rate_e, 1)
            nc.scalar.activation(rate[:], rate[:], ACT.Ln, bias=1.0).then_inc(rate_l, 1)
            act.wait_ge(rate_done, 1)
            with act.Fori(0, PASSES) as j:
                for what, l, pair in order():
                    if what == "a2":
                        act.preload_act_table_set("natural_log_exp_and_others")
                    for u in pair:
                        if what == "inT":
                            act.wait_ge(xT_ps[u], j + 1)
                            nc.scalar.activation(hT[:, u, :], bank_y[u][:], ACT.Identity).then_inc(hT_ready[u], 1)
                        elif what == "xc" and u not in DVE_CONV:
                            act.wait_ge(conv_ps[u], j * 3 + (l + 1))
                            nc.scalar.activation(xc[:, u, :], bank_c[u][:], ACT.Identity,
                                                 bias=chip.weight("cb")[:, l:l + 1]).then_inc(xc_ready[u], 1)
                        elif what == "sigmoid":
                            act.wait_ge(gates_ps[u], j * 3 + (l + 1))
                            nc.scalar.activation(r[:, u, :], bank_c[u][:], ACT.Sigmoid, bias=chip.weight("rb")[:, l:l + 1])
                            nc.scalar.activation(g[:, u, :], bank_y[u][:], ACT.Sigmoid,
                                                 bias=chip.weight("ib")[:, l:l + 1]).then_inc(gates_sb[u], 1)
                        elif what == "a2":
                            act.wait_ge(gates_sb[u], j * 3 + (l + 1))
                            nc.scalar.activation(a2[:, u, :], r[:, u, :], ACT.Exp, scale=rate16[:, l:l + 1]).then_inc(a2_ready[u], 1)
                        elif what == "log":
                            act.wait_ge(clip_ready[u], j * 3 + (l + 1))
                            nc.scalar.activation(a2[:, u, :], a2[:, u, :], ACT.Ln, scale=-1.0).then_inc(ln_ready[u], 1)
                            nc.scalar.activation(decay[:, u, :], run[:, u, :], ACT.Exp)
                        elif what == "grow":
                            act.wait_ge(t_ready[u], j * 3 + (l + 1))
                            nc.scalar.activation(grow[:, u, :], grow[:, u, :], ACT.Exp).then_inc(e_ready[u], 1)
                        elif what == "square":
                            if l < LAYERS:
                                act.wait_ge(y_ps[u], j * 3 + (l + 1))
                                nc.scalar.activation(sq[:, u, :], bank_y[u][:], ACT.Square).then_inc(sq_ready[u], 1)
                            else:
                                act.wait_ge(hT_ready[u], j * 4 + 4)
                                nc.scalar.activation(sq[:, u, :], hT[:, u, :], ACT.Square).then_inc(sq_ready[u], 1)
                        elif what == "rs":
                            act.wait_ge(m_ps[u], j * 4 + (l + 1))
                            nc.scalar.activation(rs[:, u, :], bank_c[u][:], ACT.Ln, scale=1.0 / D, bias=rms_eps[:]).then_inc(var_ln[u], 1)
                    if what == "rs":
                        for u in pair:
                            act.wait_ge(var_ln[u], j * 4 + (l + 1))
                            nc.scalar.activation(rs[:, u, :], rs[:, u, :], ACT.Exp, scale=-0.5).then_inc(rs_ready[u], 1)

        @block.gpsimd
        def _(pool):
            nc.gpsimd.memset(fresh[:], 1.0).then_inc(pool_steps, 1)
            nc.gpsimd.memset(rms_eps[:], RMS_EPS).then_inc(pool_steps, 1)
            pool.wait_ge(pool_steps, 2)
            nc.gpsimd.memset(batches(fresh[:])[:, :, 0], 0.0).then_inc(const, 1)
            norm_rstd(chip, pool, 0, mv_ready, Steps(pool, pool_steps, base=2), rstd_ready)
            with pool.Fori(0, PASSES) as j:
                steps = Steps(pool, pool_steps, j, 2, 3)
                for what, l, pair in order():
                    if what == "decay":
                        for u in pair:
                            pool.wait_ge(gates_sb[u], j * 3 + (l + 1))
                            nc.gpsimd.tensor_tensor(g[:, u, :], g[:, u, :], xc[:, u, :], ALU.mult).then_inc(ix_ready[u], 1)
                        if l == 1:
                            norm_rstd(chip, pool, j * 2 + (1 + pair[0] // 2), mv_ready, steps, rstd_ready)
                steps.close()

        @block.vector
        def _(dve):
            dve.wait_ge(const, 1)
            for k in range(LAYERS * TAPS):
                last = nc.vector.tensor_scalar(tap[:, k, :], chip.ident[:], chip.weight("cw")[:, k:k + 1], None, ALU.mult)
            last.then_inc(taps_ready, 1)
            norm_stats(chip, Steps(dve, dve_steps), 1, mv_ready)
            dve.wait_ge(rate_l, 1)
            nc.vector.tensor_scalar(rate8[:], rate[:], -8.0, None, ALU.mult)
            nc.vector.tensor_scalar(rate16[:], rate[:], -16.0, None, ALU.mult).then_inc(rate_done, 1)
            dve.wait_ge(rate_done, 1)
            norm_rows(chip, dve, 1, 0, rstd_ready, xn_ready, xn2)
            with dve.Fori(0, PASSES) as j:
                steps = Steps(dve, dve_steps, j, 4 * 2 * LAYERS + 2 + CONVS * LAYERS * (TAPS - 1), 1)
                for what, l, pair in order():
                    if what == "decay":
                        for u in pair:
                            dve.wait_ge(a2_ready[u], j * 3 + (l + 1))
                            nc.vector.tensor_scalar(a2[:, u, :], a2[:, u, :], 1.0, -1e-6, ALU.subtract, ALU.min)
                            last = nc.vector.tensor_scalar(r[:, u, :], r[:, u, :], rate8[:, l:l + 1], LOG_A_MIN, ALU.mult, ALU.max)
                        steps.done(last)
                        for u in pair:
                            last = nc.vector.tensor_tensor_scan(run[:, u, :], fresh[:], r[:, u, :], 0.0, ALU.mult, ALU.add)
                        steps.done(last)
                        for u in pair:
                            nc.vector.tensor_scalar(run[:, u, :], run[:, u, :], LOG_SUM_MIN, None, ALU.max).then_inc(clip_ready[u], 1)
                        if l == 1:
                            norm_stats(chip, steps, ((j + 1) * 2 + pair[0] // 2) % STEPS, mv_ready)
                    elif what == "conv":
                        convs = [u for u in pair if u in DVE_CONV]
                        for u in convs:
                            dve.wait_ge(hT_ready[u], j * 4 + (l + 1))
                            last = nc.vector.tensor_scalar(xc[:, u, :], hT[:, u, :], chip.weight("cw")[:, (l + 1) * TAPS - 1:(l + 1) * TAPS],
                                                           chip.weight("cb")[:, l:l + 1], ALU.mult, ALU.add)
                        for back in range(1, TAPS):
                            k = (l + 1) * TAPS - 1 - back
                            for n, u in enumerate(convs):
                                if n == 0:
                                    steps.done(last)
                                last = nc.vector.scalar_tensor_tensor(
                                    batches(xc[:, u, :])[:, :, back:], batches(hT[:, u, :])[:, :, :S - back],
                                    chip.weight("cw")[:, k:k + 1], batches(xc[:, u, :])[:, :, back:], ALU.mult, ALU.add)
                                if back == TAPS - 1:
                                    last.then_inc(xc_ready[u], 1)
                    elif what == "growlog":
                        for u in pair:
                            dve.wait_ge(ln_ready[u], j * 3 + (l + 1))
                            nc.vector.scalar_tensor_tensor(grow[:, u, :], a2[:, u, :], 0.5, run[:, u, :],
                                                           ALU.mult, ALU.subtract).then_inc(t_ready[u], 1)
                        if l == 1:
                            norm_rows(chip, dve, ((j + 1) * 2 + pair[0] // 2) % STEPS, j * 2 + (1 + pair[0] // 2), rstd_ready, xn_ready,
                                      (chip.xn, xn2)[pair[0] // 2])
                    elif what == "h":
                        for u in pair:
                            dve.wait_ge(e_ready[u], j * 3 + (l + 1))
                            dve.wait_ge(ix_ready[u], j * 3 + (l + 1))
                            last = nc.vector.tensor_tensor(grow[:, u, :], grow[:, u, :], g[:, u, :], ALU.mult)
                        steps.done(last)
                        for u in pair:
                            last = nc.vector.tensor_tensor_scan(acc[:, u, :], fresh[:], grow[:, u, :], 0.0, ALU.mult, ALU.add)
                        steps.done(last)
                        for u in pair:
                            nc.vector.tensor_tensor(acc[:, u, :], acc[:, u, :], decay[:, u, :], ALU.mult).then_inc(h_ready[u], 1)
                    elif what == "norm":
                        for u in pair:
                            dve.wait_ge(rs_ready[u], j * 4 + (l + 1))
                            nc.vector.scalar_tensor_tensor(hT[:, u, :], bank_y[u][:], chip.weight("norm_w")[:, l:l + 1],
                                                           rs[:, u, :], ALU.mult, ALU.mult).then_inc(hT_ready[u], 1)
                    elif what == "z":
                        for u in pair:
                            dve.wait_ge(rs_ready[u], j * 4 + (LAYERS + 1))
                            nc.vector.scalar_tensor_tensor(xc[:, u, :], hT[:, u, :], chip.weight("norm_out"),
                                                           rs[:, u, :], ALU.mult, ALU.mult).then_inc(z_ready[u], 1)
                    elif what == "add":
                        for u in pair:
                            dve.wait_ge(zT_ps[u], j + 1)
                            rows = chip.x[:, ds(j * (STREAMS * 4) + 4 * u, 4), :]
                            nc.vector.tensor_tensor(rows, bank_c[u][:].rearrange("p (t d) -> p t d", d=D), rows,
                                                    ALU.add).then_inc(x_done[u], 1)
                for u in range(STREAMS):
                    dve.wait_ge(x_done[u], j + 1)
                steps.close()

def stage_experts0(chip):
    nc = chip.nc
    SLOTS = E0 * CAP
    COLS = BPI * CAP
    M = I0 // P
    TE = TPI * E0
    with ExitStack() as ctx:
        def sb(name, shape, dt=F32):
            return ctx.enter_context(nc.sbuf_tensor("c0_" + name, shape, dt))

        def bank(name, shape):
            return ctx.enter_context(nc.psum_tensor("c0_" + name, shape, F32))

        sem = semaphores(nc, ctx, "c0_")

        xT = sb("xT", [P, N])
        top = sb("top", [P, TPI])
        shifted = sb("shifted", [P, TPI, E0])
        raised = sb("raised", [P, TPI, E0])
        total = sb("total", [P, TPI])
        share = sb("share", [P, TPI])
        aff_w = sb("aff", [P, P])
        aff = aff_w[:, 0:TE].rearrange("p (t e) -> p t e", e=E0)
        affT = sb("affT", [TE, P])
        best = sb("best", [TE, 2, 2, 8])
        left1 = sb("left1", [TE, P])
        left2 = sb("left2", [TE, P])
        chosen = sb("chosen", [TE, P])
        count = sb("count", [TE, P])
        key_w = sb("key", [P, P])
        key = key_w[0:TE, :]
        keyT = sb("keyT", [P, TE])
        fresh = sb("fresh", [TE, P])
        slot_i = sb("slot_i", [P, CAP], mybir.dt.int32)
        slot = sb("slot", [P, CAP])
        sel = sb("sel", [P, TE, CAP])
        selg = sb("selg", [P, TE, CAP])
        selT = sb("selT", [P, N])
        xe = sb("xe", [P, E0, BPI, CAP])
        silu = sb("silu", [P, 2, 2 * COLS])
        h = sb("h", [P, 2, 2 * COLS])
        yT = sb("yT", [P, BPI, E0, CAP])
        y = sb("y", [P, BPI, D])
        bank_x = [bank(f"x{u}", [P, HALF]) for u in range(2)]
        bank_g = [bank(f"g{u}", [P, HALF]) for u in range(2)]
        bank_u = [bank(f"u{u}", [P, HALF]) for u in range(2)]
        bank_y = [bank(f"y{u}", [P, HALF]) for u in range(2)]
        spread = [bank_g[0], bank_u[0], bank_g[1], bank_u[1]]
        const, made = sem("const"), sem("made")
        xT_ps, xT_sb, logits, shifted_ready, raised_ready, aff_ready = (
            sem(n) for n in ("xT_ps", "xT_sb", "logits", "shifted_s", "raised_s", "aff_s"))
        affT_ps, key_ready, keyT_ps, sel_ready, selg_ready = (sem(n) for n in ("affT_ps", "key_s", "keyT_ps", "sel_s", "selg_s"))
        xe_ps, xe_sb, gu_ps, silu_ready, h_ready, yT_ps, yT_sb = (
            sem(n) for n in ("xe_ps", "xe_sb", "gu_ps", "silu_s", "h_s", "yT_ps", "yT_sb"))
        selT_ps, selT_sb, y_ps, y_sb, out_ps, x_done = (sem(n) for n in ("selT_ps", "selT_sb", "y_ps", "y_sb", "out_ps", "x_done"))
        mv_ready, rstd_ready, xn_ready = sem("mv"), sem("rstd"), sem("xn")
        dve_steps, pool_steps = sem("dve"), sem("pool")
        block = ctx.enter_context(nc.Block())
        parts = [(e, m) for e in range(E0) for m in range(M // 2)]

        PE_FRONT = {"x": 3, "logits": 4, "aff": 8, "key": 13}
        ACT_FRONT = {"x": 3, "exp": 6}
        DVE_FRONT = {"shift": 5, "share": 7, "top1": 9, "top2": 10, "slots": 11, "sel": 14}

        @block.tensor
        def _(pe):
            def front(k, step):
                if step == "x":
                    for u in range(2):
                        for t in range(4):
                            last = nc.tensor.transpose(bank_x[u][:, t * P:(t + 1) * P], chip.xn[:, 4 * u + t, :], chip.ident[:])
                        last.then_inc(xT_ps, 1)
                elif step == "logits":
                    pe.wait_ge(xT_sb, k * 2 + 2)
                    for t in range(TPI):
                        last = nc.tensor.matmul(bank_x[0][:, t * E0:(t + 1) * E0], xT[:, t * P:(t + 1) * P],
                                                chip.weight("router0"), start=True, stop=True)
                    last.then_inc(logits, 1)
                elif step == "aff":
                    pe.wait_ge(aff_ready, k + 1)
                    nc.tensor.transpose(bank_x[1][:, 0:P], aff_w[:], chip.ident[:]).then_inc(affT_ps, 1)
                elif step == "key":
                    pe.wait_ge(key_ready, k + 1)
                    nc.tensor.transpose(bank_x[0][:, 0:P], key_w[:], chip.ident[:]).then_inc(keyT_ps, 1)

            for step in ("x", "logits", "aff", "key"):
                front(0, step)
            pe.wait_ge(chip.ffn0_in, 16 * 3)
            with pe.Fori(0, STEPS) as j:
                pe.wait_ge(sel_ready, j + 1)
                for q in range(4):
                    for n in range(4):
                        t, half = 4 * (q // 2) + n, slice(64 * (q % 2), 64 * (q % 2) + 64)
                        last = nc.tensor.matmul(spread[q][:, n * SLOTS:(n + 1) * SLOTS], chip.xn[half, t, :],
                                                sel[half, t * E0:(t + 1) * E0, :].rearrange("p e c -> p (e c)"),
                                                start=True, stop=True)
                    last.then_inc(xe_ps, 1)
                pe.wait_ge(selg_ready, j + 1)
                for u in range(2):
                    for t in range(4):
                        n = 4 * u + t
                        last = nc.tensor.transpose(bank_x[u][:, t * P:(t + 1) * P],
                                                   selg[:, n * E0:(n + 1) * E0, :].rearrange("p e c -> p (e c)"), chip.ident[:])
                    last.then_inc(selT_ps, 1)

                def answer(i):
                    e, m = parts[i]
                    pe.wait_ge(h_ready, j * len(parts) + i + 1)
                    if m == 0 and e >= 2:
                        pe.wait_ge(yT_sb, j * E0 + (e - 1))
                    for c in range(2):
                        n = 2 * m + c
                        last = nc.tensor.matmul(bank_y[e % 2][:, 0:COLS], chip.down0[:, e * M + n, :],
                                                h[:, i % 2, c * COLS:(c + 1) * COLS], start=(n == 0), stop=(n == M - 1))
                    if m == M // 2 - 1:
                        last.then_inc(yT_ps, 1)

                for i, (e, m) in enumerate(parts):
                    if i == PE_FRONT["x"]:
                        pe.wait_ge(xn_ready, j + 1)
                        pe.wait_ge(selT_sb, j * 2 + 2)
                    for step, at in PE_FRONT.items():
                        if at == i:
                            front(j + 1, step)
                    pe.wait_ge(xe_sb, j * 4 + 4)
                    if i >= 2:
                        pe.wait_ge(h_ready, j * len(parts) + i - 1)
                    tokens = xe[:, e, :, :].rearrange("p b c -> p (b c)")
                    for w, dst in ((chip.gate0, bank_g[i % 2]), (chip.up0, bank_u[i % 2])):
                        for c in range(2):
                            n = 2 * m + c
                            last = nc.tensor.matmul(dst[:, c * COLS:(c + 1) * COLS], w[:, e, n * P:(n + 1) * P], tokens,
                                                    start=True, stop=True)
                    last.then_inc(gu_ps, 1)
                    if i:
                        answer(i - 1)
                answer(len(parts) - 1)
                pe.wait_ge(yT_sb, j * E0 + E0)
                for q in range(4):
                    for n in range(4):
                        b = 4 * q + n
                        last = nc.tensor.transpose(spread[q][:, n * D:(n + 1) * D],
                                                   yT[:, b, :, :].rearrange("p e c -> p (e c)"), chip.ident[:])
                    last.then_inc(y_ps, 1)
                for u in range(2):
                    pe.wait_ge(y_sb, j * 4 + 2 * u + 2)
                    for t in range(4):
                        for g in range(2):
                            b = 2 * (4 * u + t) + g
                            last = nc.tensor.matmul(bank_y[u][64 * g:64 * g + 64, t * D:(t + 1) * D],
                                                    selT[:, b * S:(b + 1) * S], y[:, b, :], start=True, stop=True)
                    last.then_inc(out_ps, 1)
                pe.wait_ge(x_done, j * 2 + 2)

        @block.scalar
        def _(act):
            def front(k, step):
                if step == "x":
                    for u in range(2):
                        act.wait_ge(xT_ps, k * 2 + (u + 1))
                        nc.scalar.activation(xT[:, u * HALF:(u + 1) * HALF], bank_x[u][:], ACT.Identity).then_inc(xT_sb, 1)
                elif step == "exp":
                    act.wait_ge(shifted_ready, k + 1)
                    nc.scalar.activation(raised[:], shifted[:], ACT.Exp).then_inc(raised_ready, 1)

            for step in ACT_FRONT:
                front(0, step)
            with act.Fori(0, STEPS) as j:
                for q in range(4):
                    act.wait_ge(xe_ps, j * 4 + q + 1)
                    to = xe[:].rearrange("p e (t g) c -> p e t g c", g=2)[:, :, 4 * (q // 2):4 * (q // 2) + 4, q % 2, :]
                    nc.scalar.activation(to.rearrange("p e t c -> p t e c"),
                                         spread[q][:].rearrange("p (t e c) -> p t e c", t=4, e=E0),
                                         ACT.Identity).then_inc(xe_sb, 1)
                for u in range(2):
                    act.wait_ge(selT_ps, j * 2 + u + 1)
                    nc.scalar.activation(selT[:, u * HALF:(u + 1) * HALF], bank_x[u][:], ACT.Identity).then_inc(selT_sb, 1)
                def copy_answers(e):
                    act.wait_ge(yT_ps, j * E0 + e + 1)
                    nc.scalar.activation(yT[:, :, e, :], bank_y[e % 2][:, 0:COLS].rearrange("p (b c) -> p b c", c=CAP),
                                         ACT.Identity).then_inc(yT_sb, 1)

                for i, (e, m) in enumerate(parts):
                    act.wait_ge(gu_ps, j * len(parts) + i + 1)
                    nc.scalar.activation(silu[:, i % 2, :], bank_g[i % 2][:], ACT.Silu).then_inc(silu_ready, 1)
                    if m == 1 and e:
                        copy_answers(e - 1)
                    for step, at in ACT_FRONT.items():
                        if at == i:
                            front(j + 1, step)
                copy_answers(E0 - 1)
                for q in range(0, 4, 2):
                    act.wait_ge(y_ps, j * 4 + q + 1)
                    nc.scalar.activation(y[:, 4 * q:4 * q + 4, :].rearrange("p b d -> p (b d)"), spread[q][:],
                                         ACT.Identity).then_inc(y_sb, 1)
                    act.wait_ge(y_ps, j * 4 + q + 2)
                    nc.scalar.activation(y[:, 4 * q + 4:4 * q + 8, :].rearrange("p b d -> p (b d)"), spread[q + 1][:],
                                         ACT.Identity).then_inc(y_sb, 1)

        @block.gpsimd
        def _(pool):
            nc.gpsimd.iota(slot_i[:], [[1, CAP]], base=1, channel_multiplier=0).then_inc(made, 1)
            nc.gpsimd.memset(fresh[:], 1.0).then_inc(made, 1)
            nc.gpsimd.memset(aff_w[:], 0.0).then_inc(const, 1)
            nc.gpsimd.memset(key_w[:], 0.0).then_inc(const, 1)
            pool.wait_ge(made, 2)
            nc.gpsimd.tensor_copy(slot[:], slot_i[:]).then_inc(const, 1)
            nc.gpsimd.memset(fresh[:].rearrange("p (b s) -> p b s", s=S)[:, :, 0], 0.0).then_inc(const, 1)
            def weigh(k):
                pool.wait_ge(sel_ready, k + 1)
                nc.gpsimd.tensor_tensor(selg[:], sel[:],
                                        aff_w[:, 0:TE].unsqueeze(2).broadcast_to([P, TE, CAP]),
                                        ALU.mult).then_inc(selg_ready, 1)

            weigh(0)
            with pool.Fori(0, STEPS) as j:
                norm_rstd(chip, pool, j, mv_ready, Steps(pool, pool_steps, j, 1), rstd_ready)
                weigh(j + 1)

        @block.vector
        def _(dve):
            dve.wait_ge(const, 4)
            scores = bank_x[0][:, 0:TE].rearrange("p (t e) -> p t e", e=E0)
            along = lambda ap: ap.unsqueeze(2).broadcast_to([P, TPI, E0])

            def largest(steps, rnd, src, left):
                nc.vector.tensor_copy(chip.spare[:], chip.stats[:, 0, 0:1])
                for g in range(2):
                    last = nc.vector.max(best[:, rnd, g, :], src[:, g * S:(g + 1) * S])
                steps.done(last)
                nc.vector.tensor_copy(chip.spare[:], chip.stats[:, 0, 0:1])
                for g in range(2):
                    last = nc.vector.match_replace(left[:, g * S:(g + 1) * S], best[:, rnd, g, :],
                                                   src[:, g * S:(g + 1) * S], -1.0)
                steps.done(last)

            def front(k, step, steps):
                if step == "shift":
                    dve.wait_ge(logits, k + 1)
                    steps.done(nc.vector.tensor_reduce(top[:], scores, AX_X, ALU.max))
                    nc.vector.tensor_tensor(shifted[:], scores, along(top[:]), ALU.subtract).then_inc(shifted_ready, 1)
                elif step == "share":
                    dve.wait_ge(raised_ready, k + 1)
                    steps.done(nc.vector.tensor_reduce(total[:], raised[:], AX_X, ALU.add))
                    steps.done(nc.vector.reciprocal(share[:], total[:]))
                    nc.vector.tensor_tensor(aff, raised[:], along(share[:]), ALU.mult).then_inc(aff_ready, 1)
                elif step == "top1":
                    dve.wait_ge(affT_ps, k + 1)
                    steps.done(nc.vector.tensor_copy(affT[:], bank_x[1][0:TE, 0:P]))
                    largest(steps, 0, affT, left1)
                elif step == "top2":
                    largest(steps, 1, left1, left2)
                elif step == "slots":
                    steps.done(nc.vector.tensor_scalar(chosen[:], left2[:], 0.0, None, ALU.is_lt))
                    steps.done(nc.vector.tensor_tensor_scan(count[:], fresh[:], chosen[:], 0.0, ALU.mult, ALU.add))
                    nc.vector.tensor_tensor(key, count[:], chosen[:], ALU.mult).then_inc(key_ready, 1)
                elif step == "sel":
                    dve.wait_ge(keyT_ps, k + 1)
                    steps.done(nc.vector.tensor_copy(keyT[:], bank_x[0][:, 0:TE]))
                    nc.vector.tensor_tensor(sel[:], keyT[:].unsqueeze(2).broadcast_to([P, TE, CAP]),
                                            slot[:].unsqueeze(1).broadcast_to([P, TE, CAP]), ALU.is_equal).then_inc(sel_ready, 1)

            FRONT_STEPS = 11
            steps = Steps(dve, dve_steps)
            for step in DVE_FRONT:
                front(0, step, steps)
            assert steps.k == FRONT_STEPS
            with dve.Fori(0, STEPS) as j:
                steps = Steps(dve, dve_steps, j, FRONT_STEPS + 1, FRONT_STEPS)
                jn = (j + 1) % STEPS
                norm_stats(chip, steps, jn, mv_ready)
                dve.wait_ge(xe_ps, j * 4 + 4)
                norm_rows(chip, dve, jn, j, rstd_ready, xn_ready)
                for i in range(len(parts)):
                    dve.wait_ge(silu_ready, j * len(parts) + i + 1)
                    nc.vector.tensor_tensor(h[:, i % 2, :], silu[:, i % 2, :], bank_u[i % 2][:], ALU.mult).then_inc(h_ready, 1)
                    for step, at in DVE_FRONT.items():
                        if at == i:
                            front(j + 1, step, steps)
                for u in range(2):
                    dve.wait_ge(out_ps, j * 2 + u + 1)
                    rows = chip.x[:, ds(j * TPI + 4 * u, 4), :]
                    nc.vector.tensor_tensor(rows, bank_y[u][:].rearrange("p (t d) -> p t d", d=D), rows,
                                            ALU.add).then_inc(x_done, 1)
                steps.close()

def stage_heads(chip, ctxT_dram, mask_dram, fetch):
    nc = chip.nc
    PAIRS, UP = HEADS // 2, 4
    UNITS = BPI * PAIRS // UP
    DEEP = 3
    SLOTS = -(-UNITS // DEEP) * DEEP
    HB = BPI // 2
    HU = UNITS // 2
    PREP = [("x", 0), ("k", 0), ("k", 1), ("q", 0), ("v", 0), ("v", 1)]
    EXTRA = {s: (what, 1, c) for s, (what, c) in enumerate(PREP)}
    EXTRA |= {8: ("z", -1, 0), 10: ("out", -1, 0)}
    EXTRA |= {HU + s: (what, 2, c) for s, (what, c) in enumerate(PREP)}
    EXTRA |= {HU + 8: ("z", 0, 0), HU + 10: ("out", 0, 0)}

    def at(j, s, lag, last):
        u = s - lag
        if 0 <= u < UNITS:
            return j, u
        if SLOTS <= u and not last:
            return j + 1, u - SLOTS
        return None

    def passes(eng, body):
        body(0, range(DEEP), False)
        with eng.Fori(0, STEPS - 1) as j:
            body(j, range(DEEP, SLOTS + DEEP), False)
        body(STEPS - 1, range(DEEP, SLOTS + DEEP), True)

    VW = HD + 1
    SCALE = float(1.0 / np.sqrt(D))
    with ExitStack() as ctx:
        def sb(name, shape, dt=F32):
            return ctx.enter_context(nc.sbuf_tensor("d_" + name, shape, dt))

        sem = semaphores(nc, ctx, "d_")

        ctx_t = sb("ctx_t", [P, BPI * KV])
        mask_i = sb("mask_i", [P, KV], mybir.dt.int32)
        mask_add = sb("mask_add", [P, UP, KV], BF16)
        ident_b = sb("ident_b", [P, P], BF16)
        own = sb("own", [P, HEADS])
        xT = sb("xT", [P, HALF])
        qT = sb("qT", [P, HALF])
        qd = sb("qd", [P, BPI, HEADS, S])
        kT = sb("kT", [P, BPI * KV])
        v = sb("v", [P, BPI, HEADS, VW])
        top = sb("top", [P, UNITS, UP])
        negtop = sb("negtop", [P, UNITS, UP])
        prob = sb("prob", [P, DEEP, UP, KV])
        probT = sb("probT", [P, 2, UP * P])
        share = sb("share", [P, 2, 2, PAIRS])
        z = sb("z", [P, TPI, PAIRS, 2, HD])
        zT = sb("zT", [P, HALF])
        bk = [ctx.enter_context(nc.psum_tensor(f"d_bk{i}", [P, HALF], F32)) for i in range(8)]
        bank_t, bank_o, bank_e, bank_s = bk[0:2], bk[2:4], bk[4:7], bk[7]
        const, const2, mask_in, mask_ready, qd_zero = (sem(n) for n in ("const", "const2", "mask_in", "mask", "qd_zero"))
        ctx_in = [sem("ctx_in0"), sem("ctx_in1")]
        xT_ps, xT_sb, k_ps, k_sb, q_ps, q_sb, v_ps, v_sb = (
            sem(n) for n in ("xT_ps", "xT_sb", "k_ps", "k_sb", "q_ps", "q_sb", "v_ps", "v_sb"))
        qd_pool, qd_dve, energy, negtop_ready, prob_ready, probT_ps, probT_sa, probT_sb, o_ps = (
            sem(n) for n in ("qd_pool", "qd_dve", "energy", "negtop_s", "prob_s", "probT_ps", "probT_sa", "probT_sb", "o_ps"))
        z_ready, zT_ps, zT_sb, out_ps, x_done = (sem(n) for n in ("z_s", "zT_ps", "zT_sb", "out_ps", "x_done"))
        mv_ready, rstd_ready, xn_ready = sem("mv"), sem("rstd"), sem("xn")
        dve_steps, pool_steps = sem("dve"), sem("pool")
        block = ctx.enter_context(nc.Block())

        @block.sync
        def _(sp):
            for g in range(2):
                sp.dma_start(mask_i[64 * g:64 * g + 64, :], mask_dram).then_inc(mask_in, 16)
            W = HB * KV
            for u in range(2):
                sp.dma_start(ctx_t[:, u * W:(u + 1) * W], ctxT_dram[:, u * W:(u + 1) * W]).then_inc(ctx_in[u], 16)
            with sp.Fori(0, STEPS - 1) as j:
                for u in range(2):
                    sp.wait_ge(v_ps, j * 4 + (2 * u + 2))
                    sp.dma_start(ctx_t[:, u * W:(u + 1) * W],
                                 ctxT_dram[:, ds(j * 2 * W + (2 + u) * W, W)]).then_inc(ctx_in[u], 16)
            for u in range(2):
                sp.wait_ge(ctx_in[u], 16 * STEPS)
            fetch(sp)

        @block.tensor
        def _(pe):
            def extra(j, what, half, c, last_pass=False, bank=None):
                u, fresh = half % 2, bank is not None
                bank = bank_s if bank is None else bank
                if what == "x":
                    if half == 1 and not (type(j) is int and j == 0):
                        pe.wait_ge(x_done, j * 2)
                    elif half == 2:
                        pe.wait_ge(x_done, j * 2 + 1)
                        pe.wait_ge(xn_ready, j + 1)
                    for t in range(4):
                        last = nc.tensor.transpose(bank[:, t * P:(t + 1) * P], chip.xn[:, 4 * u + t, :], chip.ident[:])
                    last.then_inc(xT_ps, 1)
                elif what == "k":
                    if c == 0:
                        pe.wait_ge(ctx_in[u], j * 16 + 16 * (half // 2 + 1))
                    if not fresh:
                        if c == 0:
                            pe.wait_ge(xT_sb, j * 2 + (half + 1))
                        else:
                            pe.wait_ge(k_sb, j * 4 + (2 * half + 1))
                    cols = u * HB * KV + c * HALF
                    nc.tensor.matmul(bank[:], chip.weight("k_bd"), ctx_t[:, cols:cols + HALF], start=True, stop=True).then_inc(k_ps, 1)
                elif what == "q":
                    if fresh:
                        pe.wait_ge(xT_sb, 1)
                    else:
                        pe.wait_ge(k_sb, j * 4 + (2 * half + 2))
                    nc.tensor.matmul(bank[:], chip.weight("q_bd"), xT[:], start=True, stop=True).then_inc(q_ps, 1)
                elif what == "v":
                    if not fresh:
                        if c == 0:
                            pe.wait_ge(q_sb, j * 2 + (half + 1))
                        else:
                            pe.wait_ge(v_sb, j * 4 + (2 * half + 1))
                    for n in range(4):
                        b = u * HB + 4 * c + n
                        last = nc.tensor.matmul(bank[:, n * D:(n + 1) * D], ctx_t[:, b * KV:(b + 1) * KV],
                                                chip.weight("v_bd"), start=True, stop=True)
                    last.then_inc(v_ps, 1)
                elif what == "z":
                    if last_pass:
                        pe.wait_ge(x_done, j * 2 + (half + 1))
                    else:
                        pe.wait_ge(v_sb, j * 4 + 6 + 2 * half)
                    pe.wait_ge(z_ready, j * TPI + (TPI // 2 * half + 5))
                    for t in range(4):
                        last = nc.tensor.transpose(bank[:, t * P:(t + 1) * P],
                                                   z[:, 4 * u + t, :, :, :].rearrange("p a h f -> p (a h f)"), chip.ident[:])
                    last.then_inc(zT_ps, 1)
                else:
                    pe.wait_ge(zT_sb, j * 2 + (half + 2))
                    for t in range(4):
                        last = nc.tensor.matmul(bank[:, t * D:(t + 1) * D], zT[:, t * P:(t + 1) * P],
                                                chip.weight("fc"), start=True, stop=True)
                    last.then_inc(out_ps, 1)

            pe.wait_ge(const, 1)
            for n, (what, c) in enumerate(PREP):
                extra(0, what, 0, c, bank=bk[n])
            pe.wait_ge(v_sb, 2)
            pe.wait_ge(mask_ready, 2)

            def slots(j, which, last_pass):
                for s in which:
                    if now := at(j, s, 0, last_pass):
                        jp, u = now
                        b, g = u // 2, u % 2
                        if u % HU == 0:
                            half = u // HU
                            pe.wait_ge(k_sb, jp * 4 + (2 * half + 2))
                            pe.wait_ge(qd_pool, jp * 4 + (2 * half + 2))
                            pe.wait_ge(qd_dve, jp * 2 + (half + 1))
                        e = bank_e[u % DEEP]
                        nc.tensor.matmul(e[:], ident_b[:], mask_add[:].rearrange("p i k -> p (i k)"),
                                         start=True, stop=False, skip_group_check=True)
                        for i in range(UP):
                            h = 2 * (UP * g + i)
                            last = nc.tensor.matmul(e[:, i * KV:(i + 1) * KV],
                                                    qd[:, b, h:h + 2, :].rearrange("p h q -> p (h q)"),
                                                    kT[:, b * KV:(b + 1) * KV], start=False, stop=(i == UP - 1),
                                                    skip_group_check=True)
                        last.then_inc(energy, 1)
                    if now := at(j, s, DEEP - 1, last_pass):
                        jp, u = now
                        pe.wait_ge(prob_ready, jp * UNITS + (u + 1))
                        for i in range(UP):
                            last = nc.tensor.transpose(bank_t[u % 2][:, i * P:(i + 1) * P], prob[:, u % DEEP, i, :], chip.ident[:])
                        last.then_inc(probT_ps, 1)
                    if now := at(j, s, DEEP, last_pass):
                        jp, u = now
                        b, g = u // 2, u % 2
                        if u % HU == 0:
                            pe.wait_ge(v_sb, jp * 4 + (2 * (u // HU) + 2))
                        if u % 2:
                            pe.wait_ge(probT_sb, jp * HU + (u // 2 + 1))
                        else:
                            pe.wait_ge(probT_sa, jp * HU + (u // 2 + 1))
                        if u % 4 == 0:
                            pe.wait_ge(z_ready, jp * TPI + max(u // 4, 1))
                        for i in range(UP):
                            cols = (b % 2) * PAIRS * 2 * VW + (UP * g + i) * 2 * VW
                            h = 2 * (UP * g + i)
                            last = nc.tensor.matmul(bank_o[(b // 2) % 2][:, cols:cols + 2 * VW], probT[:, u % 2, i * P:(i + 1) * P],
                                                    v[:, b, h:h + 2, :].rearrange("p h f -> p (h f)"), start=True, stop=True)
                        if u % 4 == 3:
                            last.then_inc(o_ps, 1)
                    if (now := at(j, s, 0, last_pass)) and now[1] in EXTRA:
                        what, half, c = EXTRA[now[1]]
                        if not (last_pass and half == 2):
                            extra(now[0], what, half, c, last_pass and half == 0)

            passes(pe, slots)
            extra(STEPS, "z", -1, 0, True)
            extra(STEPS, "out", -1, 0)
            pe.wait_ge(x_done, STEPS * 2 + 1)

        @block.scalar
        def _(act):
            def extra(j, what, half, c, bank=bank_s):
                u = half % 2
                if what == "x":
                    act.wait_ge(xT_ps, j * 2 + (half + 1))
                    nc.scalar.activation(xT[:], bank[:], ACT.Identity).then_inc(xT_sb, 1)
                elif what == "k":
                    act.wait_ge(k_ps, j * 4 + (2 * half + c + 1))
                    cols = u * HB * KV + c * HALF
                    nc.scalar.activation(kT[:, cols:cols + HALF], bank[:], ACT.Identity).then_inc(k_sb, 1)
                elif what == "q":
                    act.wait_ge(q_ps, j * 2 + (half + 1))
                    nc.scalar.activation(qT[:], bank[:], ACT.Identity, scale=SCALE).then_inc(q_sb, 1)
                elif what == "v":
                    act.wait_ge(v_ps, j * 4 + (2 * half + c + 1))
                    b = u * HB + 4 * c
                    nc.scalar.activation(v[:, b:b + 4, :, 0:HD].rearrange("p b h f -> p (b h) f"),
                                         bank[:].rearrange("p (a f) -> p a f", f=HD), ACT.Identity).then_inc(v_sb, 1)
                elif what == "z":
                    act.wait_ge(zT_ps, j * 2 + (half + 2))
                    nc.scalar.activation(zT[:], bank[:], ACT.Identity).then_inc(zT_sb, 1)

            act.wait_ge(const, 1)
            for n, (what, c) in enumerate(PREP):
                extra(0, what, 0, c, bk[n])

            def slots(j, which, last_pass):
                for s in which:
                    if now := at(j, s, 0, last_pass):
                        jp, u = now
                        act.wait_ge(negtop_ready, jp * UNITS + (u + 1))
                        for i in range(UP):
                            last = nc.scalar.activation(prob[:, u % DEEP, i, :], bank_e[u % DEEP][:, i * KV:(i + 1) * KV], ACT.Exp,
                                                        bias=negtop[:, u, i:i + 1])
                        last.then_inc(prob_ready, 1)
                    if (now := at(j, s, DEEP - 1, last_pass)) and now[1] % 2 == 0:
                        jp, u = now
                        act.wait_ge(probT_ps, jp * UNITS + (u + 1))
                        nc.scalar.activation(probT[:, 0, :], bank_t[0][:], ACT.Identity).then_inc(probT_sa, 1)
                    if (now := at(j, s, 0, last_pass)) and now[1] in EXTRA:
                        what, half, c = EXTRA[now[1]]
                        if not (last_pass and half == 2):
                            extra(now[0], what, half, c)

            passes(act, slots)
            extra(STEPS, "z", -1, 0)

        def spread_heads(engine, heads, u, done=None):
            for h in heads:
                rows = slice(32 * (h // 4), 32 * (h // 4) + 32)
                to = qd[rows, HB * u:HB * u + HB, h, :]
                of = qT[rows, :].rearrange("p (b q) -> p b q", q=S)
                if engine is nc.gpsimd:
                    last = engine.tensor_tensor(to, of, own[rows, h:h + 1].unsqueeze(2).broadcast_to([32, HB, S]), ALU.mult)
                else:
                    last = engine.tensor_scalar(to, of, own[rows, h:h + 1], None, ALU.mult)
            if done:
                last.then_inc(done, 1)

        POOL_HEADS, DVE_HEADS = range(0, 8), range(8, HEADS)

        @block.gpsimd
        def _(pool):
            nc.gpsimd.memset(v[:, 0:HB], 1.0)
            nc.gpsimd.memset(v[:, HB:BPI], 1.0)
            nc.gpsimd.memset(own[:], 1.0).then_inc(const2, 1)
            pool.wait_ge(const2, 1)
            nc.gpsimd.affine_select(out=own[:], in_=own[:], compare_op=ALU.is_ge, fill=0.0, base=0,
                                    pattern=[[-HD, HEADS]], channel_multiplier=1).then_inc(const2, 1)
            pool.wait_ge(const2, 2)
            nc.gpsimd.affine_select(out=own[:], in_=own[:], compare_op=ALU.is_ge, fill=0.0, base=HD - 1,
                                    pattern=[[HD, HEADS]], channel_multiplier=-1).then_inc(const2, 1)
            pool.wait_ge(const2, 3)
            nc.gpsimd.tensor_copy(ident_b[:], chip.ident[:]).then_inc(const, 1)
            nc.gpsimd.memset(qd[:, HB:BPI], 0.0).then_inc(qd_zero, 1)
            pool.wait_ge(qd_zero, 2)
            pool.wait_ge(q_sb, 1)

            def spread(j, half):
                for n in range(2):
                    spread_heads(nc.gpsimd, POOL_HEADS[4 * n:4 * n + 4], half % 2, qd_pool)
                    pool.wait_ge(qd_pool, j * 4 + (2 * half + n + 1))

            def norm(j):
                norm_rstd(chip, pool, j, mv_ready, Steps(pool, pool_steps, j, 1), rstd_ready)
                pool.wait_ge(rstd_ready, j + 1)

            spread(0, 0)
            with pool.Fori(0, STEPS - 1) as j:
                norm(j)
                for half in (1, 2):
                    pool.wait_ge(q_sb, j * 2 + (half + 1))
                    spread(j, half)
            norm(STEPS - 1)
            pool.wait_ge(q_sb, STEPS * 2)
            spread(STEPS - 1, 1)

        @block.vector
        def _(dve):
            nc.vector.memset(z[:], 0.0).then_inc(z_ready, 1)
            dve.wait_ge(mask_in, 32)
            nc.vector.tensor_scalar(mask_add[:, 0, :], mask_i[:], 0.0, -1e20 * SCALE, ALU.is_equal, ALU.mult).then_inc(mask_ready, 1)
            dve.wait_ge(mask_ready, 1)
            nc.vector.tensor_copy(mask_add[:, 1:UP, :], mask_add[:, 0, :].unsqueeze(1).broadcast_to([P, UP - 1, KV])).then_inc(mask_ready, 1)
            nc.vector.memset(qd[:, 0:HB], 0.0).then_inc(qd_zero, 1)
            dve.wait_ge(qd_zero, 2)
            dve.wait_ge(const, 1)
            dve.wait_ge(q_sb, 1)
            spread_heads(nc.vector, DVE_HEADS, 0, qd_dve)
            spreading = {first + n: (half, h) for half, first in ((1, 5), (2, HU + 5)) for n, h in enumerate(DVE_HEADS)}

            def tile_rows(j, t, steps):
                dve.wait_ge(o_ps, j * TPI + (t + 1))
                o = bank_o[t % 2][:, 0:2 * PAIRS * 2 * VW].rearrange("p (b a v) -> p b a v", b=2, a=PAIRS)
                for h in range(2):
                    rows = slice(64 * h, 64 * h + 64)
                    last = nc.vector.reciprocal(share[rows, t % 2, :, :], o[rows, :, :, h * VW + HD])
                steps.done(last)
                for h in range(2):
                    rows = slice(64 * h, 64 * h + 64)
                    for g in range(2):
                        last = nc.vector.tensor_tensor(
                            z[64 * g:64 * g + 64, t, :, h, :], o[rows, g, :, h * VW:h * VW + HD],
                            share[rows, t % 2, g, :].unsqueeze(2).broadcast_to([64, PAIRS, HD]), ALU.mult)
                last.then_inc(z_ready, 1)

            def add_rows(j, half):
                dve.wait_ge(out_ps, j * 2 + (half + 2))
                rows = chip.x[:, ds((j * TPI + (STEPS * TPI + 4 * half)) % (STEPS * TPI), 4), :]
                nc.vector.tensor_tensor(rows, bank_s[:].rearrange("p (t d) -> p t d", d=D), rows, ALU.add).then_inc(x_done, 1)

            FIRST = DEEP + 1
            PER_PASS = UNITS + TPI + 1

            def slots(j, which, last_pass):
                first = which[0] == 0
                steps = Steps(dve, dve_steps) if first else Steps(dve, dve_steps, j, PER_PASS, FIRST)
                for s in which:
                    if now := at(j, s, 0, last_pass):
                        jp, u = now
                        dve.wait_ge(energy, jp * UNITS + (u + 1))
                        steps.done(nc.vector.tensor_reduce(top[:, u, :], bank_e[u % DEEP][:].rearrange("p (i k) -> p i k", k=KV),
                                                           AX_X, ALU.max))
                        nc.vector.tensor_scalar(negtop[:, u, :], top[:, u, :], -1.0, None, ALU.mult).then_inc(negtop_ready, 1)
                    if (now := at(j, s, DEEP - 1, last_pass)) and now[1] % 2:
                        dve.wait_ge(probT_ps, now[0] * UNITS + (now[1] + 1))
                        nc.vector.tensor_copy(probT[:, 1, :], bank_t[1][:]).then_inc(probT_sb, 1)
                    if now := at(j, s, 0, last_pass):
                        jp, u = now
                        if u in spreading and not (last_pass and spreading[u][0] == 2):
                            half, h = spreading[u]
                            if h == DVE_HEADS[0]:
                                dve.wait_ge(q_sb, jp * 2 + (half + 1))
                            spread_heads(nc.vector, (h,), half % 2, qd_dve if h == DVE_HEADS[-1] else None)
                        if u == 2:
                            norm_stats(chip, steps, (jp + 1) % STEPS, mv_ready)
                        if u == 6:
                            dve.wait_ge(xT_ps, jp * 2 + 2)
                            norm_rows(chip, dve, (jp + 1) % STEPS, jp, rstd_ready, xn_ready)
                        if u == 11:
                            add_rows(jp, -1)
                        if u == HU + 11:
                            add_rows(jp, 0)
                    if (now := at(j, s, DEEP + 1, last_pass)) and now[1] % 4 == 3:
                        tile_rows(now[0], now[1] // 4, steps)
                if not (first or last_pass):
                    steps.close()

            passes(dve, slots)
            add_rows(STEPS, -1)
def stage_ssm(chip, b_out_dram):
    nc = chip.nc
    C = CH // P
    with ExitStack() as ctx:
        def sb(name, shape, dt=F32):
            return ctx.enter_context(nc.sbuf_tensor("e_" + name, shape, dt))

        sem = semaphores(nc, ctx, "e_")

        xi = sb("xi", [P, TPI, D])
        stats = sb("stats", [P, TPI, 6])
        mv = sb("mv", [P, TPI, 2])
        ve = sb("ve", [P, TPI])
        rstd = sb("rstd", [P, TPI])
        xT = sb("xT", [P, 2, HALF])
        xp = sb("xp", [P, 2, C, HALF])
        xc = sb("xc", [P, 2, C, HALF])
        gate = sb("gate", [P, 2, C, HALF])
        xg = sb("xg", [P, 2, C, HALF])
        sd = sb("sd", [P, 2, C, HALF])
        y = sb("y", [P, 2, C, HALF])
        keep = sb("keep", [P, C, HALF])
        fresh = sb("fresh", [P, HALF])
        delta = sb("delta", [P, C])
        ab = sb("ab", [P, C * SN])
        tap_bias = sb("tap_bias", [P, C])
        coef = sb("coef", [P, C])
        bias = sb("bias", [P, 4, D])
        bk = [[ctx.enter_context(nc.psum_tensor(f"e_bk{u}{i}", [P, HALF], F32)) for i in range(4)] for u in range(2)]
        const, delta_a, coef_a, bias_in, keep_ready = sem("const"), sem("delta_a"), sem("coef_a"), sem("bias_in"), sem("keep_s")
        per_stream = lambda name: [sem(f"{name}{u}") for u in range(2)]
        xT_ps, xT_sb, xp_ps, xp_sb, gate_ps, gate_sb, xc_ready, xg_ready, xs_ready = (
            per_stream(n) for n in ("xT_ps", "xT_sb", "xp_ps", "xp_sb", "gate_ps", "gate_sb", "xc_s", "xg_s", "xs_s"))
        d_ps, c_ps, sd_ready, y_ready, out_ps, bank_free = (
            per_stream(n) for n in ("d_ps", "c_ps", "sd_s", "y_s", "out_ps", "bank_free"))
        normed_added, tap_bias_ready = sem("normed_added"), sem("tap_bias_s")
        mv_ready, rstd_ready, xn_ready = sem("mv_s"), sem("rstd_s"), sem("xn_s")
        mv2_ready, rstd2_ready, xi_ready = sem("mv2"), sem("rstd2"), sem("xi_s")
        dve_steps, pool_steps, first_steps = sem("dve"), sem("pool"), sem("first")
        block = ctx.enter_context(nc.Block())
        batches = lambda ap: ap.rearrange("p (b s) -> p b s", s=S)

        def inner_stats(steps):
            for t in range(TPI):
                last = nc.vector.bn_stats(stats[:, t, :], chip.xn[:, t, :])
            steps.done(last)
            nc.vector.tensor_copy(chip.spare[:], stats[:, 0, 0:1])
            for t in range(TPI):
                last = nc.vector.bn_aggr(mv[:, t, :], stats[:, t, :])
            last.then_inc(mv2_ready, 1)

        def inner_rows():
            for t in range(TPI):
                last = nc.vector.tensor_scalar(xi[:, t, :], chip.xn[:, t, :], mv[:, t, 0:1], rstd[:, t:t + 1],
                                               ALU.subtract, ALU.mult)
            last.then_inc(xi_ready, 1)

        def inner_rstd(pool, steps):
            steps.done(nc.gpsimd.tensor_tensor(ve[:], mv[:, :, 1], chip.eps[:], ALU.add))
            nc.gpsimd.tensor_tensor(rstd[:], ve[:], chip.neghalf[:], ALU.pow).then_inc(rstd2_ready, 1)

        taps = lambda c, k: chip.weight("conv_w")[:, c * TAPS + k:c * TAPS + k + 1]

        def passes(eng, first_part, turn):
            first_part(0, 0)
            with eng.Fori(0, STEPS - 1) as j:
                turn(j, 0, j)
                turn(j, 1, j + 1)
            turn(STEPS - 1, 0, STEPS - 1)
            turn(STEPS - 1, 1, None)

        @block.sync
        def _(sp):
            sp.wait_ge(const, 1)
            for t in range(4):
                sp.dma_start(bias[0:1, t, :], b_out_dram).then_inc(bias_in, 16)

        @block.tensor
        def _(pe):
            def tokens_in(j, u):
                pe.wait_ge(xi_ready, j + 1)
                for t in range(4):
                    last = nc.tensor.transpose(bk[u][0][:, t * P:(t + 1) * P], xi[:, 4 * u + t, :], chip.ident[:])
                last.then_inc(xT_ps[u], 1)

            def project(j, u):
                pe.wait_ge(xT_sb[u], j + 1)
                pe.wait_ge(bank_free[u], j + 1)
                for c in range(2 * C):
                    nc.tensor.matmul(bk[u][(1 + c) % 4][:], chip.weight("w_inT")[:, c * P:(c + 1) * P], xT[:, u, :],
                                     start=True, stop=True).then_inc(xp_ps[u] if c < C else gate_ps[u], 1)

            def first_part(j, u):
                tokens_in(j, u)
                project(j, u)

            def turn(j, u, k):
                v = 1 - u
                if k is not None:
                    tokens_in(k, v)
                pe.wait_ge(xs_ready[u], j * 2 + 2)
                pe.wait_ge(gate_sb[u], j * 2 + 2)
                for n, w, done in ((1, "w_dT", d_ps[u]), (0, "w_cT", c_ps[u])):
                    for f in range(C):
                        for i in range(C):
                            last = nc.tensor.matmul(bk[u][(1 + 2 * n + f) % 4][:],
                                                    chip.weight(w)[:, i * CH + f * P:i * CH + (f + 1) * P],
                                                    xc[:, u, i, :], start=(i == 0), stop=(i == C - 1))
                        last.then_inc(done, 1)
                if k is not None:
                    project(k, v)
                pe.wait_ge(y_ready[u], j + 1)
                nc.tensor.matmul(bk[u][1][:], chip.ones[:], bias[:].rearrange("p t d -> p (t d)"),
                                 start=True, stop=False, skip_group_check=True)
                for t in range(4):
                    for c in range(C):
                        last = nc.tensor.matmul(bk[u][1][:, t * D:(t + 1) * D], y[:, u, c, t * P:(t + 1) * P],
                                                chip.weight("w_outT")[:, c * D:(c + 1) * D], start=False,
                                                stop=(t == 3 and c == C - 1), skip_group_check=True)
                last.then_inc(out_ps[u], 1)

            pe.wait_ge(bias_in, 64)
            passes(pe, first_part, turn)

        @block.scalar
        def _(act):
            nc.scalar.activation(delta[:], chip.weight("log_delta"), ACT.Exp).then_inc(delta_a, 1)
            act.wait_ge(delta_a, 1)
            nc.scalar.activation(delta[:], delta[:], ACT.Ln, bias=1.0).then_inc(delta_a, 1)
            act.wait_ge(delta_a, 2)
            nc.scalar.activation(delta[:], delta[:], ACT.Exp, scale=-1.0).then_inc(delta_a, 1)

            def from_projection(u, c):
                nc.scalar.activation(xp[:, u, c, :], bk[u][1 + c][:], ACT.Identity, bias=chip.weight("b_in")[:, c:c + 1])
                nc.scalar.activation(xc[:, u, c, :], bk[u][1 + c][:], ACT.Identity, scale=taps(c, TAPS - 1),
                                     bias=tap_bias[:, c:c + 1]).then_inc(xp_sb[u], 1)

            act.wait_ge(tap_bias_ready, 1)

            def first_part(j, u):
                act.wait_ge(xT_ps[u], j + 1)
                nc.scalar.activation(xT[:, u, :], bk[u][0][:], ACT.Identity, scale=chip.weight("in_g"),
                                     bias=chip.weight("in_b")).then_inc(xT_sb[u], 1)
                for c in range(C):
                    act.wait_ge(xp_ps[u], j * 2 + (c + 1))
                    from_projection(u, c)
                for c in range(C):
                    act.wait_ge(gate_ps[u], j * 2 + (c + 1))
                    nc.scalar.activation(gate[:, u, c, :], bk[u][(3 + c) % 4][:], ACT.Sigmoid,
                                         bias=chip.weight("b_in")[:, C + c:C + c + 1]).then_inc(gate_sb[u], 1)
                squash(j, u)

            def squash(j, u):
                for c in range(C):
                    act.wait_ge(xc_ready[u], j * 2 + (c + 1))
                    nc.scalar.activation(xg[:, u, c, :], xc[:, u, c, :], ACT.Sigmoid).then_inc(xg_ready[u], 1)

            def turn(j, u, k):
                v = 1 - u
                if k is not None:
                    act.wait_ge(xT_ps[v], k + 1)
                    nc.scalar.activation(xT[:, v, :], bk[v][0][:], ACT.Identity, scale=chip.weight("in_g"),
                                         bias=chip.weight("in_b")).then_inc(xT_sb[v], 1)
                for c in range(C):
                    act.wait_ge(d_ps[u], j * 2 + (c + 1))
                    nc.scalar.activation(sd[:, u, c, :], bk[u][(3 + c) % 4][:], ACT.Sigmoid,
                                         bias=chip.weight("b_d")[:, c:c + 1]).then_inc(sd_ready[u], 1)
                if k is not None:
                    for c in range(C):
                        act.wait_ge(xp_ps[v], k * 2 + (c + 1))
                        from_projection(v, c)
                    for c in range(C):
                        act.wait_ge(gate_ps[v], k * 2 + (c + 1))
                        nc.scalar.activation(gate[:, v, c, :], bk[v][(3 + c) % 4][:], ACT.Sigmoid,
                                             bias=chip.weight("b_in")[:, C + c:C + c + 1]).then_inc(gate_sb[v], 1)
                    squash(k, v)

            passes(act, first_part, turn)

        @block.gpsimd
        def _(pool):
            nc.gpsimd.memset(bias[:], 0.0).then_inc(const, 1)
            nc.gpsimd.memset(fresh[:], 1.0).then_inc(pool_steps, 1)
            pool.wait_ge(pool_steps, 1)
            nc.gpsimd.memset(batches(fresh[:])[:, :, 0], 0.0).then_inc(const, 1)
            steps = Steps(pool, pool_steps, base=1)
            pool.wait_ge(mv2_ready, 1)
            inner_rstd(pool, steps)
            norm_rstd(chip, pool, 0, mv_ready, steps, rstd_ready)
            with pool.Fori(0, STEPS - 1) as j:
                steps = Steps(pool, pool_steps, j, 2, base=3)
                pool.wait_ge(mv2_ready, j + 2)
                inner_rstd(pool, steps)
                norm_rstd(chip, pool, j + 1, mv_ready, steps, rstd_ready)

        @block.vector
        def _(dve):
            steps = Steps(dve, first_steps)
            for c in range(C):
                last = nc.vector.scalar_tensor_tensor(tap_bias[:, c:c + 1], chip.weight("b_in")[:, c:c + 1], taps(c, TAPS - 1),
                                                      chip.weight("conv_b")[:, c:c + 1], ALU.mult, ALU.add)
            last.then_inc(tap_bias_ready, 1)
            dve.wait_ge(delta_a, 3)
            dve.wait_ge(const, 2)
            for c in range(C):
                nc.vector.tensor_scalar(keep[:, c, :], fresh[:], delta[:, c:c + 1], None, ALU.mult).then_inc(bank_free[c], 1)
            steps.done(nc.vector.tensor_tensor(ab[:], chip.weight("ssm_A"), chip.weight("ssm_B"), ALU.mult))
            nc.vector.tensor_reduce(coef[:], ab[:].rearrange("p (c n) -> p c n", n=SN), AX_X, ALU.add)
            def convolve(j, u, steps):
                for back in range(1, TAPS):
                    for c in range(C):
                        if back == 1:
                            dve.wait_ge(xp_sb[u], j * 2 + (c + 1))
                        last = nc.vector.scalar_tensor_tensor(
                            batches(xc[:, u, c, :])[:, :, back:], batches(xp[:, u, c, :])[:, :, :S - back],
                            taps(c, TAPS - 1 - back), batches(xc[:, u, c, :])[:, :, back:], ALU.mult, ALU.add)
                        if back == TAPS - 1:
                            last.then_inc(xc_ready[u], 1)
                    if back < TAPS - 1:
                        steps.done(last)

            def swish(j, u):
                for c in range(C):
                    dve.wait_ge(xg_ready[u], j * 2 + (c + 1))
                    nc.vector.tensor_tensor(xc[:, u, c, :], xc[:, u, c, :], xg[:, u, c, :], ALU.mult).then_inc(xs_ready[u], 1)

            def scan(j, u, steps):
                for c in range(C):
                    dve.wait_ge(sd_ready[u], j * 2 + (c + 1))
                    dve.wait_ge(c_ps[u], j * 2 + (c + 1))
                    last = nc.vector.scalar_tensor_tensor(sd[:, u, c, :], bk[u][1 + c][:], chip.weight("b_c")[:, c:c + 1],
                                                          sd[:, u, c, :], ALU.add, ALU.mult)
                steps.done(last)
                for c in range(C):
                    last = nc.vector.tensor_tensor_scan(y[:, u, c, :], keep[:, c, :], sd[:, u, c, :], 0.0, ALU.mult, ALU.add)
                steps.done(last)
                for c in range(C):
                    last = nc.vector.scalar_tensor_tensor(y[:, u, c, :], y[:, u, c, :], coef[:, c:c + 1], gate[:, u, c, :],
                                                          ALU.mult, ALU.mult)
                last.then_inc(y_ready[u], 1)

            def add_normed(k):
                rows = chip.x[:, ds(k * TPI, TPI), :]
                nc.vector.tensor_tensor(rows, chip.xn[:], rows, ALU.add).then_inc(normed_added, 1)

            def add_rows(j, u):
                dve.wait_ge(out_ps[u], j + 1)
                dve.wait_ge(normed_added, j + 1)
                rows = chip.x[:, ds(j * TPI + 4 * u, 4), :]
                nc.vector.tensor_tensor(rows, bk[u][1][:].rearrange("p (t d) -> p t d", d=D), rows, ALU.add).then_inc(bank_free[u], 1)

            def first_part(j, u):
                steps = Steps(dve, first_steps, base=1)
                inner_stats(steps)
                dve.wait_ge(rstd2_ready, 1)
                inner_rows()
                convolve(j, u, steps)
                swish(j, u)
                dve.wait_ge(xi_ready, 1)
                add_normed(0)
                norm_stats(chip, steps, 1, mv_ready)
                norm_rows(chip, dve, 1, 0, rstd_ready, xn_ready)

            def turn(j, u, k):
                last_pass = type(j) is int
                steps = Steps(dve, dve_steps, j, 10, (4 if last_pass else 5) * u)
                if not last_pass and u == 0:
                    dve.wait_ge(xn_ready, j + 1)
                    inner_stats(steps)
                    dve.wait_ge(xT_ps[1], j + 1)
                    dve.wait_ge(rstd2_ready, j + 2)
                    inner_rows()
                elif not last_pass:
                    add_normed(j + 1)
                    dve.wait_ge(bank_free[0], j + 2)
                    dve.wait_ge(bank_free[1], j + 1)
                    norm_stats(chip, steps, (j + 2) % STEPS, mv_ready)
                    norm_rows(chip, dve, (j + 2) % STEPS, j + 1, rstd_ready, xn_ready)
                scan(j, u, steps)
                if k is not None:
                    convolve(k, 1 - u, steps)
                    swish(k, 1 - u)
                add_rows(j, u)

            passes(dve, first_part, turn)

def stage_experts1(chip, router_b_dram, b2_dram):
    nc = chip.nc
    M = I1 // P
    TE = TPI * E1
    BIG = 1e30
    with ExitStack() as ctx:
        def sb(name, shape, dt=F32):
            return ctx.enter_context(nc.sbuf_tensor("f_" + name, shape, dt))

        def bank(name, shape):
            return ctx.enter_context(nc.psum_tensor("f_" + name, shape, F32))

        sem = semaphores(nc, ctx, "f_")

        xi = sb("xi", [P, TPI, D])
        stats = sb("stats", [P, TPI, 6])
        mv = sb("mv", [P, TPI, 2])
        ve = sb("ve", [P, TPI])
        rstd = sb("rstd", [P, TPI])
        xT = sb("xT", [P, N])
        rw = sb("rw", [P, E1])
        rn_b = sb("rn_b", [P, P])
        rb_row = sb("rb_row", [P, E1])
        rb = sb("rb", [P, E1])
        b1 = sb("b1", [P, E1 * M])
        b2 = sb("b2", [P, TPI, D])
        logit = sb("logit", [P, TPI, E1])
        best = sb("best", [P, TPI, 8])
        two = sb("two", [P, TPI, 8])
        left = sb("left", [P, TPI, E1])
        diff = sb("diff", [P, TPI, E1])
        raised = sb("raised", [P, TPI, E1])
        total = sb("total", [P, TPI])
        share = sb("share", [P, TPI])
        comb_w = sb("comb", [P, P])
        comb = comb_w[:, 0:TE].rearrange("p (t e) -> p t e", e=E1)
        combT = sb("combT", [P, P])
        h = sb("h", [P, 2, M, HALF])
        bank_x = [bank(f"x{u}", [P, HALF]) for u in range(2)]
        bank_h = [bank(f"h{m}", [P, HALF]) for m in range(M)]
        bank_y = [bank(f"y{u}", [P, 4, D]) for u in range(2)]
        const, bias_in, rn_ready, bias_ps, w1_ready, two_set = (
            sem(n) for n in ("const", "bias_in", "rn_s", "bias_ps", "w1_s", "two_s"))
        xT_ps, xT_sb, logits, diff_ready, raised_ready, comb_ready, combT_ps, combT_sb, b2_ps, b2_done = (
            sem(n) for n in ("xT_ps", "xT_sb", "logits", "diff_s", "raised_s", "comb_s", "combT_ps", "combT_sb", "b2_ps", "b2_done"))
        h_ps, h_ready, y_ps, x_done = (sem(n) for n in ("h_ps", "h_s", "y_ps", "x_done"))
        mv_ready, rstd_ready, xn_ready = sem("mv_s"), sem("rstd_s"), sem("xn_s")
        mv2_ready, rstd2_ready, xi_ready = sem("mv2"), sem("rstd2"), sem("xi_s")
        dve_steps, pool_steps, first_steps = sem("dve"), sem("pool"), sem("first")
        block = ctx.enter_context(nc.Block())
        units = [(e, u) for e in range(E1) for u in range(2)]
        U = len(units)

        def inner_stats(steps):
            for t in range(TPI):
                last = nc.vector.bn_stats(stats[:, t, :], chip.xn[:, t, :])
            steps.done(last)
            nc.vector.tensor_copy(chip.spare[:], stats[:, 0, 0:1])
            for t in range(TPI):
                last = nc.vector.bn_aggr(mv[:, t, :], stats[:, t, :])
            last.then_inc(mv2_ready, 1)

        def inner_rows():
            for t in range(TPI):
                last = nc.vector.tensor_scalar(xi[:, t, :], chip.xn[:, t, :], mv[:, t, 0:1], rstd[:, t:t + 1],
                                               ALU.subtract, ALU.mult)
            last.then_inc(xi_ready, 1)

        def inner_rstd(pool, steps):
            steps.done(nc.gpsimd.tensor_tensor(ve[:], mv[:, :, 1], chip.eps[:], ALU.add))
            nc.gpsimd.tensor_tensor(rstd[:], ve[:], chip.neghalf[:], ALU.pow).then_inc(rstd2_ready, 1)

        @block.sync
        def _(sp):
            sp.wait_ge(const, 3)
            for t in range(TPI):
                sp.dma_start(b2[E1 * t:E1 * t + E1, t, :], b2_dram).then_inc(bias_in, 16)
            sp.dma_start(rb_row[0:1, :], router_b_dram).then_inc(bias_in, 16)

        @block.tensor
        def _(pe):
            pe.wait_ge(chip.ffn1_in, 32)
            for e in range(E1):
                for m in range(M):
                    nc.tensor.matmul(bank_x[0][:, e * M + m:e * M + m + 1], chip.w1[:, e, m * P:(m + 1) * P],
                                     chip.weight("ln_bT")[:, e:e + 1], start=True, stop=True)
            pe.wait_ge(rn_ready, 1)
            pe.wait_ge(bias_in, 16 * (TPI + 1))
            nc.tensor.matmul(bank_x[1][:, 0:E1], rn_b[:], chip.weight("router1"), start=True, stop=False)
            nc.tensor.matmul(bank_x[1][:, 0:E1], chip.ones[:], rb_row[:], start=False, stop=True).then_inc(bias_ps, 1)
            pe.wait_ge(w1_ready, 1)
            with pe.Fori(0, STEPS) as j:
                pe.wait_ge(xi_ready, j + 1)
                for u in range(2):
                    for t in range(4):
                        last = nc.tensor.transpose(bank_x[u][:, t * P:(t + 1) * P], xi[:, 4 * u + t, :], chip.ident[:])
                    last.then_inc(xT_ps, 1)
                pe.wait_ge(xT_sb, j * 2 + 2)
                for t in range(TPI):
                    last = nc.tensor.matmul(bank_x[0][:, t * E1:(t + 1) * E1], xT[:, t * P:(t + 1) * P], rw[:],
                                            start=True, stop=True)
                last.then_inc(logits, 1)

                def up(k):
                    e, u = units[k]
                    for m in range(M):
                        if k:
                            pe.wait_ge(h_ready, j * (U * M) + ((k - 1) * M + m + 1))
                        nc.tensor.matmul(bank_h[m][:], chip.w1[:, e, m * P:(m + 1) * P], xT[:, u * HALF:(u + 1) * HALF],
                                         start=True, stop=True).then_inc(h_ps, 1)

                def down(k):
                    e, u = units[k]
                    pe.wait_ge(h_ready, j * (U * M) + (k + 1) * M)
                    if k:
                        pe.wait_ge(x_done, j * U + max(k - 1, 1))
                    for t in range(4):
                        for m in range(M):
                            last = nc.tensor.matmul(bank_y[k % 2][:, t, :], h[:, k % 2, m, t * P:(t + 1) * P],
                                                    chip.w2[:, e * M + m, :], start=(m == 0), stop=(m == M - 1))
                    last.then_inc(y_ps, 1)

                up(0)
                for k in range(1, U):
                    up(k)
                    if k == 2:
                        pe.wait_ge(comb_ready, j + 1)
                        nc.tensor.transpose(bank_x[1][:, 0:P], comb_w[:], chip.ident[:]).then_inc(combT_ps, 1)
                    if k == 3:
                        pe.wait_ge(combT_sb, j + 1)
                        for u in range(2):
                            nc.tensor.matmul(bank_x[u][:], combT[:], b2[:, 4 * u:4 * u + 4, :].rearrange("p t d -> p (t d)"),
                                             start=True, stop=True).then_inc(b2_ps, 1)
                    down(k - 1)
                down(U - 1)
                pe.wait_ge(b2_done, j * 2 + 2)
                pe.wait_ge(x_done, j * U + U - 1)

        @block.scalar
        def _(act):
            with act.Fori(0, STEPS) as j:
                for u in range(2):
                    act.wait_ge(xT_ps, j * 2 + u + 1)
                    nc.scalar.activation(xT[:, u * HALF:(u + 1) * HALF], bank_x[u][:], ACT.Identity).then_inc(xT_sb, 1)
                act.wait_ge(diff_ready, j + 1)
                nc.scalar.activation(raised[:], diff[:], ACT.Exp).then_inc(raised_ready, 1)
                for k, (e, u) in enumerate(units):
                    if k == 3:
                        act.wait_ge(combT_ps, j + 1)
                        nc.scalar.activation(combT[:], bank_x[1][:, 0:P], ACT.Identity).then_inc(combT_sb, 1)
                    for m in range(M):
                        act.wait_ge(h_ps, j * (U * M) + (k * M + m + 1))
                        nc.scalar.activation(h[:, k % 2, m, :], bank_h[m][:], ACT.Gelu,
                                             bias=b1[:, e * M + m:e * M + m + 1]).then_inc(h_ready, 1)

        @block.gpsimd
        def _(pool):
            nc.gpsimd.memset(b2[:], 0.0).then_inc(const, 1)
            nc.gpsimd.memset(rb_row[:], 0.0).then_inc(const, 1)
            nc.gpsimd.memset(comb_w[:], 0.0).then_inc(const, 1)
            nc.gpsimd.memset(two[:], BIG).then_inc(two_set, 1)
            steps = Steps(pool, pool_steps)
            pool.wait_ge(mv2_ready, 1)
            inner_rstd(pool, steps)
            with pool.Fori(0, STEPS) as j:
                steps = Steps(pool, pool_steps, j, 2, base=1)
                norm_rstd(chip, pool, j, mv_ready, steps, rstd_ready)
                pool.wait_ge(mv2_ready, j + 2)
                inner_rstd(pool, steps)

        @block.vector
        def _(dve):
            steps = Steps(dve, first_steps)
            inner_stats(steps)
            dve.wait_ge(rstd2_ready, 1)
            inner_rows()
            nc.vector.tensor_scalar(rw[:], chip.weight("router1"), chip.weight("rn_g"), None, ALU.mult)
            nc.vector.tensor_scalar(rn_b[:], chip.ones[:], chip.weight("rn_b"), None, ALU.mult).then_inc(rn_ready, 1)
            dve.wait_ge(bias_ps, 1)
            nc.vector.tensor_tensor(b1[:], bank_x[0][:, 0:E1 * M], chip.weight("b1"), ALU.add)
            nc.vector.tensor_copy(rb[:], bank_x[1][:, 0:E1])
            for e in range(E1):
                last = nc.vector.tensor_scalar(chip.w1[:, e, :], chip.w1[:, e, :], chip.weight("ln_gT")[:, e:e + 1], None, ALU.mult)
            last.then_inc(w1_ready, 1)
            dve.wait_ge(w1_ready, 1)
            dve.wait_ge(two_set, 1)
            dve.wait_ge(const, 3)
            with dve.Fori(0, STEPS) as j:
                steps = Steps(dve, dve_steps, j, 10)
                along = lambda ap: ap.unsqueeze(2).broadcast_to([P, TPI, E1])
                dve.wait_ge(logits, j + 1)
                steps.done(nc.vector.tensor_tensor(logit[:], bank_x[0][:, 0:TE].rearrange("p (t e) -> p t e", e=E1),
                                                   rb[:].unsqueeze(1).broadcast_to([P, TPI, E1]), ALU.add))
                nc.vector.tensor_copy(chip.spare[:], stats[:, 0, 0:1])
                for t in range(TPI):
                    last = nc.vector.max(best[:, t, :], logit[:, t, :])
                steps.done(last)
                nc.vector.tensor_tensor(diff[:], logit[:], along(best[:, :, 0]), ALU.subtract).then_inc(diff_ready, 1)
                steps.done(nc.vector.tensor_copy(two[:, :, 0:2], best[:, :, 0:2]))
                nc.vector.tensor_copy(chip.spare[:], stats[:, 0, 0:1])
                for t in range(TPI):
                    last = nc.vector.match_replace(left[:, t, :], two[:, t, :], logit[:, t, :], -BIG)
                steps.done(last)
                steps.done(nc.vector.tensor_scalar(left[:], left[:], -BIG, None, ALU.is_equal))
                dve.wait_ge(raised_ready, j + 1)
                steps.done(nc.vector.tensor_tensor(left[:], left[:], raised[:], ALU.mult))
                steps.done(nc.vector.tensor_reduce(total[:], left[:], AX_X, ALU.add))
                steps.done(nc.vector.reciprocal(share[:], total[:]))
                nc.vector.tensor_tensor(comb, left[:], along(share[:]), ALU.mult).then_inc(comb_ready, 1)
                dve.wait_ge(comb_ready, j + 1)
                jn = (j + 1) % STEPS
                for k, (e, u) in enumerate(units):
                    if k == 2:
                        dve.wait_ge(x_done, j * U + 2)
                        for v in range(2):
                            dve.wait_ge(b2_ps, j * 2 + v + 1)
                            rows = chip.x[:, ds(j * TPI + 4 * v, 4), :]
                            nc.vector.tensor_tensor(rows, bank_x[v][:].rearrange("p (t d) -> p t d", d=D), rows,
                                                    ALU.add).then_inc(b2_done, 1)
                        dve.wait_ge(b2_done, j * 2 + 2)
                    if k == 3:
                        norm_stats(chip, steps, jn, mv_ready)
                    if k == 4:
                        norm_rows(chip, dve, jn, j, rstd_ready, xn_ready)
                        dve.wait_ge(xn_ready, j + 1)
                        inner_stats(steps)
                    if k == 5:
                        dve.wait_ge(rstd2_ready, j + 2)
                        inner_rows()
                    dve.wait_ge(y_ps, j * U + (k + 1))
                    if k >= 2:
                        dve.wait_ge(x_done, j * U + (k - 1))
                    for t in range(4):
                        row = chip.x[:, ds(j * TPI + 4 * u + t, 1), :]
                        at = (4 * u + t) * E1 + e
                        last = nc.vector.scalar_tensor_tensor(row, bank_y[k % 2][:, t, :], comb_w[:, at:at + 1], row,
                                                              ALU.mult, ALU.add)
                    last.then_inc(x_done, 1)
                steps.close()


def stage_store(chip, out_dram):
    nc = chip.nc
    with ExitStack() as ctx:
        stored = ctx.enter_context(nc.semaphore("st_out"))
        block = ctx.enter_context(nc.Block())

        @block.sync
        def _(sp):
            o = out_dram.rearrange("(t p) d -> p t d", p=P)
            for n in range(STEPS):
                sp.dma_start(o[:, n * TPI:(n + 1) * TPI, :], chip.x[:, n * TPI:(n + 1) * TPI, :]).then_inc(stored, 16)
            sp.wait_ge(stored, 16 * STEPS)


def build(nc, a, stages="ABCDEF"):
    with ExitStack() as ctx:
        chip = Chip(nc, ctx)
        first = lambda sp: fetch_ffn0(chip, sp, a["ffn0_gate"], a["ffn0_up"], a["ffn0_down"])
        second = lambda sp: fetch_ffn1(chip, sp, a["ffn1_w1"], a["ffn1_w2"])
        with ExitStack() as early:
            chip.place_ffn0(early)
            stage_load(chip, a["x"], a["pack"], None if "A" in stages or "C" not in stages else first)
            if "A" in stages:
                stage_cross0(chip, a["ctx"], a["ctxT"], first)
            if "B" in stages:
                stage_recurrence(chip)
            if "C" in stages:
                stage_experts0(chip)
        chip.place_ffn1(ctx)
        if "D" in stages:
            stage_heads(chip, a["ctxT"], a["mask"], second)
        elif "F" in stages:
            with nc.Block() as block:
                block.sync(second)
        if "E" in stages:
            stage_ssm(chip, a["b_out"])
        if "F" in stages:
            stage_experts1(chip, a["router_b"], a["b2"])
        stage_store(chip, a["out"])


def lay_out(v):
    f = lambda name: np.asarray(v[name])
    cols = lambda a: np.ascontiguousarray(a.reshape(-1, P).T)
    wide = lambda a: np.concatenate(list(a), axis=1)
    rows = lambda a: wide(a.reshape(-1, P, a.shape[-1]))

    def heads(a):
        w = np.zeros((D, D), a.dtype)
        for h in range(HEADS):
            w[h * HD:(h + 1) * HD, h * HD:(h + 1) * HD] = a
        return w

    l0, l1, f1 = "L0_attn_", "L1_attn_", "L1_ffn_"
    part = {
        "wqT": f("L0_xattn_Wq").T, "wkT": f("L0_xattn_Wk").T, "bq": cols(f("L0_xattn_bq")), "bk": cols(f("L0_xattn_bk")),
        "wrT": wide(f(l0 + "wr_w").transpose(0, 2, 1)), "wiT": wide(f(l0 + "wi_w").transpose(0, 2, 1)),
        "woT": wide(f(l0 + "wo_w").transpose(0, 2, 1)), "cw": wide(f(l0 + "conv_w")),
        "cb": f(l0 + "conv_b").T, "rb": f(l0 + "wr_b").T, "ib": f(l0 + "wi_b").T, "log_a": f(l0 + "log_a").T,
        "norm_w": f(l0 + "norm_w").T, "norm_out": cols(f(l0 + "norm_out_w")),
        "router0": f("L0_ffn_gate_w").T,
        "q_bd": heads(f("L1_xattn_queries_weight")), "k_bd": heads(f("L1_xattn_keys_weight")),
        "v_bd": heads(f("L1_xattn_values_weight")), "fc": f("L1_xattn_fc_weight"),
        "in_g": cols(f(l1 + "ln_g")), "in_b": cols(f(l1 + "ln_b")), "w_inT": f(l1 + "W_in").T,
        "b_in": cols(f(l1 + "b_in")), "conv_w": rows(f(l1 + "conv_w")[:, 0, :]), "conv_b": cols(f(l1 + "conv_b")),
        "ssm_A": rows(f(l1 + "A")), "ssm_B": rows(f(l1 + "Bm")), "w_cT": rows(f(l1 + "W_c").T),
        "w_dT": rows(f(l1 + "W_d").T), "b_c": cols(f(l1 + "b_c")), "b_d": cols(f(l1 + "b_d")),
        "log_delta": cols(f(l1 + "log_delta")), "w_outT": rows(f(l1 + "W_out").T),
        "rn_g": cols(f(f1 + "rn_g")), "rn_b": cols(f(f1 + "rn_b")), "router1": f(f1 + "router_w").T,
        "ln_gT": f(f1 + "ln_g").T, "ln_bT": f(f1 + "ln_b").T, "b1": cols(f(f1 + "b1")),
            }
    return {
        "x": f("x").reshape(B * S, D),
        "pack": np.concatenate([part[name] for name, _ in PACK], axis=1),
        "ctx": f("ctx_1024").transpose(1, 0, 2).reshape(KV, B * D),
        "ctxT": f("ctx_1024").transpose(2, 0, 1).reshape(D, B * KV),
        "mask": f("mask_1x1xSxS2_ik0").reshape(S, KV),
        "ffn0_gate": f("L0_ffn_w_gate").transpose(2, 0, 1), "ffn0_up": f("L0_ffn_w_up").transpose(2, 0, 1),
        "ffn0_down": f("L0_ffn_w_down").transpose(0, 2, 1).reshape(E0 * I0 // P, P, D).transpose(1, 0, 2),
        "ffn1_w1": f("L1_ffn_w1").transpose(1, 0, 2), "ffn1_w2": f("L1_ffn_w2").reshape(E1 * I1 // P, P, D).transpose(1, 0, 2),
        "b_out": f(l1 + "b_out").reshape(1, D), "router_b": f(f1 + "router_b").reshape(1, E1),
        "b2": f(f1 + "b2"),
    }


def kernel(**inputs):
    import concourse.bacc as bacc
    from concourse.bass_utils import run_bass_kernel_spmd

    nc = bacc.Bacc("TRN2", target_bir_lowering=False, num_devices=1)
    arrays, aps = {}, {}
    for name, a in lay_out(inputs).items():
        a = np.ascontiguousarray(a)
        arrays[name] = a
        aps[name] = nc.dram_tensor(name, a.shape, mybir.dt.from_np(a.dtype), kind="ExternalInput").ap()
    aps["out"] = nc.dram_tensor("out", (B * S, D), F32, kind="ExternalOutput").ap()
    build(nc, aps)
    r = run_bass_kernel_spmd(nc, [arrays], core_ids=[0])
    return np.asarray(r.results[0]["out"]).reshape(B, S, D)
```

```python
from contextlib import ExitStack

import numpy as np

import concourse.bass as bass
from concourse import mybir

F32 = mybir.dt.float32
F32R = mybir.dt.float32r
BF16 = mybir.dt.bfloat16
ALU = mybir.AluOpType
ACT = mybir.ActivationFunctionType
AX_X = mybir.AxisListType.X
ds = bass.ds

P = 128
D = 128
B, S, KV = 64, 64, 128
TILES = B * S // P
TPI = 8
BPI = 2 * TPI
N = TPI * P
STEPS = TILES // TPI
HALF = N // 2
LN_EPS = 1e-5
RMS_EPS = 1e-6
LAYERS, TAPS = 3, 4
E0, CAP, I0 = 8, S // 8 * 2, 512
HEADS, HD = 16, 8
CH, SN = 256, 16
E1, I1 = 8, 512

PACK = [
    ("wqT", D), ("wkT", D), ("bq", 1), ("bk", 1),
    ("wrT", LAYERS * D), ("wiT", LAYERS * D), ("woT", LAYERS * D), ("cw", LAYERS * TAPS), ("cb", LAYERS),
    ("rb", LAYERS), ("ib", LAYERS), ("log_a", LAYERS), ("norm_w", LAYERS), ("norm_out", 1),
    ("router0", E0),
    ("q_bd", D), ("k_bd", D), ("v_bd", D), ("fc", D),
    ("in_g", 1), ("in_b", 1), ("w_inT", 2 * CH), ("b_in", 4), ("conv_w", 2 * TAPS), ("conv_b", 2),
    ("ssm_A", 2 * SN), ("ssm_B", 2 * SN), ("w_cT", 2 * CH), ("w_dT", 2 * CH), ("b_c", 2), ("b_d", 2),
    ("log_delta", 2), ("w_outT", 2 * D),
    ("rn_g", 1), ("rn_b", 1), ("router1", E1), ("ln_gT", E1), ("ln_bT", E1), ("b1", E1 * 4),
]
AT, _at = {}, 0
for _name, _w in PACK:
    AT[_name] = (_at, _at + _w)
    _at += _w
PACKED = _at


def semaphores(nc, ctx, prefix):
    taken = []

    def give_back():
        nc.clear_and_free_semaphores(taken)
        nc.all_engine_barrier()

    ctx.callback(give_back)

    def sem(name):
        taken.append(nc.alloc_semaphore(prefix + name))
        return taken[-1]

    return sem


class Steps:

    def __init__(self, eng, sem, j=0, per=0, base=0):
        self.eng, self.sem, self.j, self.per, self.base, self.k = eng, sem, j, per, base, 0

    def done(self, ins):
        self.k += 1
        ins.then_inc(self.sem, 1)
        self.eng.wait_ge(self.sem, self.j * self.per + (self.base + self.k))

    def close(self):
        assert self.k == self.per, (self.k, self.per)


class Chip:

    def __init__(self, nc, ctx):
        self.nc = nc

        def sb(name, shape, dt=F32):
            return ctx.enter_context(nc.sbuf_tensor("c_" + name, shape, dt))

        self.x = sb("x", [P, TILES, D])
        self.xn = sb("xn", [P, TPI, D])
        self.stats = sb("stats", [P, TPI, 6])
        self.mv = sb("mv", [P, TPI, 2])
        self.ve = sb("ve", [P, TPI])
        self.rstd = sb("rstd", [P, TPI])
        self.spare = sb("spare", [P, 1])
        self.eps = sb("eps", [P, TPI])
        self.neghalf = sb("neghalf", [P, TPI])
        self.w = sb("w", [P, PACKED])
        self.ident = sb("ident", [P, P])
        self.ones = sb("ones", [P, P])
        self.x_in = ctx.enter_context(nc.semaphore("x_in"))
        self.w_in = ctx.enter_context(nc.semaphore("w_in"))
        self.ffn0_in = ctx.enter_context(nc.semaphore("ffn0_in"))
        self.ffn1_in = ctx.enter_context(nc.semaphore("ffn1_in"))

    def place_ffn0(self, ctx):
        sb = lambda name, shape: ctx.enter_context(self.nc.sbuf_tensor("c_" + name, shape, F32))
        self.gate0 = sb("gate0", [P, E0, I0])
        self.up0 = sb("up0", [P, E0, I0])
        self.down0 = sb("down0", [P, E0 * I0 // P, D])

    def place_ffn1(self, ctx):
        sb = lambda name, shape: ctx.enter_context(self.nc.sbuf_tensor("c_" + name, shape, F32))
        self.w1 = sb("w1", [P, E1, I1])
        self.w2 = sb("w2", [P, E1 * I1 // P, D])

    def weight(self, name, rows=P):
        a, b = AT[name]
        return self.w[0:rows, a:b]



def norm_stats(chip, steps, jn, mv_ready):
    nc = chip.nc
    for t in range(TPI):
        last = nc.vector.bn_stats(chip.stats[:, t, :], chip.x[:, ds(jn * TPI + t, 1), :])
    steps.done(last)
    nc.vector.tensor_copy(chip.spare[:], chip.stats[:, 0, 0:1])
    for t in range(TPI):
        last = nc.vector.bn_aggr(chip.mv[:, t, :], chip.stats[:, t, :])
    last.then_inc(mv_ready, 1)


def norm_rstd(chip, pool, j, mv_ready, pool_steps, rstd_ready):
    nc = chip.nc
    pool.wait_ge(mv_ready, j + 1)
    pool_steps.done(nc.gpsimd.tensor_tensor(chip.ve[:], chip.mv[:, :, 1], chip.eps[:], ALU.add))
    nc.gpsimd.tensor_tensor(chip.rstd[:], chip.ve[:], chip.neghalf[:], ALU.pow).then_inc(rstd_ready, 1)


def norm_rows(chip, dve, jn, j, rstd_ready, xn_ready, xn=None):
    nc = chip.nc
    xn = chip.xn if xn is None else xn
    dve.wait_ge(rstd_ready, j + 1)
    for t in range(TPI):
        last = nc.vector.tensor_scalar(xn[:, t, :], chip.x[:, ds(jn * TPI + t, 1), :], chip.mv[:, t, 0:1],
                                       chip.rstd[:, t:t + 1], ALU.subtract, ALU.mult)
    last.then_inc(xn_ready, 1)


def fetch_ffn0(chip, sp, gate, up, down):
    for dst, src in ((chip.gate0, gate), (chip.up0, up), (chip.down0, down)):
        sp.dma_start(dst[:], src).then_inc(chip.ffn0_in, 16)


def fetch_ffn1(chip, sp, w1, w2):
    for dst, src in ((chip.w1, w1), (chip.w2, w2)):
        sp.dma_start(dst[:], src).then_inc(chip.ffn1_in, 16)


def stage_load(chip, x_dram, pack_dram, fetch=None, wait_all=True):
    FIRST_W = AT["bk"][1]
    nc = chip.nc
    with ExitStack() as ctx:
        sem = semaphores(nc, ctx, "")
        x_first, w_first = sem("ld_x0"), sem("ld_w0")
        made, mv_ready, rstd_ready, xn_ready = sem("ld_made"), sem("ld_mv"), sem("ld_rstd"), sem("ld_xn")
        dve_steps, pool_steps = sem("ld_dve"), sem("ld_pool")
        block = ctx.enter_context(nc.Block())

        @block.sync
        def _(sp):
            xr = x_dram.rearrange("(t p) d -> p t d", p=P)
            sp.dma_start(chip.x[:, 0:TPI, :], xr[:, 0:TPI, :]).then_inc(x_first, 16)
            for n in range(1, STEPS):
                sp.dma_start(chip.x[:, n * TPI:(n + 1) * TPI, :], xr[:, n * TPI:(n + 1) * TPI, :]).then_inc(chip.x_in, 16)
            if fetch:
                fetch(sp)
            if wait_all:
                sp.wait_ge(chip.x_in, 16 * (STEPS - 1))

        @block.scalar
        def _(act):
            act.dma_start(chip.w[:, 0:FIRST_W], pack_dram[:, 0:FIRST_W]).then_inc(w_first, 16)
            act.dma_start(chip.w[:, FIRST_W:PACKED], pack_dram[:, FIRST_W:PACKED]).then_inc(chip.w_in, 16)
            act.wait_ge(w_first, 16)
            if wait_all:
                act.wait_ge(chip.w_in, 16)

        @block.gpsimd
        def _(pool):
            nc.gpsimd.memset(chip.neghalf[:], -0.5).then_inc(made, 1)
            nc.gpsimd.memset(chip.ones[:], 1.0).then_inc(made, 1)
            nc.gpsimd.memset(chip.eps[:], LN_EPS).then_inc(made, 1)
            nc.gpsimd.memset(chip.ident[:], 0.0).then_inc(made, 1)
            pool.wait_ge(made, 4)
            nc.gpsimd.affine_select(out=chip.ident[:], in_=chip.ident[:], compare_op=ALU.not_equal, fill=1.0,
                                    base=0, pattern=[[-1, P]], channel_multiplier=1).then_inc(made, 1)
            norm_rstd(chip, pool, 0, mv_ready, Steps(pool, pool_steps), rstd_ready)

        @block.vector
        def _(dve):
            dve.wait_ge(x_first, 16)
            steps = Steps(dve, dve_steps)
            norm_stats(chip, steps, 0, mv_ready)
            norm_rows(chip, dve, 0, 0, rstd_ready, xn_ready)


def stage_cross0(chip, ctx_dram, ctxT_dram, fetch):
    nc = chip.nc
    HB, TPH = BPI // 2, TPI // 2
    SCALE = 1.0 / 32.0
    with ExitStack() as ctx:
        def sb(name, shape, dt=F32):
            return ctx.enter_context(nc.sbuf_tensor("a_" + name, shape, dt))

        def bank(name, shape):
            return ctx.enter_context(nc.psum_tensor("a_" + name, shape, F32))

        sem = semaphores(nc, ctx, "a_")

        ctx_n = sb("ctx_n", [P, 2, HB, D])
        ctx_t = sb("ctx_t", [P, 2, HB * KV])
        xT = sb("xT", [P, HALF])
        qT = sb("qT", [P, 2, HALF])
        kT = sb("kT", [P, 2, HB * KV])
        prob = sb("prob", [P, TPH, KV])
        probT = sb("probT", [P, HALF])
        top = sb("top", [P, TPH])
        negtop = sb("negtop", [P, TPH])
        total = sb("total", [P, 2, TPH])
        share = sb("share", [P, TPH])
        bank_xq = bank("xq", [P, HALF])
        bank_k = [bank(f"k{c}", [P, HALF]) for c in range(2)]
        bank_s = [bank(f"s{u}", [P, TPH, KV]) for u in range(2)]
        bank_p = bank("p", [P, HALF])
        bank_o = [bank(f"o{u}", [P, TPH, D]) for u in range(2)]
        ctxT_in, ctx_in = [sem("ctxT_in0"), sem("ctxT_in1")], [sem("ctx_in0"), sem("ctx_in1")]
        xT_ps, xT_sb, q_ps, q_sb, k_ps = (sem(n) for n in ("xT_ps", "xT_sb", "q_ps", "q_sb", "k_ps"))
        scores, negtop_ready, prob_sb, probT_ps, probT_sb = (
            sem(n) for n in ("scores", "negtop", "prob_sb", "probT_ps", "probT_sb"))
        o_ps, bank_free = sem("o_ps"), sem("bank_free")
        mv_ready, rstd_ready, xn_ready = sem("mv"), sem("rstd"), sem("xn")
        dve_steps, pool_steps = sem("dve"), sem("pool")
        block = ctx.enter_context(nc.Block())

        def passes(eng, head, turn):
            head(0, 0)
            with eng.Fori(0, STEPS - 1) as j:
                turn(j, 0, (j, 1))
                turn(j, 1, (j + 1, 0))
            turn(STEPS - 1, 0, (STEPS - 1, 1))
            turn(STEPS - 1, 1, None)

        @block.sync
        def _(sp):
            def load_t(j, u):
                sp.dma_start(ctx_t[:, u, :], ctxT_dram[:, ds((j * 2 + u) * (HB * KV), HB * KV)]).then_inc(ctxT_in[u], 16)

            def load_n(j, u):
                sp.dma_start(ctx_n[:, u, :, :].rearrange("k b d -> k (b d)"),
                             ctx_dram[:, ds((j * 2 + u) * (HB * D), HB * D)]).then_inc(ctx_in[u], 16)

            for u in range(2):
                load_t(0, u)
                load_n(0, u)
            with sp.Fori(1, STEPS) as j:
                for u in range(2):
                    sp.wait_ge(k_ps, j * 4 + (2 * u - 2))
                    load_t(j, u)
                    sp.wait_ge(o_ps, j * 2 + (u - 1))
                    load_n(j, u)
            for u in range(2):
                sp.wait_ge(ctx_in[u], 16 * STEPS)
            fetch(sp)
            sp.wait_ge(chip.w_in, 16)

        @block.tensor
        def _(pe):
            def transpose_x(j, u):
                for t in range(TPH):
                    last = nc.tensor.transpose(bank_xq[:, t * P:(t + 1) * P], chip.xn[:, TPH * u + t, :], chip.ident[:])
                last.then_inc(xT_ps, 1)

            def project_k(j, u):
                pe.wait_ge(ctxT_in[u], j * 16 + 16)
                for c in range(2):
                    nc.tensor.matmul(bank_k[c][:], chip.weight("wkT"), ctx_t[:, u, c * HALF:(c + 1) * HALF],
                                     start=True, stop=True).then_inc(k_ps, 1)

            def project_q(j, u):
                pe.wait_ge(xT_sb, j * 2 + (u + 1))
                nc.tensor.matmul(bank_xq[:], chip.weight("wqT"), xT[:], start=True, stop=True).then_inc(q_ps, 1)

            def head(j, u):
                transpose_x(j, u)
                project_k(j, u)
                project_q(j, u)

            def turn(j, u, following):
                pe.wait_ge(q_sb, j * 2 + (u + 1))
                for t in range(TPH):
                    for h in range(2):
                        b = 2 * t + h
                        last = nc.tensor.matmul(bank_s[u][64 * h:64 * h + 64, t, :], qT[:, u, b * S:(b + 1) * S],
                                                kT[:, u, b * KV:(b + 1) * KV], start=True, stop=True)
                last.then_inc(scores, 1)
                if following:
                    if u == 1:
                        pe.wait_ge(xn_ready, j + 1)
                    transpose_x(*following)
                    project_k(*following)
                for t in range(TPH):
                    pe.wait_ge(prob_sb, j * TPI + (TPH * u + t + 1))
                    last = nc.tensor.transpose(bank_p[:, t * P:(t + 1) * P], prob[:, t, :], chip.ident[:])
                last.then_inc(probT_ps, 1)
                if following:
                    project_q(*following)
                pe.wait_ge(ctx_in[u], j * 16 + 16)
                pe.wait_ge(probT_sb, j * 2 + (u + 1))
                pe.wait_ge(bank_free, j * 2 + (u + 1))
                for t in range(TPH):
                    for h in range(2):
                        b = 2 * t + h
                        last = nc.tensor.matmul(bank_o[u][64 * h:64 * h + 64, t, :], probT[:, b * S:(b + 1) * S],
                                                ctx_n[:, u, b, :], start=True, stop=True)
                last.then_inc(o_ps, 1)

            passes(pe, head, turn)

        @block.scalar
        def _(act):
            def copy_x(j, u):
                act.wait_ge(xT_ps, j * 2 + (u + 1))
                nc.scalar.activation(xT[:], bank_xq[:], ACT.Identity).then_inc(xT_sb, 1)

            def copy_k(j, u):
                for c in range(2):
                    act.wait_ge(k_ps, j * 4 + (2 * u + c + 1))
                    nc.scalar.activation(kT[:, u, c * HALF:(c + 1) * HALF], bank_k[c][:], ACT.Identity, bias=chip.weight("bk"))

            def copy_q(j, u):
                act.wait_ge(q_ps, j * 2 + (u + 1))
                nc.scalar.activation(qT[:, u, :], bank_xq[:], ACT.Identity, bias=chip.weight("bq")).then_inc(q_sb, 1)

            def head(j, u):
                copy_x(j, u)
                copy_k(j, u)
                copy_q(j, u)

            def turn(j, u, following):
                if following:
                    copy_x(*following)
                act.wait_ge(negtop_ready, j * 2 + (u + 1))
                for t in range(TPH):
                    nc.scalar.activation(prob[:, t, :], bank_s[u][:, t, :], ACT.Exp, scale=SCALE, bias=negtop[:, t:t + 1],
                                         accum_out=total[:, u, t:t + 1]).then_inc(prob_sb, 1)
                if following:
                    copy_k(*following)
                    copy_q(*following)

            passes(act, head, turn)

        @block.gpsimd
        def _(pool):
            with pool.Fori(0, STEPS) as j:
                norm_rstd(chip, pool, j, mv_ready, Steps(pool, pool_steps, j, 1), rstd_ready)

        @block.vector
        def _(dve):
            def head(j, u):
                dve.wait_ge(chip.x_in, 16 * (STEPS - 1))
                nc.vector.memset(chip.spare[:], 0.0).then_inc(bank_free, 1)

            def turn(j, u, following):
                steps = Steps(dve, dve_steps, j, 5, 3 * u)
                jn = (j + 1) % STEPS
                dve.wait_ge(scores, j * 2 + (u + 1))
                steps.done(nc.vector.tensor_reduce(top[:], bank_s[u][:], AX_X, ALU.max))
                nc.vector.tensor_scalar(negtop[:], top[:], -SCALE, None, ALU.mult).then_inc(negtop_ready, 1)
                if u == 0:
                    norm_stats(chip, steps, jn, mv_ready)
                dve.wait_ge(probT_ps, j * 2 + (u + 1))
                nc.vector.tensor_copy(probT[:], bank_p[:]).then_inc(probT_sb, 1)
                steps.done(nc.vector.reciprocal(share[:], total[:, u, :]))
                if u == 0:
                    dve.wait_ge(xT_ps, j * 2 + 2)
                    norm_rows(chip, dve, jn, j, rstd_ready, xn_ready)
                dve.wait_ge(o_ps, j * 2 + (u + 1))
                for t in range(TPH):
                    row = chip.x[:, ds(j * TPI + TPH * u + t, 1), :]
                    last = nc.vector.scalar_tensor_tensor(row, bank_o[u][:, t, :], share[:, t:t + 1], row, ALU.mult, ALU.add)
                last.then_inc(bank_free, 1)

            passes(dve, head, turn)

def stage_recurrence(chip):
    nc = chip.nc
    LOG_A_MIN, LOG_SUM_MIN = float(np.log(1e-7)), -80.0
    STREAMS = 4
    PASSES = TILES * P // (STREAMS * HALF)
    DVE_CONV = (0, 1, 2)
    CHAIN = {"conv": ("PE", 3.5), "xc": ("ACT", 0.6), "gates": ("PE", 2.5), "sigmoid": ("ACT", 1.2),
             "a2": ("ACT", 0.9), "decay": ("DVE", 1.4), "log": ("ACT", 1.1), "growlog": ("DVE", 0.9),
             "grow": ("ACT", 0.8), "h": ("DVE", 2.3), "y": ("PE", 0.9), "square": ("ACT", 0.7), "mean": ("PE", 0.9),
             "rs": ("ACT", 1.1), "norm": ("DVE", 1.0)}
    HOP = 0.372
    SWITCH = 1.3
    WAIT = 0.581
    AHEAD = 0.04

    NORM_AT = (6, 8)

    def order():
        todo = []
        for u in range(STREAMS):
            steps = [("in", 0, "PE", 0.5), ("inT", 0, "ACT", 0.6)]
            for l in range(LAYERS):
                for what, (engine, length) in CHAIN.items():
                    if what == "conv" and u in DVE_CONV:
                        engine, length = "DVE", 2.4
                    if not (what == "xc" and u in DVE_CONV):
                        steps.append((what, l, engine, length))
            steps += [(what, LAYERS, *CHAIN[what]) for what in ("square", "mean", "rs")]
            steps += [("z", 0, "DVE", 0.7), ("zT", 0, "PE", 0.5), ("add", 0, "DVE", 0.7)]
            todo.append(steps)
        at = [0] * STREAMS
        ready = [0.0] * STREAMS
        free = {"PE": 0.0, "ACT": 0.0, "DVE": 0.0}
        table = None
        while any(at[u] < len(todo[u]) for u in range(STREAMS)):
            best = None
            for u in range(STREAMS):
                if at[u] == len(todo[u]):
                    continue
                what, l, engine, length = todo[u][at[u]]
                start = max(ready[u], free[engine])
                needs = "sigmoid" if what == "sigmoid" else "log" if engine == "ACT" and what in ("a2", "log", "grow", "rs") else None
                cost = SWITCH if needs and needs != table else 0.0
                left = sum(step[3] + HOP for step in todo[u][at[u]:])
                key = (start + WAIT * cost - AHEAD * left, u)
                if best is None or key < best[0]:
                    best = key, u, start + cost, needs
            _, u, start, needs = best
            what, l, engine, length = todo[u][at[u]]
            free[engine] = start + length
            ready[u] = start + length + HOP
            table = needs or table
            at[u] += 1
            yield what, l, u

    with ExitStack() as ctx:
        def sb(name, shape, dt=F32):
            return ctx.enter_context(nc.sbuf_tensor("b_" + name, shape, dt))

        def bank(name):
            return [ctx.enter_context(nc.psum_tensor(f"b_{name}{u}", [P, HALF], F32)) for u in range(STREAMS)]

        sem = semaphores(nc, ctx, "b_")
        per_stream = lambda name: [sem(f"{name}{u}") for u in range(STREAMS)]

        def wide(name):
            return sb(name, [P, STREAMS, HALF])

        hT = wide("hT")
        xc = wide("xc")
        r = wide("r")
        g = wide("g")
        run = wide("run")
        a2 = wide("a2")
        grow = wide("grow")
        decay = wide("decay")
        acc = r
        sq = r
        rs = a2
        xn2 = sb("xn2", [P, TPI, D])
        tap = sb("tap", [P, LAYERS * TAPS, P])
        fresh = sb("fresh", [P, HALF])
        rate = sb("rate", [P, LAYERS])
        rate8 = sb("rate8", [P, LAYERS])
        rate16 = sb("rate16", [P, LAYERS])
        rms_eps = sb("rms_eps", [P, 1])
        bank_c, bank_y = bank("c"), bank("y")
        const, taps_ready, rate_e, rate_l, rate_done = (sem(n) for n in ("const", "taps", "rate_e", "rate_l", "rate"))
        (xT_ps, hT_ready, conv_ps, xc_ready, gates_ps, gates_sb, a2_ready, clip_ready, ix_ready, ln_ready, t_ready, e_ready,
         h_ready, y_ps, sq_ready, m_ps, var_ln, rs_ready, z_ready, zT_ps, x_done) = (per_stream(n) for n in (
             "xT_ps", "hT", "conv_ps", "xc", "gates_ps", "gates_sb", "a2_s", "clip", "ix", "ln", "t", "e",
             "h", "y_ps", "sq_s", "m_ps", "var_ln", "rs_s", "z", "zT_ps", "x_done"))
        mv_ready, rstd_ready, xn_ready = sem("mv"), sem("rstd"), sem("xn")
        dve_steps, pool_steps = sem("dve"), sem("pool")
        block = ctx.enter_context(nc.Block())
        batches = lambda ap: ap.rearrange("p (b s) -> p b s", s=S)

        @block.tensor
        def _(pe):
            pe.wait_ge(const, 1)
            pe.wait_ge(taps_ready, 1)
            pe.wait_ge(xn_ready, 1)
            with pe.Fori(0, PASSES) as j:
                for what, l, u in order():
                    w = slice(l * D, (l + 1) * D)
                    if what == "in":
                        rows = (chip.xn, xn2)[u // 2]
                        for t in range(4):
                            last = nc.tensor.transpose(bank_y[u][:, t * P:(t + 1) * P], rows[:, 4 * (u % 2) + t, :], chip.ident[:])
                        last.then_inc(xT_ps[u], 1)
                    elif what == "conv" and u not in DVE_CONV:
                        pe.wait_ge(hT_ready[u], j * 4 + (l + 1))
                        nc.tensor.matmul(bank_c[u][:], tap[:, l * TAPS + TAPS - 1, :], hT[:, u, :], start=True, stop=False,
                                         skip_group_check=True)
                        for back in range(1, TAPS):
                            last = nc.tensor.matmul(batches(bank_c[u][:])[:, :, back:], tap[:, l * TAPS + TAPS - 1 - back, :],
                                                    batches(hT[:, u, :])[:, :, :S - back], start=False, stop=(back == TAPS - 1),
                                                    skip_group_check=True)
                        last.then_inc(conv_ps[u], 1)
                    elif what == "gates":
                        pe.wait_ge(xc_ready[u], j * 3 + (l + 1))
                        nc.tensor.matmul(bank_c[u][:], chip.weight("wrT")[:, w], xc[:, u, :], start=True, stop=True)
                        nc.tensor.matmul(bank_y[u][:], chip.weight("wiT")[:, w], xc[:, u, :],
                                         start=True, stop=True).then_inc(gates_ps[u], 1)
                    elif what == "y":
                        pe.wait_ge(h_ready[u], j * 3 + (l + 1))
                        nc.tensor.matmul(bank_y[u][:], chip.weight("woT")[:, w], acc[:, u, :],
                                         start=True, stop=True).then_inc(y_ps[u], 1)
                    elif what == "mean":
                        pe.wait_ge(sq_ready[u], j * 4 + (l + 1))
                        nc.tensor.matmul(bank_c[u][:], chip.ones[:], sq[:, u, :], start=True, stop=True).then_inc(m_ps[u], 1)
                    elif what == "zT":
                        pe.wait_ge(z_ready[u], j + 1)
                        for t in range(4):
                            last = nc.tensor.transpose(bank_c[u][:, t * P:(t + 1) * P], xc[:, u, t * P:(t + 1) * P], chip.ident[:])
                        last.then_inc(zT_ps[u], 1)
                pe.wait_ge(xn_ready, j * 2 + 3)
                for u in range(STREAMS):
                    pe.wait_ge(x_done[u], j + 1)

        @block.scalar
        def _(act):
            act.wait_ge(const, 1)
            nc.scalar.activation(rate[:], chip.weight("log_a"), ACT.Exp, scale=-1.0).then_inc(rate_e, 1)
            act.wait_ge(rate_e, 1)
            nc.scalar.activation(rate[:], rate[:], ACT.Ln, bias=1.0).then_inc(rate_l, 1)
            act.wait_ge(rate_done, 1)
            with act.Fori(0, PASSES) as j:
                table = None
                for what, l, u in order():
                    if what in ("a2", "log", "grow", "rs") and table != "log":
                        act.preload_act_table_set("natural_log_exp_and_others")
                    table = "sigmoid" if what == "sigmoid" else "log" if what in ("a2", "log", "grow", "rs") else table
                    if what == "inT":
                        act.wait_ge(xT_ps[u], j + 1)
                        nc.scalar.activation(hT[:, u, :], bank_y[u][:], ACT.Identity).then_inc(hT_ready[u], 1)
                    elif what == "xc" and u not in DVE_CONV:
                        act.wait_ge(conv_ps[u], j * 3 + (l + 1))
                        nc.scalar.activation(xc[:, u, :], bank_c[u][:], ACT.Identity,
                                             bias=chip.weight("cb")[:, l:l + 1]).then_inc(xc_ready[u], 1)
                    elif what == "sigmoid":
                        act.wait_ge(gates_ps[u], j * 3 + (l + 1))
                        nc.scalar.activation(r[:, u, :], bank_c[u][:], ACT.Sigmoid, bias=chip.weight("rb")[:, l:l + 1])
                        nc.scalar.activation(g[:, u, :], bank_y[u][:], ACT.Sigmoid,
                                             bias=chip.weight("ib")[:, l:l + 1]).then_inc(gates_sb[u], 1)
                    elif what == "a2":
                        act.wait_ge(gates_sb[u], j * 3 + (l + 1))
                        nc.scalar.activation(a2[:, u, :], r[:, u, :], ACT.Exp, scale=rate16[:, l:l + 1]).then_inc(a2_ready[u], 1)
                    elif what == "log":
                        act.wait_ge(clip_ready[u], j * 3 + (l + 1))
                        nc.scalar.activation(a2[:, u, :], a2[:, u, :], ACT.Ln, scale=-1.0).then_inc(ln_ready[u], 1)
                        nc.scalar.activation(decay[:, u, :], run[:, u, :], ACT.Exp)
                    elif what == "grow":
                        act.wait_ge(t_ready[u], j * 3 + (l + 1))
                        nc.scalar.activation(grow[:, u, :], grow[:, u, :], ACT.Exp).then_inc(e_ready[u], 1)
                    elif what == "square":
                        if l < LAYERS:
                            act.wait_ge(y_ps[u], j * 3 + (l + 1))
                            nc.scalar.activation(sq[:, u, :], bank_y[u][:], ACT.Square).then_inc(sq_ready[u], 1)
                        else:
                            act.wait_ge(hT_ready[u], j * 4 + 4)
                            nc.scalar.activation(sq[:, u, :], hT[:, u, :], ACT.Square).then_inc(sq_ready[u], 1)
                    elif what == "rs":
                        act.wait_ge(m_ps[u], j * 4 + (l + 1))
                        nc.scalar.activation(rs[:, u, :], bank_c[u][:], ACT.Ln, scale=1.0 / D, bias=rms_eps[:]).then_inc(var_ln[u], 1)
                    if what == "rs":
                        act.wait_ge(var_ln[u], j * 4 + (l + 1))
                        nc.scalar.activation(rs[:, u, :], rs[:, u, :], ACT.Exp, scale=-0.5).then_inc(rs_ready[u], 1)

        @block.gpsimd
        def _(pool):
            nc.gpsimd.memset(fresh[:], 1.0).then_inc(pool_steps, 1)
            nc.gpsimd.memset(rms_eps[:], RMS_EPS).then_inc(pool_steps, 1)
            pool.wait_ge(pool_steps, 2)
            nc.gpsimd.memset(batches(fresh[:])[:, :, 0], 0.0).then_inc(const, 1)
            norm_rstd(chip, pool, 0, mv_ready, Steps(pool, pool_steps, base=2), rstd_ready)
            with pool.Fori(0, PASSES) as j:
                steps = Steps(pool, pool_steps, j, 2, 3)
                decays = 0
                for what, l, u in order():
                    if what == "decay":
                        pool.wait_ge(gates_sb[u], j * 3 + (l + 1))
                        nc.gpsimd.tensor_tensor(g[:, u, :], g[:, u, :], xc[:, u, :], ALU.mult).then_inc(ix_ready[u], 1)
                        decays += 1
                        if decays in NORM_AT:
                            norm_rstd(chip, pool, j * 2 + (1 + NORM_AT.index(decays)), mv_ready, steps, rstd_ready)
                steps.close()

        @block.vector
        def _(dve):
            dve.wait_ge(const, 1)
            for k in range(LAYERS * TAPS):
                last = nc.vector.tensor_scalar(tap[:, k, :], chip.ident[:], chip.weight("cw")[:, k:k + 1], None, ALU.mult)
            last.then_inc(taps_ready, 1)
            norm_stats(chip, Steps(dve, dve_steps), 1, mv_ready)
            dve.wait_ge(rate_l, 1)
            nc.vector.tensor_scalar(rate8[:], rate[:], -8.0, None, ALU.mult)
            nc.vector.tensor_scalar(rate16[:], rate[:], -16.0, None, ALU.mult).then_inc(rate_done, 1)
            dve.wait_ge(rate_done, 1)
            norm_rows(chip, dve, 1, 0, rstd_ready, xn_ready, xn2)
            with dve.Fori(0, PASSES) as j:
                decays = 0
                steps = Steps(dve, dve_steps, j, 4 * STREAMS * LAYERS + 2 + len(DVE_CONV) * LAYERS * (TAPS - 1), 1)
                for what, l, u in order():
                    if what == "decay":
                        dve.wait_ge(a2_ready[u], j * 3 + (l + 1))
                        nc.vector.tensor_scalar(a2[:, u, :], a2[:, u, :], 1.0, -1e-6, ALU.subtract, ALU.min)
                        last = nc.vector.tensor_scalar(r[:, u, :], r[:, u, :], rate8[:, l:l + 1], LOG_A_MIN, ALU.mult, ALU.max)
                        steps.done(last)
                        last = nc.vector.tensor_tensor_scan(run[:, u, :], fresh[:], r[:, u, :], 0.0, ALU.mult, ALU.add)
                        steps.done(last)
                        nc.vector.tensor_scalar(run[:, u, :], run[:, u, :], LOG_SUM_MIN, None, ALU.max).then_inc(clip_ready[u], 1)
                        decays += 1
                        for n, when in enumerate(NORM_AT):
                            tiles = ((j + 1) * 2 + n) % STEPS
                            if decays == when:
                                norm_stats(chip, steps, tiles, mv_ready)
                            if decays == when + 1:
                                for v in (2 * n, 2 * n + 1):
                                    dve.wait_ge(xT_ps[v], j + 1)
                                norm_rows(chip, dve, tiles, j * 2 + (1 + n), rstd_ready, xn_ready, (chip.xn, xn2)[n])
                    elif what == "conv" and u in DVE_CONV:
                        dve.wait_ge(hT_ready[u], j * 4 + (l + 1))
                        k = (l + 1) * TAPS - 1
                        last = nc.vector.tensor_scalar(xc[:, u, :], hT[:, u, :], chip.weight("cw")[:, k:k + 1],
                                                       chip.weight("cb")[:, l:l + 1], ALU.mult, ALU.add)
                        for back in range(1, TAPS):
                            steps.done(last)
                            last = nc.vector.scalar_tensor_tensor(
                                batches(xc[:, u, :])[:, :, back:], batches(hT[:, u, :])[:, :, :S - back],
                                chip.weight("cw")[:, k - back:k - back + 1], batches(xc[:, u, :])[:, :, back:], ALU.mult, ALU.add)
                        last.then_inc(xc_ready[u], 1)
                    elif what == "growlog":
                        dve.wait_ge(ln_ready[u], j * 3 + (l + 1))
                        nc.vector.scalar_tensor_tensor(grow[:, u, :], a2[:, u, :], 0.5, run[:, u, :],
                                                       ALU.mult, ALU.subtract).then_inc(t_ready[u], 1)
                    elif what == "h":
                        dve.wait_ge(e_ready[u], j * 3 + (l + 1))
                        dve.wait_ge(ix_ready[u], j * 3 + (l + 1))
                        last = nc.vector.tensor_tensor(grow[:, u, :], grow[:, u, :], g[:, u, :], ALU.mult)
                        steps.done(last)
                        last = nc.vector.tensor_tensor_scan(acc[:, u, :], fresh[:], grow[:, u, :], 0.0, ALU.mult, ALU.add)
                        steps.done(last)
                        nc.vector.tensor_tensor(acc[:, u, :], acc[:, u, :], decay[:, u, :], ALU.mult).then_inc(h_ready[u], 1)
                    elif what == "norm":
                        dve.wait_ge(rs_ready[u], j * 4 + (l + 1))
                        nc.vector.scalar_tensor_tensor(hT[:, u, :], bank_y[u][:], chip.weight("norm_w")[:, l:l + 1],
                                                       rs[:, u, :], ALU.mult, ALU.mult).then_inc(hT_ready[u], 1)
                    elif what == "z":
                        dve.wait_ge(rs_ready[u], j * 4 + (LAYERS + 1))
                        nc.vector.scalar_tensor_tensor(xc[:, u, :], hT[:, u, :], chip.weight("norm_out"),
                                                       rs[:, u, :], ALU.mult, ALU.mult).then_inc(z_ready[u], 1)
                    elif what == "add":
                        dve.wait_ge(zT_ps[u], j + 1)
                        rows = chip.x[:, ds(j * (STREAMS * 4) + 4 * u, 4), :]
                        nc.vector.tensor_tensor(rows, bank_c[u][:].rearrange("p (t d) -> p t d", d=D), rows,
                                                ALU.add).then_inc(x_done[u], 1)
                for u in range(STREAMS):
                    dve.wait_ge(x_done[u], j + 1)
                steps.close()

def stage_experts0(chip):
    nc = chip.nc
    SLOTS = E0 * CAP
    COLS = BPI * CAP
    M = I0 // P
    TE = TPI * E0
    with ExitStack() as ctx:
        def sb(name, shape, dt=F32):
            return ctx.enter_context(nc.sbuf_tensor("c0_" + name, shape, dt))

        def bank(name, shape):
            return ctx.enter_context(nc.psum_tensor("c0_" + name, shape, F32))

        sem = semaphores(nc, ctx, "c0_")

        xT = sb("xT", [P, N])
        top = sb("top", [P, TPI])
        shifted = sb("shifted", [P, TPI, E0])
        raised = sb("raised", [P, TPI, E0])
        total = sb("total", [P, TPI])
        share = sb("share", [P, TPI])
        aff_w = sb("aff", [P, P])
        aff = aff_w[:, 0:TE].rearrange("p (t e) -> p t e", e=E0)
        affT = sb("affT", [TE, P])
        best = sb("best", [TE, 2, 2, 8])
        left1 = sb("left1", [TE, P])
        left2 = sb("left2", [TE, P])
        chosen = sb("chosen", [TE, P])
        count = sb("count", [TE, P])
        key_w = sb("key", [P, P])
        key = key_w[0:TE, :]
        keyT = sb("keyT", [P, TE])
        fresh = sb("fresh", [TE, P])
        slot_i = sb("slot_i", [P, CAP], mybir.dt.int32)
        slot = sb("slot", [P, CAP])
        sel = sb("sel", [P, TE, CAP])
        selg = sb("selg", [P, TE, CAP])
        selT = sb("selT", [P, N])
        xe = sb("xe", [P, E0, BPI, CAP])
        silu = sb("silu", [P, 2, 2 * COLS])
        h = sb("h", [P, 2, 2 * COLS])
        yT = sb("yT", [P, BPI, E0, CAP])
        y = sb("y", [P, BPI, D])
        bank_x = [bank(f"x{u}", [P, HALF]) for u in range(2)]
        bank_g = [bank(f"g{u}", [P, HALF]) for u in range(2)]
        bank_u = [bank(f"u{u}", [P, HALF]) for u in range(2)]
        bank_y = [bank(f"y{u}", [P, HALF]) for u in range(2)]
        spread = [bank_g[0], bank_u[0], bank_g[1], bank_u[1]]
        const, made = sem("const"), sem("made")
        xT_ps, xT_sb, logits, shifted_ready, raised_ready, aff_ready = (
            sem(n) for n in ("xT_ps", "xT_sb", "logits", "shifted_s", "raised_s", "aff_s"))
        affT_ps, key_ready, keyT_ps, sel_ready, selg_ready = (sem(n) for n in ("affT_ps", "key_s", "keyT_ps", "sel_s", "selg_s"))
        xe_ps, xe_sb, gu_ps, silu_ready, h_ready, yT_ps, yT_sb = (
            sem(n) for n in ("xe_ps", "xe_sb", "gu_ps", "silu_s", "h_s", "yT_ps", "yT_sb"))
        selT_ps, selT_sb, y_ps, y_sb, out_ps, x_done = (sem(n) for n in ("selT_ps", "selT_sb", "y_ps", "y_sb", "out_ps", "x_done"))
        mv_ready, rstd_ready, xn_ready = sem("mv"), sem("rstd"), sem("xn")
        dve_steps, pool_steps = sem("dve"), sem("pool")
        block = ctx.enter_context(nc.Block())
        parts = [(e, m) for e in range(E0) for m in range(M // 2)]

        PE_FRONT = {"x": 3, "logits": 4, "aff": 8, "key": 13}
        ACT_FRONT = {"x": 3, "exp": 6}
        DVE_FRONT = {"shift": 5, "share": 7, "top1": 9, "top2": 10, "slots": 11, "sel": 14}

        @block.tensor
        def _(pe):
            def front(k, step):
                if step == "x":
                    for u in range(2):
                        for t in range(4):
                            last = nc.tensor.transpose(bank_x[u][:, t * P:(t + 1) * P], chip.xn[:, 4 * u + t, :], chip.ident[:])
                        last.then_inc(xT_ps, 1)
                elif step == "logits":
                    pe.wait_ge(xT_sb, k * 2 + 2)
                    for t in range(TPI):
                        last = nc.tensor.matmul(bank_x[0][:, t * E0:(t + 1) * E0], xT[:, t * P:(t + 1) * P],
                                                chip.weight("router0"), start=True, stop=True)
                    last.then_inc(logits, 1)
                elif step == "aff":
                    pe.wait_ge(aff_ready, k + 1)
                    nc.tensor.transpose(bank_x[1][:, 0:P], aff_w[:], chip.ident[:]).then_inc(affT_ps, 1)
                elif step == "key":
                    pe.wait_ge(key_ready, k + 1)
                    nc.tensor.transpose(bank_x[0][:, 0:P], key_w[:], chip.ident[:]).then_inc(keyT_ps, 1)

            for step in ("x", "logits", "aff", "key"):
                front(0, step)
            pe.wait_ge(chip.ffn0_in, 16 * 3)
            with pe.Fori(0, STEPS) as j:
                pe.wait_ge(sel_ready, j + 1)
                for q in range(4):
                    for n in range(4):
                        t, half = 4 * (q // 2) + n, slice(64 * (q % 2), 64 * (q % 2) + 64)
                        last = nc.tensor.matmul(spread[q][:, n * SLOTS:(n + 1) * SLOTS], chip.xn[half, t, :],
                                                sel[half, t * E0:(t + 1) * E0, :].rearrange("p e c -> p (e c)"),
                                                start=True, stop=True)
                    last.then_inc(xe_ps, 1)
                pe.wait_ge(selg_ready, j + 1)
                for u in range(2):
                    for t in range(4):
                        n = 4 * u + t
                        last = nc.tensor.transpose(bank_x[u][:, t * P:(t + 1) * P],
                                                   selg[:, n * E0:(n + 1) * E0, :].rearrange("p e c -> p (e c)"), chip.ident[:])
                    last.then_inc(selT_ps, 1)

                def answer(i):
                    e, m = parts[i]
                    pe.wait_ge(h_ready, j * len(parts) + i + 1)
                    if m == 0 and e >= 2:
                        pe.wait_ge(yT_sb, j * E0 + (e - 1))
                    for c in range(2):
                        n = 2 * m + c
                        last = nc.tensor.matmul(bank_y[e % 2][:, 0:COLS], chip.down0[:, e * M + n, :],
                                                h[:, i % 2, c * COLS:(c + 1) * COLS], start=(n == 0), stop=(n == M - 1))
                    if m == M // 2 - 1:
                        last.then_inc(yT_ps, 1)

                for i, (e, m) in enumerate(parts):
                    if i == PE_FRONT["x"]:
                        pe.wait_ge(xn_ready, j + 1)
                        pe.wait_ge(selT_sb, j * 2 + 2)
                    for step, at in PE_FRONT.items():
                        if at == i:
                            front(j + 1, step)
                    pe.wait_ge(xe_sb, j * 4 + 4)
                    if i >= 2:
                        pe.wait_ge(h_ready, j * len(parts) + i - 1)
                    tokens = xe[:, e, :, :].rearrange("p b c -> p (b c)")
                    for w, dst in ((chip.gate0, bank_g[i % 2]), (chip.up0, bank_u[i % 2])):
                        for c in range(2):
                            n = 2 * m + c
                            last = nc.tensor.matmul(dst[:, c * COLS:(c + 1) * COLS], w[:, e, n * P:(n + 1) * P], tokens,
                                                    start=True, stop=True)
                    last.then_inc(gu_ps, 1)
                    if i:
                        answer(i - 1)
                answer(len(parts) - 1)
                pe.wait_ge(yT_sb, j * E0 + E0)
                for q in range(4):
                    for n in range(4):
                        b = 4 * q + n
                        last = nc.tensor.transpose(spread[q][:, n * D:(n + 1) * D],
                                                   yT[:, b, :, :].rearrange("p e c -> p (e c)"), chip.ident[:])
                    last.then_inc(y_ps, 1)
                for u in range(2):
                    pe.wait_ge(y_sb, j * 4 + 2 * u + 2)
                    for t in range(4):
                        for g in range(2):
                            b = 2 * (4 * u + t) + g
                            last = nc.tensor.matmul(bank_y[u][64 * g:64 * g + 64, t * D:(t + 1) * D],
                                                    selT[:, b * S:(b + 1) * S], y[:, b, :], start=True, stop=True)
                    last.then_inc(out_ps, 1)
                pe.wait_ge(x_done, j * 2 + 2)

        @block.scalar
        def _(act):
            def front(k, step):
                if step == "x":
                    for u in range(2):
                        act.wait_ge(xT_ps, k * 2 + (u + 1))
                        nc.scalar.activation(xT[:, u * HALF:(u + 1) * HALF], bank_x[u][:], ACT.Identity).then_inc(xT_sb, 1)
                elif step == "exp":
                    act.wait_ge(shifted_ready, k + 1)
                    nc.scalar.activation(raised[:], shifted[:], ACT.Exp).then_inc(raised_ready, 1)

            for step in ACT_FRONT:
                front(0, step)
            with act.Fori(0, STEPS) as j:
                for q in range(4):
                    act.wait_ge(xe_ps, j * 4 + q + 1)
                    to = xe[:].rearrange("p e (t g) c -> p e t g c", g=2)[:, :, 4 * (q // 2):4 * (q // 2) + 4, q % 2, :]
                    nc.scalar.activation(to.rearrange("p e t c -> p t e c"),
                                         spread[q][:].rearrange("p (t e c) -> p t e c", t=4, e=E0),
                                         ACT.Identity).then_inc(xe_sb, 1)
                for u in range(2):
                    act.wait_ge(selT_ps, j * 2 + u + 1)
                    nc.scalar.activation(selT[:, u * HALF:(u + 1) * HALF], bank_x[u][:], ACT.Identity).then_inc(selT_sb, 1)
                def copy_answers(e):
                    act.wait_ge(yT_ps, j * E0 + e + 1)
                    nc.scalar.activation(yT[:, :, e, :], bank_y[e % 2][:, 0:COLS].rearrange("p (b c) -> p b c", c=CAP),
                                         ACT.Identity).then_inc(yT_sb, 1)

                for i, (e, m) in enumerate(parts):
                    act.wait_ge(gu_ps, j * len(parts) + i + 1)
                    nc.scalar.activation(silu[:, i % 2, :], bank_g[i % 2][:], ACT.Silu).then_inc(silu_ready, 1)
                    if m == 1 and e:
                        copy_answers(e - 1)
                    for step, at in ACT_FRONT.items():
                        if at == i:
                            front(j + 1, step)
                copy_answers(E0 - 1)
                for q in range(0, 4, 2):
                    act.wait_ge(y_ps, j * 4 + q + 1)
                    nc.scalar.activation(y[:, 4 * q:4 * q + 4, :].rearrange("p b d -> p (b d)"), spread[q][:],
                                         ACT.Identity).then_inc(y_sb, 1)
                    act.wait_ge(y_ps, j * 4 + q + 2)
                    nc.scalar.activation(y[:, 4 * q + 4:4 * q + 8, :].rearrange("p b d -> p (b d)"), spread[q + 1][:],
                                         ACT.Identity).then_inc(y_sb, 1)

        @block.gpsimd
        def _(pool):
            nc.gpsimd.iota(slot_i[:], [[1, CAP]], base=1, channel_multiplier=0).then_inc(made, 1)
            nc.gpsimd.memset(fresh[:], 1.0).then_inc(made, 1)
            nc.gpsimd.memset(aff_w[:], 0.0).then_inc(const, 1)
            nc.gpsimd.memset(key_w[:], 0.0).then_inc(const, 1)
            pool.wait_ge(made, 2)
            nc.gpsimd.tensor_copy(slot[:], slot_i[:]).then_inc(const, 1)
            nc.gpsimd.memset(fresh[:].rearrange("p (b s) -> p b s", s=S)[:, :, 0], 0.0).then_inc(const, 1)
            def weigh(k):
                pool.wait_ge(sel_ready, k + 1)
                nc.gpsimd.tensor_tensor(selg[:], sel[:],
                                        aff_w[:, 0:TE].unsqueeze(2).broadcast_to([P, TE, CAP]),
                                        ALU.mult).then_inc(selg_ready, 1)

            weigh(0)
            with pool.Fori(0, STEPS) as j:
                norm_rstd(chip, pool, j, mv_ready, Steps(pool, pool_steps, j, 1), rstd_ready)
                weigh(j + 1)

        @block.vector
        def _(dve):
            dve.wait_ge(const, 4)
            scores = bank_x[0][:, 0:TE].rearrange("p (t e) -> p t e", e=E0)
            along = lambda ap: ap.unsqueeze(2).broadcast_to([P, TPI, E0])

            def largest(steps, rnd, src, left):
                nc.vector.tensor_copy(chip.spare[:], chip.stats[:, 0, 0:1])
                for g in range(2):
                    last = nc.vector.max(best[:, rnd, g, :], src[:, g * S:(g + 1) * S])
                steps.done(last)
                nc.vector.tensor_copy(chip.spare[:], chip.stats[:, 0, 0:1])
                for g in range(2):
                    last = nc.vector.match_replace(left[:, g * S:(g + 1) * S], best[:, rnd, g, :],
                                                   src[:, g * S:(g + 1) * S], -1.0)
                steps.done(last)

            def front(k, step, steps):
                if step == "shift":
                    dve.wait_ge(logits, k + 1)
                    steps.done(nc.vector.tensor_reduce(top[:], scores, AX_X, ALU.max))
                    nc.vector.tensor_tensor(shifted[:], scores, along(top[:]), ALU.subtract).then_inc(shifted_ready, 1)
                elif step == "share":
                    dve.wait_ge(raised_ready, k + 1)
                    steps.done(nc.vector.tensor_reduce(total[:], raised[:], AX_X, ALU.add))
                    steps.done(nc.vector.reciprocal(share[:], total[:]))
                    nc.vector.tensor_tensor(aff, raised[:], along(share[:]), ALU.mult).then_inc(aff_ready, 1)
                elif step == "top1":
                    dve.wait_ge(affT_ps, k + 1)
                    steps.done(nc.vector.tensor_copy(affT[:], bank_x[1][0:TE, 0:P]))
                    largest(steps, 0, affT, left1)
                elif step == "top2":
                    largest(steps, 1, left1, left2)
                elif step == "slots":
                    steps.done(nc.vector.tensor_scalar(chosen[:], left2[:], 0.0, None, ALU.is_lt))
                    steps.done(nc.vector.tensor_tensor_scan(count[:], fresh[:], chosen[:], 0.0, ALU.mult, ALU.add))
                    nc.vector.tensor_tensor(key, count[:], chosen[:], ALU.mult).then_inc(key_ready, 1)
                elif step == "sel":
                    dve.wait_ge(keyT_ps, k + 1)
                    steps.done(nc.vector.tensor_copy(keyT[:], bank_x[0][:, 0:TE]))
                    nc.vector.tensor_tensor(sel[:], keyT[:].unsqueeze(2).broadcast_to([P, TE, CAP]),
                                            slot[:].unsqueeze(1).broadcast_to([P, TE, CAP]), ALU.is_equal).then_inc(sel_ready, 1)

            FRONT_STEPS = 11
            steps = Steps(dve, dve_steps)
            for step in DVE_FRONT:
                front(0, step, steps)
            assert steps.k == FRONT_STEPS
            with dve.Fori(0, STEPS) as j:
                steps = Steps(dve, dve_steps, j, FRONT_STEPS + 1, FRONT_STEPS)
                jn = (j + 1) % STEPS
                norm_stats(chip, steps, jn, mv_ready)
                dve.wait_ge(xe_ps, j * 4 + 4)
                norm_rows(chip, dve, jn, j, rstd_ready, xn_ready)
                for i in range(len(parts)):
                    dve.wait_ge(silu_ready, j * len(parts) + i + 1)
                    nc.vector.tensor_tensor(h[:, i % 2, :], silu[:, i % 2, :], bank_u[i % 2][:], ALU.mult).then_inc(h_ready, 1)
                    for step, at in DVE_FRONT.items():
                        if at == i:
                            front(j + 1, step, steps)
                for u in range(2):
                    dve.wait_ge(out_ps, j * 2 + u + 1)
                    rows = chip.x[:, ds(j * TPI + 4 * u, 4), :]
                    nc.vector.tensor_tensor(rows, bank_y[u][:].rearrange("p (t d) -> p t d", d=D), rows,
                                            ALU.add).then_inc(x_done, 1)
                steps.close()

def stage_heads(chip, ctxT_dram, mask_dram, fetch):
    nc = chip.nc
    PAIRS, UP = HEADS // 2, 4
    UNITS = BPI * PAIRS // UP
    DEEP = 3
    SLOTS = -(-UNITS // DEEP) * DEEP
    HB = BPI // 2
    HU = UNITS // 2
    PREP = [("x", 0), ("k", 0), ("k", 1), ("q", 0), ("v", 0), ("v", 1)]
    EXTRA = {s: (what, 1, c) for s, (what, c) in enumerate(PREP)}
    EXTRA |= {8: ("z", -1, 0), 10: ("out", -1, 0)}
    EXTRA |= {HU + s: (what, 2, c) for s, (what, c) in enumerate(PREP)}
    EXTRA |= {HU + 8: ("z", 0, 0), HU + 10: ("out", 0, 0)}

    def at(j, s, lag, last):
        u = s - lag
        if 0 <= u < UNITS:
            return j, u
        if SLOTS <= u and not last:
            return j + 1, u - SLOTS
        return None

    def passes(eng, body):
        body(0, range(DEEP), False)
        with eng.Fori(0, STEPS - 1) as j:
            body(j, range(DEEP, SLOTS + DEEP), False)
        body(STEPS - 1, range(DEEP, SLOTS + DEEP), True)

    VW = HD + 1
    SCALE = float(1.0 / np.sqrt(D))
    with ExitStack() as ctx:
        def sb(name, shape, dt=F32):
            return ctx.enter_context(nc.sbuf_tensor("d_" + name, shape, dt))

        sem = semaphores(nc, ctx, "d_")

        ctx_t = sb("ctx_t", [P, BPI * KV])
        mask_i = sb("mask_i", [P, KV], mybir.dt.int32)
        mask_add = sb("mask_add", [P, UP, KV], BF16)
        ident_b = sb("ident_b", [P, P], BF16)
        own = sb("own", [P, HEADS])
        xT = sb("xT", [P, HALF])
        qT = sb("qT", [P, HALF])
        qd = sb("qd", [P, BPI, HEADS, S])
        kT = sb("kT", [P, BPI * KV])
        v = sb("v", [P, BPI, HEADS, VW])
        top = sb("top", [P, UNITS, UP])
        negtop = sb("negtop", [P, UNITS, UP])
        prob = sb("prob", [P, DEEP, UP, KV])
        probT = sb("probT", [P, 2, UP * P])
        share = sb("share", [P, 2, 2, PAIRS])
        z = sb("z", [P, TPI, PAIRS, 2, HD])
        zT = sb("zT", [P, HALF])
        bk = [ctx.enter_context(nc.psum_tensor(f"d_bk{i}", [P, HALF], F32)) for i in range(8)]
        bank_t, bank_o, bank_e, bank_s = bk[0:2], bk[2:4], bk[4:7], bk[7]
        const, const2, mask_in, mask_ready, qd_zero = (sem(n) for n in ("const", "const2", "mask_in", "mask", "qd_zero"))
        ctx_in = [sem("ctx_in0"), sem("ctx_in1")]
        xT_ps, xT_sb, k_ps, k_sb, q_ps, q_sb, v_ps, v_sb = (
            sem(n) for n in ("xT_ps", "xT_sb", "k_ps", "k_sb", "q_ps", "q_sb", "v_ps", "v_sb"))
        qd_pool, qd_dve, energy, negtop_ready, prob_ready, probT_ps, probT_sa, probT_sb, o_ps = (
            sem(n) for n in ("qd_pool", "qd_dve", "energy", "negtop_s", "prob_s", "probT_ps", "probT_sa", "probT_sb", "o_ps"))
        z_ready, zT_ps, zT_sb, out_ps, x_done = (sem(n) for n in ("z_s", "zT_ps", "zT_sb", "out_ps", "x_done"))
        mv_ready, rstd_ready, xn_ready = sem("mv"), sem("rstd"), sem("xn")
        dve_steps, pool_steps = sem("dve"), sem("pool")
        block = ctx.enter_context(nc.Block())

        @block.sync
        def _(sp):
            for g in range(2):
                sp.dma_start(mask_i[64 * g:64 * g + 64, :], mask_dram).then_inc(mask_in, 16)
            W = HB * KV
            for u in range(2):
                sp.dma_start(ctx_t[:, u * W:(u + 1) * W], ctxT_dram[:, u * W:(u + 1) * W]).then_inc(ctx_in[u], 16)
            with sp.Fori(0, STEPS - 1) as j:
                for u in range(2):
                    sp.wait_ge(v_ps, j * 4 + (2 * u + 2))
                    sp.dma_start(ctx_t[:, u * W:(u + 1) * W],
                                 ctxT_dram[:, ds(j * 2 * W + (2 + u) * W, W)]).then_inc(ctx_in[u], 16)
            for u in range(2):
                sp.wait_ge(ctx_in[u], 16 * STEPS)
            fetch(sp)

        @block.tensor
        def _(pe):
            def extra(j, what, half, c, last_pass=False, bank=None):
                u, fresh = half % 2, bank is not None
                bank = bank_s if bank is None else bank
                if what == "x":
                    if half == 1 and not (type(j) is int and j == 0):
                        pe.wait_ge(x_done, j * 2)
                    elif half == 2:
                        pe.wait_ge(x_done, j * 2 + 1)
                        pe.wait_ge(xn_ready, j + 1)
                    for t in range(4):
                        last = nc.tensor.transpose(bank[:, t * P:(t + 1) * P], chip.xn[:, 4 * u + t, :], chip.ident[:])
                    last.then_inc(xT_ps, 1)
                elif what == "k":
                    if c == 0:
                        pe.wait_ge(ctx_in[u], j * 16 + 16 * (half // 2 + 1))
                    if not fresh:
                        if c == 0:
                            pe.wait_ge(xT_sb, j * 2 + (half + 1))
                        else:
                            pe.wait_ge(k_sb, j * 4 + (2 * half + 1))
                    cols = u * HB * KV + c * HALF
                    nc.tensor.matmul(bank[:], chip.weight("k_bd"), ctx_t[:, cols:cols + HALF], start=True, stop=True).then_inc(k_ps, 1)
                elif what == "q":
                    if fresh:
                        pe.wait_ge(xT_sb, 1)
                    else:
                        pe.wait_ge(k_sb, j * 4 + (2 * half + 2))
                    nc.tensor.matmul(bank[:], chip.weight("q_bd"), xT[:], start=True, stop=True).then_inc(q_ps, 1)
                elif what == "v":
                    if not fresh:
                        if c == 0:
                            pe.wait_ge(q_sb, j * 2 + (half + 1))
                        else:
                            pe.wait_ge(v_sb, j * 4 + (2 * half + 1))
                    for n in range(4):
                        b = u * HB + 4 * c + n
                        last = nc.tensor.matmul(bank[:, n * D:(n + 1) * D], ctx_t[:, b * KV:(b + 1) * KV],
                                                chip.weight("v_bd"), start=True, stop=True)
                    last.then_inc(v_ps, 1)
                elif what == "z":
                    if last_pass:
                        pe.wait_ge(x_done, j * 2 + (half + 1))
                    else:
                        pe.wait_ge(v_sb, j * 4 + 6 + 2 * half)
                    pe.wait_ge(z_ready, j * TPI + (TPI // 2 * half + 5))
                    for t in range(4):
                        last = nc.tensor.transpose(bank[:, t * P:(t + 1) * P],
                                                   z[:, 4 * u + t, :, :, :].rearrange("p a h f -> p (a h f)"), chip.ident[:])
                    last.then_inc(zT_ps, 1)
                else:
                    pe.wait_ge(zT_sb, j * 2 + (half + 2))
                    for t in range(4):
                        last = nc.tensor.matmul(bank[:, t * D:(t + 1) * D], zT[:, t * P:(t + 1) * P],
                                                chip.weight("fc"), start=True, stop=True)
                    last.then_inc(out_ps, 1)

            pe.wait_ge(const, 1)
            for n, (what, c) in enumerate(PREP):
                extra(0, what, 0, c, bank=bk[n])
            pe.wait_ge(v_sb, 2)
            pe.wait_ge(mask_ready, 2)

            def slots(j, which, last_pass):
                for s in which:
                    if now := at(j, s, 0, last_pass):
                        jp, u = now
                        b, g = u // 2, u % 2
                        if u % HU == 0:
                            half = u // HU
                            pe.wait_ge(k_sb, jp * 4 + (2 * half + 2))
                            pe.wait_ge(qd_pool, jp * 4 + (2 * half + 2))
                            pe.wait_ge(qd_dve, jp * 2 + (half + 1))
                        e = bank_e[u % DEEP]
                        nc.tensor.matmul(e[:], ident_b[:], mask_add[:].rearrange("p i k -> p (i k)"),
                                         start=True, stop=False, skip_group_check=True)
                        for i in range(UP):
                            h = 2 * (UP * g + i)
                            last = nc.tensor.matmul(e[:, i * KV:(i + 1) * KV],
                                                    qd[:, b, h:h + 2, :].rearrange("p h q -> p (h q)"),
                                                    kT[:, b * KV:(b + 1) * KV], start=False, stop=(i == UP - 1),
                                                    skip_group_check=True)
                        last.then_inc(energy, 1)
                    if now := at(j, s, DEEP - 1, last_pass):
                        jp, u = now
                        pe.wait_ge(prob_ready, jp * UNITS + (u + 1))
                        for i in range(UP):
                            last = nc.tensor.transpose(bank_t[u % 2][:, i * P:(i + 1) * P], prob[:, u % DEEP, i, :], chip.ident[:])
                        last.then_inc(probT_ps, 1)
                    if now := at(j, s, DEEP, last_pass):
                        jp, u = now
                        b, g = u // 2, u % 2
                        if u % HU == 0:
                            pe.wait_ge(v_sb, jp * 4 + (2 * (u // HU) + 2))
                        if u % 2:
                            pe.wait_ge(probT_sb, jp * HU + (u // 2 + 1))
                        else:
                            pe.wait_ge(probT_sa, jp * HU + (u // 2 + 1))
                        if u % 4 == 0:
                            pe.wait_ge(z_ready, jp * TPI + max(u // 4, 1))
                        for i in range(UP):
                            cols = (b % 2) * PAIRS * 2 * VW + (UP * g + i) * 2 * VW
                            h = 2 * (UP * g + i)
                            last = nc.tensor.matmul(bank_o[(b // 2) % 2][:, cols:cols + 2 * VW], probT[:, u % 2, i * P:(i + 1) * P],
                                                    v[:, b, h:h + 2, :].rearrange("p h f -> p (h f)"), start=True, stop=True)
                        if u % 4 == 3:
                            last.then_inc(o_ps, 1)
                    if (now := at(j, s, 0, last_pass)) and now[1] in EXTRA:
                        what, half, c = EXTRA[now[1]]
                        if not (last_pass and half == 2):
                            extra(now[0], what, half, c, last_pass and half == 0)

            passes(pe, slots)
            extra(STEPS, "z", -1, 0, True)
            extra(STEPS, "out", -1, 0)
            pe.wait_ge(x_done, STEPS * 2 + 1)

        @block.scalar
        def _(act):
            def extra(j, what, half, c, bank=bank_s):
                u = half % 2
                if what == "x":
                    act.wait_ge(xT_ps, j * 2 + (half + 1))
                    nc.scalar.activation(xT[:], bank[:], ACT.Identity).then_inc(xT_sb, 1)
                elif what == "k":
                    act.wait_ge(k_ps, j * 4 + (2 * half + c + 1))
                    cols = u * HB * KV + c * HALF
                    nc.scalar.activation(kT[:, cols:cols + HALF], bank[:], ACT.Identity).then_inc(k_sb, 1)
                elif what == "q":
                    act.wait_ge(q_ps, j * 2 + (half + 1))
                    nc.scalar.activation(qT[:], bank[:], ACT.Identity, scale=SCALE).then_inc(q_sb, 1)
                elif what == "v":
                    act.wait_ge(v_ps, j * 4 + (2 * half + c + 1))
                    b = u * HB + 4 * c
                    nc.scalar.activation(v[:, b:b + 4, :, 0:HD].rearrange("p b h f -> p (b h) f"),
                                         bank[:].rearrange("p (a f) -> p a f", f=HD), ACT.Identity).then_inc(v_sb, 1)
                elif what == "z":
                    act.wait_ge(zT_ps, j * 2 + (half + 2))
                    nc.scalar.activation(zT[:], bank[:], ACT.Identity).then_inc(zT_sb, 1)

            act.wait_ge(const, 1)
            for n, (what, c) in enumerate(PREP):
                extra(0, what, 0, c, bk[n])

            def slots(j, which, last_pass):
                for s in which:
                    if now := at(j, s, 0, last_pass):
                        jp, u = now
                        act.wait_ge(negtop_ready, jp * UNITS + (u + 1))
                        for i in range(UP):
                            last = nc.scalar.activation(prob[:, u % DEEP, i, :], bank_e[u % DEEP][:, i * KV:(i + 1) * KV], ACT.Exp,
                                                        bias=negtop[:, u, i:i + 1])
                        last.then_inc(prob_ready, 1)
                    if (now := at(j, s, DEEP - 1, last_pass)) and now[1] % 2 == 0:
                        jp, u = now
                        act.wait_ge(probT_ps, jp * UNITS + (u + 1))
                        nc.scalar.activation(probT[:, 0, :], bank_t[0][:], ACT.Identity).then_inc(probT_sa, 1)
                    if (now := at(j, s, 0, last_pass)) and now[1] in EXTRA:
                        what, half, c = EXTRA[now[1]]
                        if not (last_pass and half == 2):
                            extra(now[0], what, half, c)

            passes(act, slots)
            extra(STEPS, "z", -1, 0)

        def spread_heads(engine, heads, u, done=None):
            for h in heads:
                rows = slice(32 * (h // 4), 32 * (h // 4) + 32)
                to = qd[rows, HB * u:HB * u + HB, h, :]
                of = qT[rows, :].rearrange("p (b q) -> p b q", q=S)
                if engine is nc.gpsimd:
                    last = engine.tensor_tensor(to, of, own[rows, h:h + 1].unsqueeze(2).broadcast_to([32, HB, S]), ALU.mult)
                else:
                    last = engine.tensor_scalar(to, of, own[rows, h:h + 1], None, ALU.mult)
            if done:
                last.then_inc(done, 1)

        POOL_HEADS, DVE_HEADS = range(0, 8), range(8, HEADS)

        @block.gpsimd
        def _(pool):
            nc.gpsimd.memset(v[:, 0:HB], 1.0)
            nc.gpsimd.memset(v[:, HB:BPI], 1.0)
            nc.gpsimd.memset(own[:], 1.0).then_inc(const2, 1)
            pool.wait_ge(const2, 1)
            nc.gpsimd.affine_select(out=own[:], in_=own[:], compare_op=ALU.is_ge, fill=0.0, base=0,
                                    pattern=[[-HD, HEADS]], channel_multiplier=1).then_inc(const2, 1)
            pool.wait_ge(const2, 2)
            nc.gpsimd.affine_select(out=own[:], in_=own[:], compare_op=ALU.is_ge, fill=0.0, base=HD - 1,
                                    pattern=[[HD, HEADS]], channel_multiplier=-1).then_inc(const2, 1)
            pool.wait_ge(const2, 3)
            nc.gpsimd.tensor_copy(ident_b[:], chip.ident[:]).then_inc(const, 1)
            nc.gpsimd.memset(qd[:, HB:BPI], 0.0).then_inc(qd_zero, 1)
            pool.wait_ge(qd_zero, 2)
            pool.wait_ge(q_sb, 1)

            def spread(j, half):
                for n in range(2):
                    spread_heads(nc.gpsimd, POOL_HEADS[4 * n:4 * n + 4], half % 2, qd_pool)
                    pool.wait_ge(qd_pool, j * 4 + (2 * half + n + 1))

            def norm(j):
                norm_rstd(chip, pool, j, mv_ready, Steps(pool, pool_steps, j, 1), rstd_ready)
                pool.wait_ge(rstd_ready, j + 1)

            spread(0, 0)
            with pool.Fori(0, STEPS - 1) as j:
                norm(j)
                for half in (1, 2):
                    pool.wait_ge(q_sb, j * 2 + (half + 1))
                    spread(j, half)
            norm(STEPS - 1)
            pool.wait_ge(q_sb, STEPS * 2)
            spread(STEPS - 1, 1)

        @block.vector
        def _(dve):
            nc.vector.memset(z[:], 0.0).then_inc(z_ready, 1)
            dve.wait_ge(mask_in, 32)
            nc.vector.tensor_scalar(mask_add[:, 0, :], mask_i[:], 0.0, -1e20 * SCALE, ALU.is_equal, ALU.mult).then_inc(mask_ready, 1)
            dve.wait_ge(mask_ready, 1)
            nc.vector.tensor_copy(mask_add[:, 1:UP, :], mask_add[:, 0, :].unsqueeze(1).broadcast_to([P, UP - 1, KV])).then_inc(mask_ready, 1)
            nc.vector.memset(qd[:, 0:HB], 0.0).then_inc(qd_zero, 1)
            dve.wait_ge(qd_zero, 2)
            dve.wait_ge(const, 1)
            dve.wait_ge(q_sb, 1)
            spread_heads(nc.vector, DVE_HEADS, 0, qd_dve)
            spreading = {first + n: (half, h) for half, first in ((1, 5), (2, HU + 5)) for n, h in enumerate(DVE_HEADS)}

            def tile_rows(j, t, steps):
                dve.wait_ge(o_ps, j * TPI + (t + 1))
                o = bank_o[t % 2][:, 0:2 * PAIRS * 2 * VW].rearrange("p (b a v) -> p b a v", b=2, a=PAIRS)
                for h in range(2):
                    rows = slice(64 * h, 64 * h + 64)
                    last = nc.vector.reciprocal(share[rows, t % 2, :, :], o[rows, :, :, h * VW + HD])
                steps.done(last)
                for h in range(2):
                    rows = slice(64 * h, 64 * h + 64)
                    for g in range(2):
                        last = nc.vector.tensor_tensor(
                            z[64 * g:64 * g + 64, t, :, h, :], o[rows, g, :, h * VW:h * VW + HD],
                            share[rows, t % 2, g, :].unsqueeze(2).broadcast_to([64, PAIRS, HD]), ALU.mult)
                last.then_inc(z_ready, 1)

            def add_rows(j, half):
                dve.wait_ge(out_ps, j * 2 + (half + 2))
                rows = chip.x[:, ds((j * TPI + (STEPS * TPI + 4 * half)) % (STEPS * TPI), 4), :]
                nc.vector.tensor_tensor(rows, bank_s[:].rearrange("p (t d) -> p t d", d=D), rows, ALU.add).then_inc(x_done, 1)

            FIRST = DEEP + 1
            PER_PASS = UNITS + TPI + 1

            def slots(j, which, last_pass):
                first = which[0] == 0
                steps = Steps(dve, dve_steps) if first else Steps(dve, dve_steps, j, PER_PASS, FIRST)
                for s in which:
                    if now := at(j, s, 0, last_pass):
                        jp, u = now
                        dve.wait_ge(energy, jp * UNITS + (u + 1))
                        steps.done(nc.vector.tensor_reduce(top[:, u, :], bank_e[u % DEEP][:].rearrange("p (i k) -> p i k", k=KV),
                                                           AX_X, ALU.max))
                        nc.vector.tensor_scalar(negtop[:, u, :], top[:, u, :], -1.0, None, ALU.mult).then_inc(negtop_ready, 1)
                    if (now := at(j, s, DEEP - 1, last_pass)) and now[1] % 2:
                        dve.wait_ge(probT_ps, now[0] * UNITS + (now[1] + 1))
                        nc.vector.tensor_copy(probT[:, 1, :], bank_t[1][:]).then_inc(probT_sb, 1)
                    if now := at(j, s, 0, last_pass):
                        jp, u = now
                        if u in spreading and not (last_pass and spreading[u][0] == 2):
                            half, h = spreading[u]
                            if h == DVE_HEADS[0]:
                                dve.wait_ge(q_sb, jp * 2 + (half + 1))
                            spread_heads(nc.vector, (h,), half % 2, qd_dve if h == DVE_HEADS[-1] else None)
                        if u == 2:
                            norm_stats(chip, steps, (jp + 1) % STEPS, mv_ready)
                        if u == 6:
                            dve.wait_ge(xT_ps, jp * 2 + 2)
                            norm_rows(chip, dve, (jp + 1) % STEPS, jp, rstd_ready, xn_ready)
                        if u == 11:
                            add_rows(jp, -1)
                        if u == HU + 11:
                            add_rows(jp, 0)
                    if (now := at(j, s, DEEP + 1, last_pass)) and now[1] % 4 == 3:
                        tile_rows(now[0], now[1] // 4, steps)
                if not (first or last_pass):
                    steps.close()

            passes(dve, slots)
            add_rows(STEPS, -1)
def stage_ssm(chip, b_out_dram):
    nc = chip.nc
    C = CH // P
    with ExitStack() as ctx:
        def sb(name, shape, dt=F32):
            return ctx.enter_context(nc.sbuf_tensor("e_" + name, shape, dt))

        sem = semaphores(nc, ctx, "e_")

        xi = sb("xi", [P, TPI, D])
        stats = sb("stats", [P, TPI, 6])
        mv = sb("mv", [P, TPI, 2])
        ve = sb("ve", [P, TPI])
        rstd = sb("rstd", [P, TPI])
        xT = sb("xT", [P, 2, HALF])
        xp = sb("xp", [P, 2, C, HALF])
        xc = sb("xc", [P, 2, C, HALF])
        gate = sb("gate", [P, 2, C, HALF])
        xg = sb("xg", [P, 2, C, HALF])
        sd = sb("sd", [P, 2, C, HALF])
        y = sb("y", [P, 2, C, HALF])
        keep = sb("keep", [P, C, HALF])
        fresh = sb("fresh", [P, HALF])
        delta = sb("delta", [P, C])
        ab = sb("ab", [P, C * SN])
        tap_bias = sb("tap_bias", [P, C])
        coef = sb("coef", [P, C])
        bias = sb("bias", [P, 4, D])
        bk = [[ctx.enter_context(nc.psum_tensor(f"e_bk{u}{i}", [P, HALF], F32)) for i in range(4)] for u in range(2)]
        const, delta_a, coef_a, bias_in, keep_ready = sem("const"), sem("delta_a"), sem("coef_a"), sem("bias_in"), sem("keep_s")
        per_stream = lambda name: [sem(f"{name}{u}") for u in range(2)]
        xT_ps, xT_sb, xp_ps, xp_sb, gate_ps, gate_sb, xc_ready, xg_ready, xs_ready = (
            per_stream(n) for n in ("xT_ps", "xT_sb", "xp_ps", "xp_sb", "gate_ps", "gate_sb", "xc_s", "xg_s", "xs_s"))
        d_ps, c_ps, sd_ready, y_ready, out_ps, bank_free = (
            per_stream(n) for n in ("d_ps", "c_ps", "sd_s", "y_s", "out_ps", "bank_free"))
        normed_added, tap_bias_ready = sem("normed_added"), sem("tap_bias_s")
        mv_ready, rstd_ready, xn_ready = sem("mv_s"), sem("rstd_s"), sem("xn_s")
        mv2_ready, rstd2_ready, xi_ready = sem("mv2"), sem("rstd2"), sem("xi_s")
        dve_steps, pool_steps, first_steps = sem("dve"), sem("pool"), sem("first")
        block = ctx.enter_context(nc.Block())
        batches = lambda ap: ap.rearrange("p (b s) -> p b s", s=S)

        def inner_stats(steps):
            for t in range(TPI):
                last = nc.vector.bn_stats(stats[:, t, :], chip.xn[:, t, :])
            steps.done(last)
            nc.vector.tensor_copy(chip.spare[:], stats[:, 0, 0:1])
            for t in range(TPI):
                last = nc.vector.bn_aggr(mv[:, t, :], stats[:, t, :])
            last.then_inc(mv2_ready, 1)

        def inner_rows():
            for t in range(TPI):
                last = nc.vector.tensor_scalar(xi[:, t, :], chip.xn[:, t, :], mv[:, t, 0:1], rstd[:, t:t + 1],
                                               ALU.subtract, ALU.mult)
            last.then_inc(xi_ready, 1)

        def inner_rstd(pool, steps):
            steps.done(nc.gpsimd.tensor_tensor(ve[:], mv[:, :, 1], chip.eps[:], ALU.add))
            nc.gpsimd.tensor_tensor(rstd[:], ve[:], chip.neghalf[:], ALU.pow).then_inc(rstd2_ready, 1)

        taps = lambda c, k: chip.weight("conv_w")[:, c * TAPS + k:c * TAPS + k + 1]

        def passes(eng, first_part, turn):
            first_part(0, 0)
            with eng.Fori(0, STEPS - 1) as j:
                turn(j, 0, j)
                turn(j, 1, j + 1)
            turn(STEPS - 1, 0, STEPS - 1)
            turn(STEPS - 1, 1, None)

        @block.sync
        def _(sp):
            sp.wait_ge(const, 1)
            for t in range(4):
                sp.dma_start(bias[0:1, t, :], b_out_dram).then_inc(bias_in, 16)

        @block.tensor
        def _(pe):
            def tokens_in(j, u):
                pe.wait_ge(xi_ready, j + 1)
                for t in range(4):
                    last = nc.tensor.transpose(bk[u][0][:, t * P:(t + 1) * P], xi[:, 4 * u + t, :], chip.ident[:])
                last.then_inc(xT_ps[u], 1)

            def project(j, u):
                pe.wait_ge(xT_sb[u], j + 1)
                pe.wait_ge(bank_free[u], j + 1)
                for c in range(2 * C):
                    nc.tensor.matmul(bk[u][(1 + c) % 4][:], chip.weight("w_inT")[:, c * P:(c + 1) * P], xT[:, u, :],
                                     start=True, stop=True).then_inc(xp_ps[u] if c < C else gate_ps[u], 1)

            def first_part(j, u):
                tokens_in(j, u)
                project(j, u)

            def turn(j, u, k):
                v = 1 - u
                if k is not None:
                    tokens_in(k, v)
                pe.wait_ge(xs_ready[u], j * 2 + 2)
                pe.wait_ge(gate_sb[u], j * 2 + 2)
                for n, w, done in ((1, "w_dT", d_ps[u]), (0, "w_cT", c_ps[u])):
                    for f in range(C):
                        for i in range(C):
                            last = nc.tensor.matmul(bk[u][(1 + 2 * n + f) % 4][:],
                                                    chip.weight(w)[:, i * CH + f * P:i * CH + (f + 1) * P],
                                                    xc[:, u, i, :], start=(i == 0), stop=(i == C - 1))
                        last.then_inc(done, 1)
                if k is not None:
                    project(k, v)
                pe.wait_ge(y_ready[u], j + 1)
                nc.tensor.matmul(bk[u][1][:], chip.ones[:], bias[:].rearrange("p t d -> p (t d)"),
                                 start=True, stop=False, skip_group_check=True)
                for t in range(4):
                    for c in range(C):
                        last = nc.tensor.matmul(bk[u][1][:, t * D:(t + 1) * D], y[:, u, c, t * P:(t + 1) * P],
                                                chip.weight("w_outT")[:, c * D:(c + 1) * D], start=False,
                                                stop=(t == 3 and c == C - 1), skip_group_check=True)
                last.then_inc(out_ps[u], 1)

            pe.wait_ge(bias_in, 64)
            passes(pe, first_part, turn)

        @block.scalar
        def _(act):
            nc.scalar.activation(delta[:], chip.weight("log_delta"), ACT.Exp).then_inc(delta_a, 1)
            act.wait_ge(delta_a, 1)
            nc.scalar.activation(delta[:], delta[:], ACT.Ln, bias=1.0).then_inc(delta_a, 1)
            act.wait_ge(delta_a, 2)
            nc.scalar.activation(delta[:], delta[:], ACT.Exp, scale=-1.0).then_inc(delta_a, 1)

            def from_projection(u, c):
                nc.scalar.activation(xp[:, u, c, :], bk[u][1 + c][:], ACT.Identity, bias=chip.weight("b_in")[:, c:c + 1])
                nc.scalar.activation(xc[:, u, c, :], bk[u][1 + c][:], ACT.Identity, scale=taps(c, TAPS - 1),
                                     bias=tap_bias[:, c:c + 1]).then_inc(xp_sb[u], 1)

            act.wait_ge(tap_bias_ready, 1)

            def first_part(j, u):
                act.wait_ge(xT_ps[u], j + 1)
                nc.scalar.activation(xT[:, u, :], bk[u][0][:], ACT.Identity, scale=chip.weight("in_g"),
                                     bias=chip.weight("in_b")).then_inc(xT_sb[u], 1)
                for c in range(C):
                    act.wait_ge(xp_ps[u], j * 2 + (c + 1))
                    from_projection(u, c)
                for c in range(C):
                    act.wait_ge(gate_ps[u], j * 2 + (c + 1))
                    nc.scalar.activation(gate[:, u, c, :], bk[u][(3 + c) % 4][:], ACT.Sigmoid,
                                         bias=chip.weight("b_in")[:, C + c:C + c + 1]).then_inc(gate_sb[u], 1)
                squash(j, u)

            def squash(j, u):
                for c in range(C):
                    act.wait_ge(xc_ready[u], j * 2 + (c + 1))
                    nc.scalar.activation(xg[:, u, c, :], xc[:, u, c, :], ACT.Sigmoid).then_inc(xg_ready[u], 1)

            def turn(j, u, k):
                v = 1 - u
                if k is not None:
                    act.wait_ge(xT_ps[v], k + 1)
                    nc.scalar.activation(xT[:, v, :], bk[v][0][:], ACT.Identity, scale=chip.weight("in_g"),
                                         bias=chip.weight("in_b")).then_inc(xT_sb[v], 1)
                for c in range(C):
                    act.wait_ge(d_ps[u], j * 2 + (c + 1))
                    nc.scalar.activation(sd[:, u, c, :], bk[u][(3 + c) % 4][:], ACT.Sigmoid,
                                         bias=chip.weight("b_d")[:, c:c + 1]).then_inc(sd_ready[u], 1)
                if k is not None:
                    for c in range(C):
                        act.wait_ge(xp_ps[v], k * 2 + (c + 1))
                        from_projection(v, c)
                    for c in range(C):
                        act.wait_ge(gate_ps[v], k * 2 + (c + 1))
                        nc.scalar.activation(gate[:, v, c, :], bk[v][(3 + c) % 4][:], ACT.Sigmoid,
                                             bias=chip.weight("b_in")[:, C + c:C + c + 1]).then_inc(gate_sb[v], 1)
                    squash(k, v)

            passes(act, first_part, turn)

        @block.gpsimd
        def _(pool):
            nc.gpsimd.memset(bias[:], 0.0).then_inc(const, 1)
            nc.gpsimd.memset(fresh[:], 1.0).then_inc(pool_steps, 1)
            pool.wait_ge(pool_steps, 1)
            nc.gpsimd.memset(batches(fresh[:])[:, :, 0], 0.0).then_inc(const, 1)
            steps = Steps(pool, pool_steps, base=1)
            pool.wait_ge(mv2_ready, 1)
            inner_rstd(pool, steps)
            norm_rstd(chip, pool, 0, mv_ready, steps, rstd_ready)
            with pool.Fori(0, STEPS - 1) as j:
                steps = Steps(pool, pool_steps, j, 2, base=3)
                pool.wait_ge(mv2_ready, j + 2)
                inner_rstd(pool, steps)
                norm_rstd(chip, pool, j + 1, mv_ready, steps, rstd_ready)

        @block.vector
        def _(dve):
            steps = Steps(dve, first_steps)
            for c in range(C):
                last = nc.vector.scalar_tensor_tensor(tap_bias[:, c:c + 1], chip.weight("b_in")[:, c:c + 1], taps(c, TAPS - 1),
                                                      chip.weight("conv_b")[:, c:c + 1], ALU.mult, ALU.add)
            last.then_inc(tap_bias_ready, 1)
            dve.wait_ge(delta_a, 3)
            dve.wait_ge(const, 2)
            for c in range(C):
                nc.vector.tensor_scalar(keep[:, c, :], fresh[:], delta[:, c:c + 1], None, ALU.mult).then_inc(bank_free[c], 1)
            steps.done(nc.vector.tensor_tensor(ab[:], chip.weight("ssm_A"), chip.weight("ssm_B"), ALU.mult))
            nc.vector.tensor_reduce(coef[:], ab[:].rearrange("p (c n) -> p c n", n=SN), AX_X, ALU.add)
            def convolve(j, u, steps):
                for back in range(1, TAPS):
                    for c in range(C):
                        if back == 1:
                            dve.wait_ge(xp_sb[u], j * 2 + (c + 1))
                        last = nc.vector.scalar_tensor_tensor(
                            batches(xc[:, u, c, :])[:, :, back:], batches(xp[:, u, c, :])[:, :, :S - back],
                            taps(c, TAPS - 1 - back), batches(xc[:, u, c, :])[:, :, back:], ALU.mult, ALU.add)
                        if back == TAPS - 1:
                            last.then_inc(xc_ready[u], 1)
                    if back < TAPS - 1:
                        steps.done(last)

            def swish(j, u):
                for c in range(C):
                    dve.wait_ge(xg_ready[u], j * 2 + (c + 1))
                    nc.vector.tensor_tensor(xc[:, u, c, :], xc[:, u, c, :], xg[:, u, c, :], ALU.mult).then_inc(xs_ready[u], 1)

            def scan(j, u, steps):
                for c in range(C):
                    dve.wait_ge(sd_ready[u], j * 2 + (c + 1))
                    dve.wait_ge(c_ps[u], j * 2 + (c + 1))
                    last = nc.vector.scalar_tensor_tensor(sd[:, u, c, :], bk[u][1 + c][:], chip.weight("b_c")[:, c:c + 1],
                                                          sd[:, u, c, :], ALU.add, ALU.mult)
                steps.done(last)
                for c in range(C):
                    last = nc.vector.tensor_tensor_scan(y[:, u, c, :], keep[:, c, :], sd[:, u, c, :], 0.0, ALU.mult, ALU.add)
                steps.done(last)
                for c in range(C):
                    last = nc.vector.scalar_tensor_tensor(y[:, u, c, :], y[:, u, c, :], coef[:, c:c + 1], gate[:, u, c, :],
                                                          ALU.mult, ALU.mult)
                last.then_inc(y_ready[u], 1)

            def add_normed(k):
                rows = chip.x[:, ds(k * TPI, TPI), :]
                nc.vector.tensor_tensor(rows, chip.xn[:], rows, ALU.add).then_inc(normed_added, 1)

            def add_rows(j, u):
                dve.wait_ge(out_ps[u], j + 1)
                dve.wait_ge(normed_added, j + 1)
                rows = chip.x[:, ds(j * TPI + 4 * u, 4), :]
                nc.vector.tensor_tensor(rows, bk[u][1][:].rearrange("p (t d) -> p t d", d=D), rows, ALU.add).then_inc(bank_free[u], 1)

            def first_part(j, u):
                steps = Steps(dve, first_steps, base=1)
                inner_stats(steps)
                dve.wait_ge(rstd2_ready, 1)
                inner_rows()
                convolve(j, u, steps)
                swish(j, u)
                dve.wait_ge(xi_ready, 1)
                add_normed(0)
                norm_stats(chip, steps, 1, mv_ready)
                norm_rows(chip, dve, 1, 0, rstd_ready, xn_ready)

            def turn(j, u, k):
                last_pass = type(j) is int
                steps = Steps(dve, dve_steps, j, 10, (4 if last_pass else 5) * u)
                if not last_pass and u == 0:
                    dve.wait_ge(xn_ready, j + 1)
                    inner_stats(steps)
                    dve.wait_ge(xT_ps[1], j + 1)
                    dve.wait_ge(rstd2_ready, j + 2)
                    inner_rows()
                elif not last_pass:
                    add_normed(j + 1)
                    dve.wait_ge(bank_free[0], j + 2)
                    dve.wait_ge(bank_free[1], j + 1)
                    norm_stats(chip, steps, (j + 2) % STEPS, mv_ready)
                    norm_rows(chip, dve, (j + 2) % STEPS, j + 1, rstd_ready, xn_ready)
                scan(j, u, steps)
                if k is not None:
                    convolve(k, 1 - u, steps)
                    swish(k, 1 - u)
                add_rows(j, u)

            passes(dve, first_part, turn)

def stage_experts1(chip, router_b_dram, b2_dram):
    nc = chip.nc
    M = I1 // P
    TPH = TPI // 2
    TE = TPH * E1
    BIG = 1e30
    with ExitStack() as ctx:
        def sb(name, shape, dt=F32):
            return ctx.enter_context(nc.sbuf_tensor("f_" + name, shape, dt))

        def bank(name, shape):
            return ctx.enter_context(nc.psum_tensor("f_" + name, shape, F32))

        sem = semaphores(nc, ctx, "f_")

        xi = sb("xi", [P, TPI, D])
        stats = sb("stats", [P, TPI, 6])
        mv = sb("mv", [P, TPI, 2])
        ve = sb("ve", [P, TPI])
        rstd = sb("rstd", [P, TPI])
        xT = sb("xT", [P, HALF])
        xT_hi = sb("xT_hi", [P, 2, HALF], F32R)
        xT_lo = sb("xT_lo", [P, 2, HALF], F32R)
        w1_hi = sb("w1_hi", [P, E1, I1], F32R)
        w1_lo = sb("w1_lo", [P, E1, I1], F32R)
        rw = sb("rw", [P, E1])
        rn_b = sb("rn_b", [P, P])
        rb_row = sb("rb_row", [P, E1])
        rb = sb("rb", [P, E1])
        b1 = sb("b1", [P, E1 * M])
        b2 = sb("b2", [P, TPH, D])
        logit = sb("logit", [P, TPH, E1])
        best = sb("best", [P, TPH, 8])
        two = sb("two", [P, TPH, 8])
        left = sb("left", [P, TPH, E1])
        diff = sb("diff", [P, TPH, E1])
        raised = sb("raised", [P, TPH, E1])
        total = sb("total", [P, TPH])
        share = sb("share", [P, TPH])
        comb_w = sb("comb", [P, 2, P])
        combT = sb("combT", [P, P])
        h = sb("h", [P, 2, M, HALF])
        bank_x, bank_r = bank("x", [P, HALF]), bank("r", [P, HALF])
        bank_h = [bank(f"h{m}", [P, HALF]) for m in range(M)]
        bank_y = [bank(f"y{u}", [P, 4, D]) for u in range(2)]
        const, bias_in, rn_ready, bias_ps, w1_ready, two_set = (
            sem(n) for n in ("const", "bias_in", "rn_s", "bias_ps", "w1_s", "two_s"))
        xT_high, xT_split, w1_scaled, w1_high = (sem(n) for n in ("xT_high", "xT_split", "w1_scaled", "w1_high"))
        b1_ps = sem("b1_ps")
        bias_done, b1_ready = sem("bias_done"), sem("b1_s")
        xT_ps, xT_sb, logits, diff_ready, raised_ready, comb_ready, combT_ps, combT_sb, b2_ps, b2_done = (
            sem(n) for n in ("xT_ps", "xT_sb", "logits", "diff_s", "raised_s", "comb_s", "combT_ps", "combT_sb", "b2_ps", "b2_done"))
        h_ps, h_ready, y_ps, x_done = (sem(n) for n in ("h_ps", "h_s", "y_ps", "x_done"))
        mv_ready, rstd_ready, xn_ready = sem("mv_s"), sem("rstd_s"), sem("xn_s")
        mv2_ready, rstd2_ready, xi_ready = sem("mv2"), sem("rstd2"), sem("xi_s")
        dve_steps, pool_steps, first_steps = sem("dve"), sem("pool"), sem("first")
        block = ctx.enter_context(nc.Block())
        units = [(e, u) for u in range(2) for e in range(E1)]
        U = len(units)

        def inner_stats(steps):
            for t in range(TPI):
                last = nc.vector.bn_stats(stats[:, t, :], chip.xn[:, t, :])
            steps.done(last)
            nc.vector.tensor_copy(chip.spare[:], stats[:, 0, 0:1])
            for t in range(TPI):
                last = nc.vector.bn_aggr(mv[:, t, :], stats[:, t, :])
            last.then_inc(mv2_ready, 1)

        def inner_rows():
            for t in range(TPI):
                last = nc.vector.tensor_scalar(xi[:, t, :], chip.xn[:, t, :], mv[:, t, 0:1], rstd[:, t:t + 1],
                                               ALU.subtract, ALU.mult)
            last.then_inc(xi_ready, 1)

        def inner_rstd(pool, steps):
            steps.done(nc.gpsimd.tensor_tensor(ve[:], mv[:, :, 1], chip.eps[:], ALU.add))
            nc.gpsimd.tensor_tensor(rstd[:], ve[:], chip.neghalf[:], ALU.pow).then_inc(rstd2_ready, 1)

        @block.sync
        def _(sp):
            sp.wait_ge(const, 3)
            for t in range(TPH):
                sp.dma_start(b2[E1 * t:E1 * t + E1, t, :], b2_dram).then_inc(bias_in, 16)
            sp.dma_start(rb_row[0:1, :], router_b_dram).then_inc(bias_in, 16)

        PE_FRONT = {"x": 3, "logits": 5}
        ACT_FRONT = {"x": 3, "exp": 6}
        DVE_FRONT = {"split": 3, "best": 5, "share": 7}

        @block.tensor
        def _(pe):
            def front(n, u, step):
                if step == "x":
                    for t in range(TPH):
                        last = nc.tensor.transpose(bank_x[:, t * P:(t + 1) * P], xi[:, TPH * u + t, :], chip.ident[:])
                    last.then_inc(xT_ps, 1)
                elif step == "logits":
                    pe.wait_ge(xT_sb, n + 1)
                    for t in range(TPH):
                        last = nc.tensor.matmul(bank_r[:, t * E1:(t + 1) * E1], xT[:, t * P:(t + 1) * P], rw[:],
                                                start=True, stop=True)
                    last.then_inc(logits, 1)

            pe.wait_ge(chip.ffn1_in, 32)
            bank_b1 = bank_y[0][:].rearrange("p t d -> p (t d)")
            for e in range(E1):
                for m in range(M):
                    last = nc.tensor.matmul(bank_b1[:, e * M + m:e * M + m + 1], chip.w1[:, e, m * P:(m + 1) * P],
                                            chip.weight("ln_bT")[:, e:e + 1], start=True, stop=True)
                last.then_inc(b1_ps, 1)
            pe.wait_ge(rn_ready, 1)
            pe.wait_ge(bias_in, 16 * (TPH + 1))
            nc.tensor.matmul(bank_y[1][:, 0, 0:E1], rn_b[:], chip.weight("router1"), start=True, stop=False)
            nc.tensor.matmul(bank_y[1][:, 0, 0:E1], chip.ones[:], rb_row[:], start=False, stop=True).then_inc(bias_ps, 1)
            pe.wait_ge(xi_ready, 1)
            front(0, 0, "x")
            front(0, 0, "logits")
            pe.wait_ge(bias_done, 1)
            pe.wait_ge(b1_ready, 1)
            with pe.Fori(0, STEPS) as j:
                def up(k):
                    e, u = units[k]
                    if e == 0:
                        pe.wait_ge(xT_split, j * 2 + (u + 1))
                    if u == 0:
                        pe.wait_ge(w1_ready, e + 1)
                    for m in range(M):
                        if k:
                            pe.wait_ge(h_ready, j * (U * M) + ((k - 1) * M + m + 1))
                        inner = slice(m * P, (m + 1) * P)
                        nc.tensor.matmul(bank_h[m][:], w1_hi[:, e, inner], xT_hi[:, u, :], start=True, stop=False)
                        nc.tensor.matmul(bank_h[m][:], w1_hi[:, e, inner], xT_lo[:, u, :], start=False, stop=False)
                        nc.tensor.matmul(bank_h[m][:], w1_lo[:, e, inner], xT_hi[:, u, :],
                                         start=False, stop=True).then_inc(h_ps, 1)

                def down(k):
                    e, u = units[k]
                    pe.wait_ge(h_ready, j * (U * M) + (k + 1) * M)
                    if k:
                        pe.wait_ge(x_done, j * U + k)
                    for t in range(TPH):
                        for m in range(M):
                            last = nc.tensor.matmul(bank_y[k % 2][:, t, :], h[:, k % 2, m, t * P:(t + 1) * P],
                                                    chip.w2[:, e * M + m, :], start=(m == 0), stop=(m == M - 1))
                    last.then_inc(y_ps, 1)

                up(0)
                for k in range(U):
                    e, u = units[k]
                    if k + 1 < U:
                        up(k + 1)
                    if e == 0:
                        pe.wait_ge(comb_ready, j * 2 + (u + 1))
                        nc.tensor.transpose(bank_r[:, 0:P], comb_w[:, u, :], chip.ident[:]).then_inc(combT_ps, 1)
                    if e == 1:
                        pe.wait_ge(combT_sb, j * 2 + (u + 1))
                        nc.tensor.matmul(bank_x[:], combT[:], b2[:].rearrange("p t d -> p (t d)"),
                                         start=True, stop=True).then_inc(b2_ps, 1)
                    if e == PE_FRONT["x"]:
                        pe.wait_ge(b2_done, j * 2 + (u + 1))
                        pe.wait_ge(xi_ready, j + (u + 1))
                    for step, at in PE_FRONT.items():
                        if at == e:
                            front(j * 2 + (u + 1), 1 - u, step)
                    down(k)
                pe.wait_ge(x_done, j * U + U)

        @block.scalar
        def _(act):
            def front(n, u, step):
                if step == "x":
                    act.wait_ge(xT_ps, n + 1)
                    nc.scalar.activation(xT[:], bank_x[:], ACT.Identity).then_inc(xT_sb, 1)
                    act.wait_ge(xT_sb, n + 1)
                    nc.scalar.activation(xT_hi[:, u, :], xT[:], ACT.Identity).then_inc(xT_high, 1)
                elif step == "exp":
                    act.wait_ge(diff_ready, n + 1)
                    nc.scalar.activation(raised[:], diff[:], ACT.Exp).then_inc(raised_ready, 1)

            for e in range(2):
                act.wait_ge(w1_scaled, e + 1)
                nc.scalar.activation(w1_hi[:, e, :], chip.w1[:, e, :], ACT.Identity).then_inc(w1_high, 1)
            front(0, 0, "x")
            for e in range(2, E1):
                act.wait_ge(w1_scaled, e + 1)
                nc.scalar.activation(w1_hi[:, e, :], chip.w1[:, e, :], ACT.Identity).then_inc(w1_high, 1)
            front(0, 0, "exp")
            act.wait_ge(b1_ready, 1)
            with act.Fori(0, STEPS) as j:
                for k, (e, u) in enumerate(units):
                    if e == 1:
                        act.wait_ge(combT_ps, j * 2 + (u + 1))
                        nc.scalar.activation(combT[:], bank_r[:, 0:P], ACT.Identity).then_inc(combT_sb, 1)
                    for m in range(M):
                        act.wait_ge(h_ps, j * (U * M) + (k * M + m + 1))
                        nc.scalar.activation(h[:, k % 2, m, :], bank_h[m][:], ACT.Gelu,
                                             bias=b1[:, e * M + m:e * M + m + 1]).then_inc(h_ready, 1)
                    for step, at in ACT_FRONT.items():
                        if at == e:
                            front(j * 2 + (u + 1), 1 - u, step)

        @block.gpsimd
        def _(pool):
            nc.gpsimd.memset(b2[:], 0.0).then_inc(const, 1)
            nc.gpsimd.memset(rb_row[:], 0.0).then_inc(const, 1)
            nc.gpsimd.memset(comb_w[:], 0.0).then_inc(const, 1)
            nc.gpsimd.memset(two[:], BIG).then_inc(two_set, 1)
            steps = Steps(pool, pool_steps)
            pool.wait_ge(mv2_ready, 1)
            inner_rstd(pool, steps)
            with pool.Fori(0, STEPS) as j:
                steps = Steps(pool, pool_steps, j, 2, base=1)
                norm_rstd(chip, pool, j, mv_ready, steps, rstd_ready)
                pool.wait_ge(mv2_ready, j + 2)
                inner_rstd(pool, steps)

        @block.vector
        def _(dve):
            steps = Steps(dve, first_steps)
            inner_stats(steps)
            dve.wait_ge(rstd2_ready, 1)
            inner_rows()
            nc.vector.tensor_scalar(rw[:], chip.weight("router1"), chip.weight("rn_g"), None, ALU.mult)
            nc.vector.tensor_scalar(rn_b[:], chip.ones[:], chip.weight("rn_b"), None, ALU.mult).then_inc(rn_ready, 1)

            def split_weights(experts):
                for e in experts:
                    dve.wait_ge(w1_high, e + 1)
                    nc.vector.tensor_tensor(w1_lo[:, e, :], chip.w1[:, e, :], w1_hi[:, e, :].bitcast(F32),
                                            ALU.subtract).then_inc(w1_ready, 1)

            along = lambda ap: ap.unsqueeze(2).broadcast_to([P, TPH, E1])
            comb = lambda u: comb_w[:, u, 0:TE].rearrange("p (t e) -> p t e", e=E1)

            def front(n, u, step, steps):
                if step == "split":
                    dve.wait_ge(xT_high, n + 1)
                    nc.vector.tensor_tensor(xT_lo[:, u, :], xT[:], xT_hi[:, u, :].bitcast(F32),
                                            ALU.subtract).then_inc(xT_split, 1)
                elif step == "best":
                    dve.wait_ge(logits, n + 1)
                    steps.done(nc.vector.tensor_tensor(logit[:], bank_r[:, 0:TE].rearrange("p (t e) -> p t e", e=E1),
                                                       rb[:].unsqueeze(1).broadcast_to([P, TPH, E1]), ALU.add))
                    nc.vector.tensor_copy(chip.spare[:], stats[:, 0, 0:1])
                    for t in range(TPH):
                        last = nc.vector.max(best[:, t, :], logit[:, t, :])
                    steps.done(last)
                    nc.vector.tensor_tensor(diff[:], logit[:], along(best[:, :, 0]), ALU.subtract).then_inc(diff_ready, 1)
                    steps.done(nc.vector.tensor_copy(two[:, :, 0:2], best[:, :, 0:2]))
                    nc.vector.tensor_copy(chip.spare[:], stats[:, 0, 0:1])
                    for t in range(TPH):
                        last = nc.vector.match_replace(left[:, t, :], two[:, t, :], logit[:, t, :], -BIG)
                    steps.done(last)
                    steps.done(nc.vector.tensor_scalar(left[:], left[:], -BIG, None, ALU.is_equal))
                elif step == "share":
                    dve.wait_ge(raised_ready, n + 1)
                    steps.done(nc.vector.tensor_tensor(left[:], left[:], raised[:], ALU.mult))
                    steps.done(nc.vector.tensor_reduce(total[:], left[:], AX_X, ALU.add))
                    steps.done(nc.vector.reciprocal(share[:], total[:]))
                    nc.vector.tensor_tensor(comb(u), left[:], along(share[:]), ALU.mult).then_inc(comb_ready, 1)

            ROUTER_STEPS = 8
            for e in range(E1):
                dve.wait_ge(b1_ps, e + 1)
                nc.vector.tensor_scalar(chip.w1[:, e, :], chip.w1[:, e, :], chip.weight("ln_gT")[:, e:e + 1], None,
                                        ALU.mult).then_inc(w1_scaled, 1)
            nc.vector.tensor_tensor(b1[:], bank_y[0][:].rearrange("p t d -> p (t d)")[:, 0:E1 * M], chip.weight("b1"),
                                    ALU.add).then_inc(b1_ready, 1)
            split_weights(range(2))
            front(0, 0, "split", steps)
            dve.wait_ge(bias_ps, 1)
            nc.vector.tensor_copy(rb[:], bank_y[1][:, 0, 0:E1]).then_inc(bias_done, 1)
            dve.wait_ge(bias_done, 1)
            dve.wait_ge(two_set, 1)
            dve.wait_ge(const, 3)
            steps = Steps(dve, dve_steps)
            front(0, 0, "best", steps)
            split_weights(range(2, E1))
            front(0, 0, "share", steps)
            assert steps.k == ROUTER_STEPS
            nc.vector.tensor_copy(chip.spare[:], stats[:, 0, 0:1]).then_inc(x_done, 1)
            with dve.Fori(0, STEPS) as j:
                steps = Steps(dve, dve_steps, j, 2 * ROUTER_STEPS + 2, ROUTER_STEPS)
                jn = (j + 1) % STEPS
                for k, (e, u) in enumerate(units):
                    if e == 0:
                        dve.wait_ge(comb_ready, j * 2 + (u + 1))
                    if e == 2:
                        dve.wait_ge(b2_ps, j * 2 + (u + 1))
                        dve.wait_ge(x_done, j * U + (k + 1))
                        rows = chip.x[:, ds(j * TPI + TPH * u, TPH), :]
                        nc.vector.tensor_tensor(rows, bank_x[:].rearrange("p (t d) -> p t d", d=D), rows,
                                                ALU.add).then_inc(b2_done, 1)
                        dve.wait_ge(b2_done, j * 2 + (u + 1))
                    if (u, e) == (0, 4):
                        norm_stats(chip, steps, jn, mv_ready)
                    if (u, e) == (0, 6):
                        norm_rows(chip, dve, jn, j, rstd_ready, xn_ready)
                    if (u, e) == (1, 0):
                        dve.wait_ge(xn_ready, j + 1)
                        inner_stats(steps)
                    if (u, e) == (1, 1):
                        dve.wait_ge(xT_ps, j * 2 + 2)
                        dve.wait_ge(rstd2_ready, j + 2)
                        inner_rows()
                    dve.wait_ge(y_ps, j * U + (k + 1))
                    if e:
                        dve.wait_ge(x_done, j * U + (k + 1))
                    for t in range(TPH):
                        row = chip.x[:, ds(j * TPI + TPH * u + t, 1), :]
                        at = t * E1 + e
                        last = nc.vector.scalar_tensor_tensor(row, bank_y[k % 2][:, t, :], comb_w[:, u, at:at + 1], row,
                                                              ALU.mult, ALU.add)
                    last.then_inc(x_done, 1)
                    for step, at in DVE_FRONT.items():
                        if at == e:
                            front(j * 2 + (u + 1), 1 - u, step, steps)
                steps.close()

def stage_store(chip, out_dram):
    nc = chip.nc
    with ExitStack() as ctx:
        stored = ctx.enter_context(nc.semaphore("st_out"))
        block = ctx.enter_context(nc.Block())

        @block.sync
        def _(sp):
            o = out_dram.rearrange("(t p) d -> p t d", p=P)
            for n in range(STEPS):
                sp.dma_start(o[:, n * TPI:(n + 1) * TPI, :], chip.x[:, n * TPI:(n + 1) * TPI, :]).then_inc(stored, 16)
            sp.wait_ge(stored, 16 * STEPS)


def build(nc, a, stages="ABCDEF"):
    with ExitStack() as ctx:
        chip = Chip(nc, ctx)
        first = lambda sp: fetch_ffn0(chip, sp, a["ffn0_gate"], a["ffn0_up"], a["ffn0_down"])
        second = lambda sp: fetch_ffn1(chip, sp, a["ffn1_w1"], a["ffn1_w2"])
        with ExitStack() as early:
            chip.place_ffn0(early)
            stage_load(chip, a["x"], a["pack"], None if "A" in stages or "C" not in stages else first,
                       wait_all="A" not in stages)
            if "A" in stages:
                stage_cross0(chip, a["ctx"], a["ctxT"], first)
            if "B" in stages:
                stage_recurrence(chip)
            if "C" in stages:
                stage_experts0(chip)
        chip.place_ffn1(ctx)
        if "D" in stages:
            stage_heads(chip, a["ctxT"], a["mask"], second)
        elif "F" in stages:
            with nc.Block() as block:
                block.sync(second)
        if "E" in stages:
            stage_ssm(chip, a["b_out"])
        if "F" in stages:
            stage_experts1(chip, a["router_b"], a["b2"])
        stage_store(chip, a["out"])


def lay_out(v):
    f = lambda name: np.asarray(v[name])
    cols = lambda a: np.ascontiguousarray(a.reshape(-1, P).T)
    wide = lambda a: np.concatenate(list(a), axis=1)
    rows = lambda a: wide(a.reshape(-1, P, a.shape[-1]))

    def heads(a):
        w = np.zeros((D, D), a.dtype)
        for h in range(HEADS):
            w[h * HD:(h + 1) * HD, h * HD:(h + 1) * HD] = a
        return w

    l0, l1, f1 = "L0_attn_", "L1_attn_", "L1_ffn_"
    part = {
        "wqT": f("L0_xattn_Wq").T, "wkT": f("L0_xattn_Wk").T, "bq": cols(f("L0_xattn_bq")), "bk": cols(f("L0_xattn_bk")),
        "wrT": wide(f(l0 + "wr_w").transpose(0, 2, 1)), "wiT": wide(f(l0 + "wi_w").transpose(0, 2, 1)),
        "woT": wide(f(l0 + "wo_w").transpose(0, 2, 1)), "cw": wide(f(l0 + "conv_w")),
        "cb": f(l0 + "conv_b").T, "rb": f(l0 + "wr_b").T, "ib": f(l0 + "wi_b").T, "log_a": f(l0 + "log_a").T,
        "norm_w": f(l0 + "norm_w").T, "norm_out": cols(f(l0 + "norm_out_w")),
        "router0": f("L0_ffn_gate_w").T,
        "q_bd": heads(f("L1_xattn_queries_weight")), "k_bd": heads(f("L1_xattn_keys_weight")),
        "v_bd": heads(f("L1_xattn_values_weight")), "fc": f("L1_xattn_fc_weight"),
        "in_g": cols(f(l1 + "ln_g")), "in_b": cols(f(l1 + "ln_b")), "w_inT": f(l1 + "W_in").T,
        "b_in": cols(f(l1 + "b_in")), "conv_w": rows(f(l1 + "conv_w")[:, 0, :]), "conv_b": cols(f(l1 + "conv_b")),
        "ssm_A": rows(f(l1 + "A")), "ssm_B": rows(f(l1 + "Bm")), "w_cT": rows(f(l1 + "W_c").T),
        "w_dT": rows(f(l1 + "W_d").T), "b_c": cols(f(l1 + "b_c")), "b_d": cols(f(l1 + "b_d")),
        "log_delta": cols(f(l1 + "log_delta")), "w_outT": rows(f(l1 + "W_out").T),
        "rn_g": cols(f(f1 + "rn_g")), "rn_b": cols(f(f1 + "rn_b")), "router1": f(f1 + "router_w").T,
        "ln_gT": f(f1 + "ln_g").T, "ln_bT": f(f1 + "ln_b").T, "b1": cols(f(f1 + "b1")),
            }
    return {
        "x": f("x").reshape(B * S, D),
        "pack": np.concatenate([part[name] for name, _ in PACK], axis=1),
        "ctx": f("ctx_1024").transpose(1, 0, 2).reshape(KV, B * D),
        "ctxT": f("ctx_1024").transpose(2, 0, 1).reshape(D, B * KV),
        "mask": f("mask_1x1xSxS2_ik0").reshape(S, KV),
        "ffn0_gate": f("L0_ffn_w_gate").transpose(2, 0, 1), "ffn0_up": f("L0_ffn_w_up").transpose(2, 0, 1),
        "ffn0_down": f("L0_ffn_w_down").transpose(0, 2, 1).reshape(E0 * I0 // P, P, D).transpose(1, 0, 2),
        "ffn1_w1": f("L1_ffn_w1").transpose(1, 0, 2), "ffn1_w2": f("L1_ffn_w2").reshape(E1 * I1 // P, P, D).transpose(1, 0, 2),
        "b_out": f(l1 + "b_out").reshape(1, D), "router_b": f(f1 + "router_b").reshape(1, E1),
        "b2": f(f1 + "b2"),
    }


def kernel(**inputs):
    import concourse.bacc as bacc
    from concourse.bass_utils import run_bass_kernel_spmd

    nc = bacc.Bacc("TRN2", target_bir_lowering=False, num_devices=1)
    arrays, aps = {}, {}
    for name, a in lay_out(inputs).items():
        a = np.ascontiguousarray(a)
        arrays[name] = a
        aps[name] = nc.dram_tensor(name, a.shape, mybir.dt.from_np(a.dtype), kind="ExternalInput").ap()
    aps["out"] = nc.dram_tensor("out", (B * S, D), F32, kind="ExternalOutput").ap()
    build(nc, aps)
    r = run_bass_kernel_spmd(nc, [arrays], core_ids=[0])
    return np.asarray(r.results[0]["out"]).reshape(B, S, D)
```
